# Optimizing a Trainium2 kernel written in Bass

```python
import numpy as np
import jax
import jax.numpy as jnp

def _softmax(x, axis=-1):
    return jax.nn.softmax(x, axis=axis)

def _gelu(x):
    return jax.nn.gelu(x, approximate=True)

def _silu(x):
    return jax.nn.silu(x)

def _sigmoid(x):
    return jax.nn.sigmoid(x)

def _layernorm(x, axis=-1, eps=1e-05):
    m = jnp.mean(x, axis=axis, keepdims=True)
    v = jnp.var(x, axis=axis, keepdims=True)
    return (x - m) / jnp.sqrt(v + eps)

def _scatter_add(tgt, idx, src, axis=0):
    return tgt.at[idx].add(src)

def _segment_sum(src, seg, n):
    return jax.ops.segment_sum(src, seg, n)
kernel_name = 'mk_prb_d2_jaxref_r4_6b225a'

def setup_inputs(seed: int=0):
    np.random.seed(seed)
    _w = jnp.asarray

    def _L0_attn_setup():
        import jax, jax.numpy as jnp
        import numpy as np
        B, S, D, H = (2, 512, 256, 16)
        HS = D // H
        key = jax.random.key(seed)
        k1, k2, k3 = jax.random.split(key, 3)
        x = jax.random.normal(k1, (B, S, D), dtype=jnp.float32)
        c_attn_w = jax.random.normal(k2, (D, 3 * D), dtype=jnp.float32) * (1.0 / np.sqrt(D))
        c_attn_b = jnp.zeros((3 * D,), dtype=jnp.float32)
        c_proj_w = jax.random.normal(k3, (D, D), dtype=jnp.float32) * (1.0 / np.sqrt(D))
        c_proj_b = jnp.zeros((D,), dtype=jnp.float32)
        return {'x': x, 'c_attn_w': c_attn_w, 'c_attn_b': c_attn_b, 'c_proj_w': c_proj_w, 'c_proj_b': c_proj_b}
    _L0_attn_in = _L0_attn_setup()

    def _L0_ffn_setup():
        import jax, jax.numpy as jnp
        import numpy as np
        from jax.scipy.linalg import expm
        B, S, D, E, K, NROT = (2, 512, 256, 8, 2, 3)
        DF = 4 * D
        EPS = 1e-05
        key = jax.random.key(seed)
        ks = jax.random.split(key, 8)
        s = lambda d: 1.0 / np.sqrt(d)
        return {'x': jax.random.normal(ks[0], (B, S, D), jnp.float32), 'ln_g': jnp.ones((D,), jnp.float32), 'ln_b': jnp.zeros((D,), jnp.float32), 'abel_w': jax.random.normal(ks[1], (D, D), jnp.float32) * s(D), 'abel_b': jnp.zeros((D,), jnp.float32), 'gate_w_moe': jax.random.normal(ks[2], (D, E), jnp.float32) * s(D), 'gate_b_moe': jnp.zeros((E,), jnp.float32), 'w1': jax.random.normal(ks[3], (E, D, DF), jnp.float32) * s(D), 'b1': jnp.zeros((E, DF), jnp.float32), 'w2': jax.random.normal(ks[4], (E, DF, D), jnp.float32) * s(DF), 'b2': jnp.zeros((E, D), jnp.float32), 'gens': jax.random.normal(ks[5], (NROT, D, D), jnp.float32) * 0.02, 'mix_w': jax.random.normal(ks[6], (2 * D, 1), jnp.float32) * s(2 * D), 'mix_b': jnp.zeros((1,), jnp.float32)}
    _L0_ffn_in = _L0_ffn_setup()

    def _L1_attn_setup():
        import jax, jax.numpy as jnp
        from jax import lax
        import numpy as np
        BATCH, SEQ = (2, 512)
        D_MODEL, D_STATE, D_CONV = (256, 16, 4)
        D_INNER = 2 * D_MODEL
        DT_RANK = D_MODEL // 16
        DT_MIN, DT_MAX = (0.001, 0.1)

        def _mamba_fwd(hidden_states, in_proj_w, conv_w, conv_b, x_proj_w, dt_proj_w, dt_proj_b, A_log, D, out_proj_w):
            silu = jax.nn.silu
            b, l, _ = hidden_states.shape
            xz = hidden_states @ in_proj_w.T
            x, z = jnp.split(xz, 2, axis=-1)
            xc = jnp.transpose(x, (0, 2, 1))
            xc = lax.conv_general_dilated(xc, conv_w, window_strides=(1,), padding=[(D_CONV - 1, 0)], feature_group_count=D_INNER, dimension_numbers=('NCH', 'OIH', 'NCH')) + conv_b[None, :, None]
            x = silu(jnp.transpose(xc, (0, 2, 1)))
            A = -jnp.exp(A_log)
            xp = x @ x_proj_w.T
            dt, Bm, C = jnp.split(xp, [DT_RANK, DT_RANK + D_STATE], axis=-1)
            dt = jax.nn.softplus(dt @ dt_proj_w.T + dt_proj_b)

            def step(h, ins):
                dt_t, B_t, C_t, x_t = ins
                dA = jnp.exp(dt_t[:, :, None] * A)
                h = dA * h + dt_t[:, :, None] * B_t[:, None, :] * x_t[:, :, None]
                y = jnp.einsum('bdn,bn->bd', h, C_t)
                return (h, y)
            h0 = jnp.zeros((b, D_INNER, D_STATE), hidden_states.dtype)
            xs = (jnp.transpose(dt, (1, 0, 2)), jnp.transpose(Bm, (1, 0, 2)), jnp.transpose(C, (1, 0, 2)), jnp.transpose(x, (1, 0, 2)))
            _, ys = lax.scan(step, h0, xs)
            y = jnp.transpose(ys, (1, 0, 2)) + x * D
            return y * silu(z) @ out_proj_w.T
        key = jax.random.key(seed)
        ks = jax.random.split(key, 8)
        s = 0.02
        dt = jnp.exp(jax.random.uniform(ks[0], (D_INNER,)) * (np.log(DT_MAX) - np.log(DT_MIN)) + np.log(DT_MIN))
        dt = jnp.clip(dt, 0.0001, None)
        inv_dt = dt + jnp.log(-jnp.expm1(-dt))
        dt_std = DT_RANK ** (-0.5)
        return {'hidden_states': jax.random.normal(ks[1], (BATCH, SEQ, D_MODEL), jnp.float32), 'in_proj_w': jax.random.normal(ks[2], (2 * D_INNER, D_MODEL), jnp.float32) * s, 'conv_w': jax.random.normal(ks[3], (D_INNER, 1, D_CONV), jnp.float32) * s, 'conv_b': jnp.zeros((D_INNER,), jnp.float32), 'x_proj_w': jax.random.normal(ks[4], (DT_RANK + 2 * D_STATE, D_INNER), jnp.float32) * s, 'dt_proj_w': jax.random.uniform(ks[5], (D_INNER, DT_RANK), jnp.float32, -dt_std, dt_std), 'dt_proj_b': inv_dt, 'A_log': jnp.log(jnp.tile(jnp.arange(1, D_STATE + 1, dtype=jnp.float32), (D_INNER, 1))), 'D': jnp.ones((D_INNER,), jnp.float32), 'out_proj_w': jax.random.normal(ks[6], (D_MODEL, D_INNER), jnp.float32) * s}
    _L1_attn_in = _L1_attn_setup()

    def _L1_ffn_setup():
        import jax, jax.numpy as jnp
        import numpy as np
        THRESH_FACTOR = 0.7

        def ternary_quantize(w):
            delta = THRESH_FACTOR * jnp.mean(jnp.abs(w))
            return jnp.where(w > delta, 1.0, jnp.where(w < -delta, -1.0, 0.0)).astype(w.dtype)
        key = jax.random.key(seed)
        k1, k2, k3 = jax.random.split(key, 3)
        B, S, D_IN, D_OUT = (8, 1024, 256, 256)
        inp = {'input': jax.random.normal(k1, (B, S, D_IN), dtype=jnp.float32), 'weight': jax.random.normal(k2, (D_OUT, D_IN), dtype=jnp.float32) * (1.0 / np.sqrt(D_IN)), 'alpha': jnp.ones((1,), dtype=jnp.float32), 'bias': jax.random.normal(k3, (D_OUT,), dtype=jnp.float32) * (1.0 / np.sqrt(D_IN))}
        return inp
    _L1_ffn_in = _L1_ffn_setup()
    _d = {'L0_attn_x': _L0_attn_in['x'], 'L0_attn_c_attn_w': _L0_attn_in['c_attn_w'], 'L0_attn_c_attn_b': _L0_attn_in['c_attn_b'], 'L0_attn_c_proj_w': _L0_attn_in['c_proj_w'], 'L0_attn_c_proj_b': _L0_attn_in['c_proj_b'], 'L0_ffn_ln_g': _L0_ffn_in['ln_g'], 'L0_ffn_ln_b': _L0_ffn_in['ln_b'], 'L0_ffn_abel_w': _L0_ffn_in['abel_w'], 'L0_ffn_abel_b': _L0_ffn_in['abel_b'], 'L0_ffn_gate_w_moe': _L0_ffn_in['gate_w_moe'], 'L0_ffn_gate_b_moe': _L0_ffn_in['gate_b_moe'], 'L0_ffn_w1': _L0_ffn_in['w1'], 'L0_ffn_b1': _L0_ffn_in['b1'], 'L0_ffn_w2': _L0_ffn_in['w2'], 'L0_ffn_b2': _L0_ffn_in['b2'], 'L0_ffn_gens': _L0_ffn_in['gens'], 'L0_ffn_mix_w': _L0_ffn_in['mix_w'], 'L0_ffn_mix_b': _L0_ffn_in['mix_b'], 'L1_attn_in_proj_w': _L1_attn_in['in_proj_w'], 'L1_attn_conv_w': _L1_attn_in['conv_w'], 'L1_attn_conv_b': _L1_attn_in['conv_b'], 'L1_attn_x_proj_w': _L1_attn_in['x_proj_w'], 'L1_attn_dt_proj_w': _L1_attn_in['dt_proj_w'], 'L1_attn_dt_proj_b': _L1_attn_in['dt_proj_b'], 'L1_attn_A_log': _L1_attn_in['A_log'], 'L1_attn_D': _L1_attn_in['D'], 'L1_attn_out_proj_w': _L1_attn_in['out_proj_w'], 'L1_ffn_weight': _L1_ffn_in['weight'], 'L1_ffn_alpha': _L1_ffn_in['alpha'], 'L1_ffn_bias': _L1_ffn_in['bias']}
    _x0 = _d['L0_attn_x']
    _d['L0_attn_x'] = jax.random.normal(jax.random.fold_in(jax.random.key(seed), 1), (2, 2048, 256), dtype=_x0.dtype)
    del _x0
    return _d

def reference(L0_attn_x, L0_attn_c_attn_w, L0_attn_c_attn_b, L0_attn_c_proj_w, L0_attn_c_proj_b, L0_ffn_ln_g, L0_ffn_ln_b, L0_ffn_abel_w, L0_ffn_abel_b, L0_ffn_gate_w_moe, L0_ffn_gate_b_moe, L0_ffn_w1, L0_ffn_b1, L0_ffn_w2, L0_ffn_b2, L0_ffn_gens, L0_ffn_mix_w, L0_ffn_mix_b, L1_attn_in_proj_w, L1_attn_conv_w, L1_attn_conv_b, L1_attn_x_proj_w, L1_attn_dt_proj_w, L1_attn_dt_proj_b, L1_attn_A_log, L1_attn_D, L1_attn_out_proj_w, L1_ffn_weight, L1_ffn_alpha, L1_ffn_bias):

    def _L0_attn_ref(x, c_attn_w, c_attn_b, c_proj_w, c_proj_b):
        import jax, jax.numpy as jnp
        import numpy as np
        B, S, D, H = (2, 512, 256, 16)
        HS = D // H
        b, s, d = x.shape
        qkv = x @ c_attn_w + c_attn_b
        q, k, v = jnp.split(qkv, 3, axis=-1)
        q = q.reshape(b, s, H, HS).transpose(0, 2, 1, 3)
        k = k.reshape(b, s, H, HS).transpose(0, 2, 1, 3)
        v = v.reshape(b, s, H, HS).transpose(0, 2, 1, 3)
        scale = jnp.float32(HS) ** (-0.5)
        scores = jnp.einsum('bhqd,bhkd->bhqk', q, k) * scale
        causal = jnp.tril(jnp.ones((s, s), dtype=bool))
        scores = jnp.where(causal[None, None, :, :], scores, jnp.float32(-jnp.inf))
        weights = jax.nn.softmax(scores, axis=-1)
        attn = jnp.einsum('bhqk,bhkd->bhqd', weights, v)
        attn = attn.transpose(0, 2, 1, 3).reshape(b, s, d)
        out = attn @ c_proj_w + c_proj_b
        return out

    def _L0_ffn_ref(x, ln_g, ln_b, abel_w, abel_b, gate_w_moe, gate_b_moe, w1, b1, w2, b2, gens, mix_w, mix_b):
        import jax, jax.numpy as jnp
        import numpy as np
        from jax.scipy.linalg import expm
        B, S, D, E, K, NROT = (2, 512, 256, 8, 2, 3)
        DF = 4 * D
        EPS = 1e-05
        residual = x
        mu = jnp.mean(x, axis=-1, keepdims=True)
        var = jnp.mean((x - mu) ** 2, axis=-1, keepdims=True)
        xn = (x - mu) * jax.lax.rsqrt(var + EPS) * ln_g + ln_b
        abel = jax.nn.gelu(xn @ abel_w + abel_b, approximate=False)
        logits = xn @ gate_w_moe + gate_b_moe
        tw, ti = jax.lax.top_k(logits, K)
        tw = jax.nn.softmax(tw, axis=-1)
        onehot = (ti[..., None] == jnp.arange(E)).astype(tw.dtype)
        wdense = jnp.sum(tw[..., None] * onehot, axis=2)
        h = jax.nn.gelu(jnp.einsum('bsd,edf->besf', xn, w1) + b1[None, :, None, :], approximate=False)
        eo = jnp.einsum('besf,efd->besd', h, w2) + b2[None, :, None, :]
        moe = jnp.einsum('besd,bse->bsd', eo, wdense)
        rot = expm(gens[0])
        for i in range(1, NROT):
            rot = rot @ expm(gens[i])
        nonabel = moe @ rot
        combined = jnp.concatenate([abel, nonabel], axis=-1)
        g = jax.nn.sigmoid(combined @ mix_w + mix_b)
        return residual + abel * (1.0 - g) + nonabel * g

    def _L1_attn_ref(hidden_states, in_proj_w, conv_w, conv_b, x_proj_w, dt_proj_w, dt_proj_b, A_log, D, out_proj_w):
        import jax, jax.numpy as jnp
        from jax import lax
        import numpy as np
        BATCH, SEQ = (2, 512)
        D_MODEL, D_STATE, D_CONV = (256, 16, 4)
        D_INNER = 2 * D_MODEL
        DT_RANK = D_MODEL // 16
        DT_MIN, DT_MAX = (0.001, 0.1)

        def _mamba_fwd(hidden_states, in_proj_w, conv_w, conv_b, x_proj_w, dt_proj_w, dt_proj_b, A_log, D, out_proj_w):
            silu = jax.nn.silu
            b, l, _ = hidden_states.shape
            xz = hidden_states @ in_proj_w.T
            x, z = jnp.split(xz, 2, axis=-1)
            xc = jnp.transpose(x, (0, 2, 1))
            xc = lax.conv_general_dilated(xc, conv_w, window_strides=(1,), padding=[(D_CONV - 1, 0)], feature_group_count=D_INNER, dimension_numbers=('NCH', 'OIH', 'NCH')) + conv_b[None, :, None]
            x = silu(jnp.transpose(xc, (0, 2, 1)))
            A = -jnp.exp(A_log)
            xp = x @ x_proj_w.T
            dt, Bm, C = jnp.split(xp, [DT_RANK, DT_RANK + D_STATE], axis=-1)
            dt = jax.nn.softplus(dt @ dt_proj_w.T + dt_proj_b)

            def step(h, ins):
                dt_t, B_t, C_t, x_t = ins
                dA = jnp.exp(dt_t[:, :, None] * A)
                h = dA * h + dt_t[:, :, None] * B_t[:, None, :] * x_t[:, :, None]
                y = jnp.einsum('bdn,bn->bd', h, C_t)
                return (h, y)
            h0 = jnp.zeros((b, D_INNER, D_STATE), hidden_states.dtype)
            xs = (jnp.transpose(dt, (1, 0, 2)), jnp.transpose(Bm, (1, 0, 2)), jnp.transpose(C, (1, 0, 2)), jnp.transpose(x, (1, 0, 2)))
            _, ys = lax.scan(step, h0, xs)
            y = jnp.transpose(ys, (1, 0, 2)) + x * D
            return y * silu(z) @ out_proj_w.T
        return _mamba_fwd(hidden_states, in_proj_w, conv_w, conv_b, x_proj_w, dt_proj_w, dt_proj_b, A_log, D, out_proj_w)

    def _L1_ffn_ref(input, weight, alpha, bias):
        import jax, jax.numpy as jnp
        import numpy as np
        THRESH_FACTOR = 0.7

        def ternary_quantize(w):
            delta = THRESH_FACTOR * jnp.mean(jnp.abs(w))
            return jnp.where(w > delta, 1.0, jnp.where(w < -delta, -1.0, 0.0)).astype(w.dtype)
        w_ternary = ternary_quantize(weight)
        w_eff = w_ternary * alpha
        out = jnp.einsum('bsd,od->bso', input, w_eff) + bias
        return out
    x = L0_attn_x
    xn = _layernorm(x, axis=-1)
    x = x + _L0_attn_ref(xn, L0_attn_c_attn_w, L0_attn_c_attn_b, L0_attn_c_proj_w, L0_attn_c_proj_b) + _L0_ffn_ref(xn, L0_ffn_ln_g, L0_ffn_ln_b, L0_ffn_abel_w, L0_ffn_abel_b, L0_ffn_gate_w_moe, L0_ffn_gate_b_moe, L0_ffn_w1, L0_ffn_b1, L0_ffn_w2, L0_ffn_b2, L0_ffn_gens, L0_ffn_mix_w, L0_ffn_mix_b)
    xn = _layernorm(x, axis=-1)
    x = x + _L1_attn_ref(xn, L1_attn_in_proj_w, L1_attn_conv_w, L1_attn_conv_b, L1_attn_x_proj_w, L1_attn_dt_proj_w, L1_attn_dt_proj_b, L1_attn_A_log, L1_attn_D, L1_attn_out_proj_w) + _L1_ffn_ref(xn, L1_ffn_weight, L1_ffn_alpha, L1_ffn_bias)
    return x

_drawn_inputs = setup_inputs


def setup_inputs(seed=0):
    import zlib

    import numpy as np

    out = dict(_drawn_inputs(seed))
    spreads = {'L0_attn_c_attn_b': (0.0, 0.1),
     'L0_attn_c_proj_b': (0.0, 0.1),
     'L0_ffn_ln_g': (1.0, 0.2),
     'L0_ffn_ln_b': (0.0, 0.1),
     'L0_ffn_abel_b': (0.0, 0.621),
     'L0_ffn_gate_b_moe': (0.0, 0.1),
     'L0_ffn_b1': (0.0, 0.471),
     'L0_ffn_b2': (0.0, 0.306),
     'L1_attn_conv_b': (0.0, 0.8),
     'L1_attn_D': (1.0, 0.6)}
    factors = {'L1_attn_in_proj_w': 8.0,
     'L1_attn_conv_w': 8.0,
     'L1_attn_x_proj_w': 8.0,
     'L1_attn_dt_proj_w': 8.0,
     'L1_attn_dt_proj_b': 8.0,
     'L1_attn_A_log': 8.0,
     'L1_attn_out_proj_w': 8.0,
     'L1_ffn_bias': 64.0}
    for name, (base, spread) in spreads.items():
        noise = np.random.default_rng([zlib.crc32(name.encode()), seed]).standard_normal(out[name].shape)
        drawn = base * np.exp(spread * noise) if base else spread * noise
        out[name] = jnp.asarray(drawn.astype(out[name].dtype))
    for name, factor in factors.items():
        out[name] = (out[name] * factor).astype(out[name].dtype)
    return out
```

```python
from contextlib import ExitStack

import concourse.bass as bass
from concourse import mybir

F32 = mybir.dt.float32
BF16 = mybir.dt.bfloat16
I32 = mybir.dt.int32
ALU = mybir.AluOpType
ACT = mybir.ActivationFunctionType
AX = mybir.AxisListType
ds = bass.ds

P = 128
B, S, D = 2, 2048, 256
T = B * S
NT = T // P
KD = D // P
H, HS = 16, 16
SCALE = float(HS) ** -0.5
E, DF = 8, 4 * D
KF = DF // P
NROT = 3
EPS = 1e-5
CH = 512
TPC = CH // P
NC = T // CH
CPB = S // CH
QT = S // P
HG = 4
NG = B * H // HG
GPB = NG // B
GR = HG * HS
QPART = (0, 0, 1, 0, 2, 1)
KPART = (0, 1, 0, 2, 0, 1)
ROWS = len(QPART) * HS
FULL = ROWS + 3
MASKED = -1e30
TAYLOR = 10
INNER = 2 * D
KI = INNER // P
NS = 16
RANK = D // 16
TAPS = 4
NX = RANK + 2 * NS
NQ = NS // 4


class Chain:

    def __init__(self, eng, sem):
        self.eng, self.sem, self.base, self.turn, self.n = eng, sem, 0, 0, 0

    def enter(self, turn):
        self.base, self.n, self.turn = self.base + self.n, 0, turn

    def leave(self, turns, per):
        assert self.n == per, (self.n, per)
        self.base, self.turn, self.n = self.base + turns * per, 0, 0

    def mark(self, ins):
        ins.then_inc(self.sem, 1)
        self.n += 1
        return self.base + self.turn + self.n

    def link(self, ins):
        self.eng.wait_ge(self.sem, self.mark(ins))

    def straight(self):
        self.base, self.n = self.base + self.n, 0

    def settle(self):
        self.eng.wait_ge(self.sem, self.base + self.turn + self.n)


def max_units():
    out = []
    for qc in range(CPB):
        units = [("max", h, t, k0, min(1024, P * (t + 1) - k0)) for h in range(HG)
                 for t in range(TPC * qc, TPC * (qc + 1)) for k0 in range(0, P * (t + 1), 1024)]
        if qc:
            units.insert(2, ("turn", qc - 1))
        out += units
    return out + [("turn", CPB - 1)]


EU = [(h, qc, kt, max(0, kt * P - qc * CH))
      for qc in range(CPB) for kt in range(TPC * (qc + 1)) for h in range(HG)]
MU = max_units()
NM, NE = len(MU), len(EU)
STEPS = NE // HG
SRING, PRING = 3, 8
LAST_STEP = [max(n // HG for n in range(NE) if EU[n][1] == qc) for qc in range(CPB)]


def period_plan(with_exp, with_max):
    out, m, late = [], 0, []
    for n in range(NE if with_exp else 0):
        out.append(("score", n))
        if n % HG == HG - 1 and n > HG:
            step = n // HG - 1
            out.append(("pv", step))
            if step in LAST_STEP:
                late.append((n + 6, LAST_STEP.index(step)))
        while with_max and m * NE < NM * (n + 1):
            out.append(MU[m])
            m += 1
        if late and late[0][0] == n:
            out.append(("back", late.pop(0)[1]))
    if with_exp:
        out.append(("pv", STEPS - 1))
        out += [("back", qc) for _, qc in late] + [("back", CPB - 1)]
    elif with_max:
        out += MU
    return out


def ring_of(plan):
    return [u for u in plan if u[0] in ("max", "turn", "back")]


FULL_PLAN, FIRST_PLAN, LAST_PLAN = period_plan(True, True), period_plan(False, True), period_plan(True, False)
NR = len(ring_of(FULL_PLAN))


def build(nc, x, aw, ab, pw, pb, ln_g, ln_b, abel_w, abel_b, gate_w, gate_b, w1, b1, w2, b2, gens, gens_t,
          mix_w, mix_b, in_wt, conv_w, conv_b, xp_wt, dt_wt, dt_b, a_log, dd, out_wt, tern_wt, alpha, tern_b, out):
    with ExitStack() as ctx:
        ctx.enter_context(nc.allow_non_contiguous_dma(reason="vectors of a few hundred elements"))

        def sb(name, shape, dt=F32, at=ctx):
            return at.enter_context(nc.sbuf_tensor(name, shape, dt))

        def sem(name):
            return ctx.enter_context(nc.semaphore(name))

        def dram(name, shape, dt=F32):
            return nc.dram_tensor(name, shape, dt, kind="Internal").ap()

        def row(t):
            return t.rearrange("(a n) -> a n", a=1)

        def cols(t):
            return t.rearrange("(k p) -> p k", p=P)

        def rows(t):
            return t.rearrange("(t p) d -> p t d", p=P)

        def fat(t):
            return t.rearrange("(k p) n -> p k n", p=P)

        qk_d = dram("qk_parts", [3, 2, NG * GR, S], BF16)
        v_d = dram("v_rows", [T, D])
        xn_d = dram("xn_rows", [T, D])
        ab_d = dram("abel_rows", [T, D])
        at_d = dram("attn_rows", [T, D])
        max_d = dram("max_rows", [CPB, 3, HG * CH], BF16)
        x1_d = dram("x1_rows", [T, D])
        x1T_d = dram("x1_columns", [NC, P, KD, CH])

        ps = ctx.enter_context(nc.psum_tensor("ps", [P, 8, 512], F32))
        idf = sb("idf", [P, P])
        ones_r = sb("ones_r", [1, P])
        m0 = ExitStack()
        idb = sb("idb", [P, P], BF16, at=m0)
        mask_q = sb("mask_q", [P, P], BF16, at=m0)
        mask_k = sb("mask_k", [P, P], BF16, at=m0)
        ones_s = sb("ones_s", [P, P], at=m0)
        xn2T = sb("xn2T", [P, KD, T], at=m0)
        wd = sb("wd", [P, NT, E], at=m0)
        rot = sb("rot", [P, KD, D], at=m0)

        m1 = ExitStack()
        X = sb("X", [P, NT, D], at=m1)
        XN = sb("XN", [P, NT, D], at=m1)
        st = sb("st", [P, NT, 6], at=m1)
        sm = sb("sm", [P, 12, NT], at=m1)
        me = ExitStack()
        ga = sb("ga", [P, NROT, KD, D], at=me)
        gt = sb("gt", [P, NROT, KD, D], at=me)
        gb = sb("gb", [P, NROT, KD, D], at=me)
        er = sb("er", [P, NROT, KD, D], at=me)
        et = sb("et", [P, NROT, KD, D], at=me)
        kid = sb("kid", [P, TAYLOR, KD, D], BF16, at=me)
        nrm = sb("nrm", [P, 8], at=me)
        nri = sb("nri", [P, 8], I32, at=me)
        me.close()
        wqkv = sb("wqkv", [P, KD, 3 * D], at=m1)
        bqk = sb("bqk", [P, 4], at=m1)
        bv = sb("bv", [1, D], at=m1)
        wab = sb("wab", [P, KD, D], at=m1)
        bab = sb("bab", [1, D], at=m1)
        wg = sb("wg", [P, KD, E], at=m1)
        bg = sb("bg", [1, E], at=m1)
        lng = sb("lng", [P, 2, KD], at=m1)
        XNc = sb("XNc", [P, TPC, D], at=m1)
        x2h = sb("x2h", [P, TPC, D], at=m1)
        xTc = sb("xTc", [P, KD, CH], at=m1)
        x2c = sb("x2c", [P, KD, CH], at=m1)
        qf = sb("qf", [P, 2, CH], at=m1)
        qr = sb("qr", [P, CH], at=m1)
        q3 = sb("q3", [P, 4, 3, CH], BF16, at=m1)
        Vc = sb("Vc", [P, TPC, D], at=m1)
        ABc = sb("ABc", [P, TPC, D], at=m1)
        lgt = sb("lgt", [P, NT, E], at=m1)
        top = sb("top", [P, 4, NT, E], at=m1)
        m1.close()

        m2 = ExitStack()
        qs = sb("qs", [P, 2, HG, S], BF16, at=m2)
        ks = sb("ks", [P, 2, HG, S], BF16, at=m2)
        vg = sb("vg", [P, 2, QT, HG, 32], at=m2)
        vl = sb("vl", [P, QT, GR], at=m2)
        Pt = sb("Pt", [P, PRING, CH], at=m2)
        oT = sb("oT", [P, CH], at=m2)
        ao = sb("ao", [P, TPC, GR], at=m2)
        rec = sb("rec", [P, TPC, HG], at=m2)
        mp = sb("mp", [P, CPB, HG, TPC, 2], at=m2)
        mn = sb("mn", [P, CPB, HG * TPC], at=m2)
        n3 = sb("n3", [HG * TPC, CPB, 3, P], BF16, at=m2)
        nr = sb("nr", [HG * TPC, P], at=m2)
        m2.close()

        m3 = ExitStack()
        moe = sb("moe", [P, NT, D], at=m3)
        m3b = ExitStack()
        W1 = sb("W1", [P, 2, KD, DF], at=m3b)
        W2 = sb("W2", [P, 2, KF, D], at=m3b)
        B1 = sb("B1", [P, E, KF], at=m3b)
        hT = sb("hT", [P, 2, KF, CH], at=m3b)
        m3b.close()
        wpj = sb("wpj", [P, KD, D], at=m3)
        bpj = sb("bpj", [1, D], at=m3)
        B2 = sb("B2", [E, D], at=m3)
        mixw = sb("mixw", [P, 2, D], at=m3)
        mixb = sb("mixb", [P, 1], at=m3)
        inx = sb("inx", [P, 2, 4, TPC, D], at=m3)
        atT = sb("atT", [P, KD, CH], at=m3)
        mot = sb("mot", [P, TPC, D], at=m3)
        moT = sb("moT", [P, KD, CH], at=m3)
        wdc = sb("wdc", [P, TPC, E], at=m3)
        wdT = sb("wdT", [E, CH], at=m3)
        cmb = sb("cmb", [P, 4, TPC, D], at=m3)
        x1c = sb("x1c", [P, TPC, D], at=m3)
        gate = sb("gate", [P, 4, TPC], at=m3)
        x1s = sb("x1s", [P, TPC, 6], at=m3)
        x1v = sb("x1v", [P, TPC, 2], at=m3)
        x1r = sb("x1r", [P, 3, TPC], at=m3)
        x1n = sb("x1n", [P, TPC, D], at=m3)
        x1T = sb("x1T", [P, KD, CH], at=m3)
        m3.close()
        m0.close()

        inw = sb("inw", [P, KD, 2 * INNER])
        cw = sb("cw", [P, KI, TAPS])
        cb = sb("cb", [P, KI])
        xpw = sb("xpw", [P, KI, NX])
        dtw = sb("dtw", [2 * NS + RANK, INNER])
        dtb = sb("dtb", [P, KI])
        A = sb("A", [P, KI, NS])
        Dv = sb("Dv", [P, KI])
        outw = sb("outw", [P, KI, D])
        tw = sb("tw", [P, KD, D])
        tsum = sb("tsum", [P, 8])
        alph = sb("alph", [P, 1])
        tb = sb("tb", [1, D])
        sel = sb("sel", [6 * NS, 2 * NS, P], BF16)
        flag = sb("flag", [P, NC + 1])
        xin = sb("xin", [P, 2, KD, CH])
        xraw = sb("xraw", [P, KI, TAPS - 1 + CH])
        xs = sb("xs", [P, 2, KI, CH])
        zs = sb("zs", [P, 2, KI, CH])
        dt = sb("dt", [P, 2, KI, CH])
        dtx = sb("dtx", [P, 2, KI, CH])
        te = sb("te", [P, 2, CH])
        tl = sb("tl", [P, 2, CH])
        xps = sb("xps", [NX, CH])
        bcr = sb("bcr", [2 * NS, CH])
        bc2 = sb("bc2", [2 * NS, CH], BF16)
        bc3 = sb("bc3", [6 * NS, 2, CH], BF16)
        Bq = sb("Bq", [P, 2, 4, CH])
        Cq = sb("Cq", [P, 2, 4, CH])
        dA = sb("dA", [P, 2, 4, CH])
        hh = sb("hh", [P, 4, 4, CH])
        tq = hh[:, 0, 0, :].rearrange("p (k n) -> p k n", k=KD)
        onef = hh[:, 1, 0, 0:P]
        hst = sb("hst", [P, 4 * NQ, 4])
        xo = sb("xo", [P, TPC, D])

        s_phase = sem("s_phase")
        s_alone = sem("s_alone")
        c_dve, c_act, c_pool, s_const = sem("c_dve"), sem("c_act"), sem("c_pool"), sem("s_const")
        s_x, s_w, s_g = sem("s_x"), sem("s_w"), sem("s_g")
        s_nrm_abs, s_nrm_ps, s_sc, s_scaled = sem("s_nrm_abs"), sem("s_nrm_ps"), sem("s_sc"), sem("s_scaled")
        s_hor, s_hev, s_sqp, s_sqe, s_fin, s_fev = (sem(n) for n in ("s_hor", "s_hev", "s_sqp", "s_sqe", "s_fin", "s_fev"))
        s_var, s_std, s_xn = sem("s_var"), sem("s_std"), sem("s_xn")
        s_xnc, s_x2h = sem("s_xnc"), sem("s_x2h")
        s_tx, s_xT, s_t2, s_x2c = sem("s_tx"), sem("s_xT"), sem("s_t2"), sem("s_x2c")
        s_qp, s_qf, s_q3, s_qd = sem("s_qp"), sem("s_qf"), sem("s_q3"), sem("s_qd")
        s_vp, s_vc, s_vd = sem("s_vp"), sem("s_vc"), sem("s_vd")
        s_ap, s_ac, s_ad = sem("s_ap"), sem("s_ac"), sem("s_ad")
        s_lp, s_lc, s_nd, s_x2t = sem("s_lp"), sem("s_lc"), sem("s_nd"), sem("s_x2t")
        s_top, s_tex = sem("s_top"), sem("s_tex")
        s_stack = sem("s_stack")
        s_qk = [sem(f"s_qk{i}") for i in range(2)]
        s_vl, s_vg = sem("s_vl"), sem("s_vg")
        s_full, s_free = sem("s_full"), sem("s_free")
        s_score, s_exp, s_pv = sem("s_score"), sem("s_exp"), sem("s_pv")
        s_md = sem("s_md")
        s_oT, s_aod = sem("s_oT"), sem("s_aod")
        s_mn, s_mr, s_mrow = sem("s_mn"), sem("s_mr"), [sem(f"s_mrow{i}") for i in range(CPB)]
        s_ew, s_b = [sem(f"s_ew{i}") for i in range(2)], sem("s_b")
        s_hp, s_hT, s_op, s_moe, s_mz = sem("s_hp"), sem("s_hT"), sem("s_op"), sem("s_moe"), sem("s_mz")
        s_cw, s_ci = sem("s_cw"), [sem(f"s_ci{i}") for i in range(2)]
        s_cwd, s_ctp, s_cT, s_cpr, s_cmo, s_cmp, s_cmT, s_cnb = (sem(f"s_c_{n}") for n in ("wd", "tp", "T", "pr", "mo", "mp", "mT", "nb"))
        s_cz, s_cg, s_cb, s_cx, s_co = (sem(f"s_c_{n}") for n in ("z", "g", "b", "x", "o"))

        s_x1s, s_x1q, s_x1n, s_x1t, s_x1T, s_x1d = (sem(n) for n in ("s_x1s", "s_x1q", "s_x1n", "s_x1t", "s_x1T", "s_x1d"))
        s_lw, s_xin, s_xo, s_od = sem("s_lw"), [sem(f"s_xin{i}") for i in range(2)], sem("s_xo"), sem("s_od")
        s_setup, s_abs, s_tps, s_A, s_tern = (sem(n) for n in ("s_setup", "s_abs", "s_tps", "s_A", "s_tern"))
        s_wfull, s_wfree = sem("s_wfull"), sem("s_wfree")
        s_raw, s_conv, s_tail, s_xs, s_zs, s_xps, s_bc3 = (sem(n) for n in ("s_raw", "s_conv", "s_tail", "s_xs", "s_zs", "s_xps", "s_bc3"))
        s_sp, s_ln, s_poly, s_dt, s_bu = (sem(n) for n in ("s_sp", "s_ln", "s_poly", "s_dt", "s_bu"))
        s_cfull, s_cfree = sem("s_cfull"), sem("s_cfree")
        s_dA, s_h, s_hc, s_acc, s_y, s_yz, s_add = (sem(n) for n in ("s_dA", "s_h", "s_hc", "s_acc", "s_y", "s_yz", "s_add"))

        block = ctx.enter_context(nc.Block())

        def stage_end(eng, k):
            eng.drain().then_inc(s_phase, 1)
            eng.wait_ge(s_phase, 5 * k)

        def alone(eng):
            eng.sem_inc(s_alone, 1)

        x_t = x.rearrange("b (t p) d -> p (b t) d", p=P)
        out_t = out.rearrange("b (t p) d -> p (b t) d", p=P)

        @block.sync
        def _(sp):
            n = NT // 4
            for c in range(4):
                sp.dma_start(X[:, c * n:(c + 1) * n, :], x_t[:, c * n:(c + 1) * n, :]).then_inc(s_x, 16)
            sp.dma_start(ga[:, :, :, :], gens.rearrange("g (k p) n -> p g k n", p=P)).then_inc(s_g, 16)
            sp.dma_start(gt[:, :, :, :], gens_t.rearrange("g (k p) n -> p g k n", p=P)).then_inc(s_g, 16)
            sp.sem_inc(s_nd, 16)
            sp.sem_inc(s_qd, 64)
            sp.sem_inc(s_vd, 16)
            sp.sem_inc(s_ad, 16)
            sp.sem_inc(s_aod, 16)
            stage_end(sp, 1)

            sp.dma_start(wqkv[:, :, :], fat(aw)).then_inc(s_w, 16)
            sp.dma_start(bqk[:, :], cols(ab[0:2 * D])).then_inc(s_w, 16)
            sp.dma_start(bv[:, :], row(ab[2 * D:3 * D])).then_inc(s_w, 16)
            sp.dma_start(wab[:, :, :], fat(abel_w)).then_inc(s_w, 16)
            sp.dma_start(bab[:, :], row(abel_b)).then_inc(s_w, 16)
            sp.dma_start(wg[:, :, :], fat(gate_w)).then_inc(s_w, 16)
            sp.dma_start(bg[:, :], row(gate_b)).then_inc(s_w, 16)
            sp.dma_start(lng[:, 0, :], cols(ln_g)).then_inc(s_w, 16)
            sp.dma_start(lng[:, 1, :], cols(ln_b)).then_inc(s_w, 16)
            with sp.Fori(0, NC) as n:
                b, c = n // CPB, n % CPB
                sp.wait_ge(s_xnc, n + 1)
                sp.dma_start(rows(xn_d)[:, ds(n * TPC, TPC), :], XNc[:, :, :]).then_inc(s_nd, 16)
                for m in range(4):
                    sp.wait_ge(s_q3, n * 4 + (m + 1 + 1))
                    dst = qk_d[:, m // 2, :, :].rearrange("a r t -> r a t")[
                        ds(b * (2 * P) + (m % 2) * P, P), :, ds(c * CH, CH)]
                    sp.dma_start(dst, q3[:, m, :, :]).then_inc(s_qd, 16)
                sp.wait_ge(s_vc, n + 2)
                sp.dma_start(rows(v_d)[:, ds(n * TPC, TPC), :], Vc[:, :, :]).then_inc(s_vd, 16)
                sp.wait_ge(s_ac, n + 2)
                sp.dma_start(rows(ab_d)[:, ds(n * TPC, TPC), :], ABc[:, :, :]).then_inc(s_ad, 16)
            sp.wait_ge(s_nd, 16 * (NC + 1))
            sp.wait_ge(s_qd, 64 * (NC + 1))
            sp.wait_ge(s_vd, 16 * (NC + 1))
            sp.wait_ge(s_ad, 16 * (NC + 1))
            stage_end(sp, 2)

            def load_group(g, par):
                for c in range(len(QPART)):
                    for w, (buf, part) in enumerate(((qs, QPART[c]), (ks, KPART[c]))):
                        src = qk_d[part, w, ds(g * GR, GR), :].rearrange("(h d) t -> d h t", h=HG)
                        sp.dma_start(buf[c * HS:(c + 1) * HS, par, :, :], src).then_inc(s_qk[par], 16)

            def batch_rows(t, g):
                return t.rearrange("(b t p) n -> b p t n", p=P, b=B)[g // GPB, :, :, ds((g % GPB) * GR, GR)]

            def load_v(g):
                sp.dma_start(vl[:, :, :], batch_rows(v_d, g)).then_inc(s_vl, 16)

            def store_max(g, par, qc):
                sp.wait_ge(s_mr, g * CPB + (qc + 1))
                sp.dma_start(max_d[qc].rearrange("a (r q) -> r a q", q=P), n3[:, qc, :, :]).then_inc(s_md, 16)
                sp.wait_ge(s_md, (g * CPB + (qc + 1)) * 16)
                sp.dma_start(qs[ROWS:FULL, par, :, qc * CH:(qc + 1) * CH],
                             max_d[qc].rearrange("a (h n) -> a h n", h=HG)).then_inc(s_mrow[qc], 16)

            def period(g, par, plan, base, more, stack):
                if more:
                    sp.wait_ge(s_vg, g + 1)
                    load_v(g + 1)
                for r, u in enumerate(ring_of(plan)):
                    if u[0] == "turn":
                        store_max(g + 1, 1 - par, u[1])
                    if u[0] == "back":
                        sp.wait_ge(s_free, base + (r + 1))
                        sp.dma_start(batch_rows(at_d, g)[:, u[1] * TPC:(u[1] + 1) * TPC, :],
                                     ao[:, :, :]).then_inc(s_aod, 16)
                if stack:
                    sp.wait_ge(s_pv, (g + 1) * STEPS + 2)
                    load_group(g + 2, par)

            load_v(0)
            load_group(0, 0)
            load_group(1, 1)
            for qc in range(CPB):
                store_max(0, 0, qc)
            with sp.Fori(0, NG // 2 - 1) as i:
                for par in range(2):
                    g = i * 2 + par
                    period(g, par, FULL_PLAN, g * NR + NM, True, True)
            period(NG - 2, 0, FULL_PLAN, NM + (NG - 2) * NR, True, False)
            period(NG - 1, 1, LAST_PLAN, NM + (NG - 1) * NR, False, False)
            sp.wait_ge(s_aod, 16 * (NG * CPB + 1))
            stage_end(sp, 3)

            def load_expert(e, par):
                sp.dma_start(W1[:, par, :, :], w1[e, :, :].rearrange("(k p) f -> p k f", p=P)).then_inc(s_ew[par], 16)
                sp.dma_start(W2[:, par, :, :], w2[e, :, :].rearrange("(k p) f -> p k f", p=P)).then_inc(s_ew[par], 16)

            sp.dma_start(B1[:, :, :], b1.rearrange("e (k p) -> p e k", p=P)).then_inc(s_b, 16)
            load_expert(0, 0)
            load_expert(1, 1)
            with sp.Fori(1, E // 2) as i:
                for par in range(2):
                    sp.wait_ge(s_op, (i * 2 + par - 1) * NT + 2 * TPC)
                    load_expert(i * 2 + par, par)
            stage_end(sp, 4)

            sp.dma_start(wpj[:, :, :], fat(pw)).then_inc(s_cw, 16)
            sp.dma_start(bpj[:, :], row(pb)).then_inc(s_cw, 16)
            sp.dma_start(B2[:, :], b2).then_inc(s_cw, 16)
            sp.dma_start(mixw[:, :, :], mix_w.rearrange("(a k n) c -> a k (n c)", a=1, k=2).broadcast_to([P, 2, D])).then_inc(s_cw, 16)
            sp.dma_start(mixb[:, :], row(mix_b).broadcast_to([P, 1])).then_inc(s_cw, 16)

            def load_chunk(c, par):
                for k, src in enumerate((x_t, rows(xn_d), rows(ab_d), rows(at_d))):
                    sp.dma_start(inx[:, par, k, :, :], src[:, ds(c * TPC, TPC), :]).then_inc(s_ci[par], 16)

            def store_chunk(c):
                sp.wait_ge(s_cx, c + 2)
                sp.dma_start(rows(x1_d)[:, ds(c * TPC, TPC), :], x1c[:, :, :]).then_inc(s_co, 16)
                sp.wait_ge(s_x1T, c + 1)
                sp.dma_start(x1T_d[c, :, :, :], x1T[:, :, :]).then_inc(s_x1d, 16)

            load_chunk(0, 0)
            load_chunk(1, 1)
            sp.sem_inc(s_co, 16)
            sp.sem_inc(s_x1d, 16)
            with sp.Fori(0, NC // 2 - 1) as i:
                for par in range(2):
                    store_chunk(i * 2 + par)
                    load_chunk(i * 2 + (par + 2), par)
            store_chunk(NC - 2)
            store_chunk(NC - 1)
            sp.wait_ge(s_co, 16 * (NC + 1))
            sp.wait_ge(s_x1d, 16 * (NC + 1))
            stage_end(sp, 5)

            for dst, src in ((tw[:, :, :], fat(tern_wt)), (alph[:, :], row(alpha).broadcast_to([P, 1])),
                             (inw[:, :, :], fat(in_wt)), (cw[:, :, :], conv_w.rearrange("(k p) a t -> p k (a t)", p=P)),
                             (cb[:, :], cols(conv_b)), (xpw[:, :, :], fat(xp_wt)), (dtw[2 * NS:, :], dt_wt),
                             (dtb[:, :], cols(dt_b)), (A[:, :, :], a_log.rearrange("(k p) n -> p k n", p=P)),
                             (Dv[:, :], cols(dd)), (outw[:, :, :], fat(out_wt)), (tb[:, :], row(tern_b))):
                sp.dma_start(dst, src).then_inc(s_lw, 16)

            def load_columns(n, par):
                sp.dma_start(xin[:, par, :, :], x1T_d[n, :, :, :]).then_inc(s_xin[par], 16)

            def finish(n):
                sp.dma_start(xo[:, :, :], rows(x1_d)[:, ds(n * TPC, TPC), :]).then_inc(s_xo, 16)
                sp.wait_ge(s_add, n + 1)
                sp.dma_start(out_t[:, ds(n * TPC, TPC), :], xo[:, :, :]).then_inc(s_od, 16)
                sp.wait_ge(s_od, n * 16 + 16)

            load_columns(0, 0)
            load_columns(1, 1)
            finish(0)
            load_columns(2, 0)
            with sp.Fori(0, (NC - 4) // 2) as i:
                for k in (1, 2):
                    finish(i * 2 + k)
                    load_columns(i * 2 + (k + 2), k % 2)
            finish(NC - 3)
            load_columns(NC - 1, 1)
            finish(NC - 2)
            finish(NC - 1)
            stage_end(sp, 6)

        @block.gpsimd
        def _(pool):
            po = Chain(pool, c_pool)
            po.mark(pool.memset(idf[:, :], 0.0))
            po.mark(pool.memset(idb[:, :], 0.0))
            po.mark(pool.memset(mask_q[:, :], 0.0))
            po.mark(pool.memset(mask_k[:, :], 0.0))
            po.mark(pool.memset(kid[:, :, :, :], 0.0))
            pool.memset(ones_r[:, :], 1.0).then_inc(s_const, 1)
            pool.memset(ones_s[:, :], 1.0).then_inc(s_const, 1)
            po.settle()
            for m in (idf, idb):
                pool.affine_select(out=m[:, :], in_=m[:, :], compare_op=ALU.not_equal, fill=1.0, base=0,
                                   pattern=[[-1, P]], channel_multiplier=1).then_inc(s_const, 1)
            pool.affine_select(out=mask_q[:, :], in_=mask_q[:, :], compare_op=ALU.is_ge, fill=MASKED, base=0,
                               pattern=[[-1, P]], channel_multiplier=1).then_inc(s_const, 1)
            pool.affine_select(out=mask_k[:, :], in_=mask_k[:, :], compare_op=ALU.is_ge, fill=MASKED, base=0,
                               pattern=[[1, P]], channel_multiplier=-1).then_inc(s_const, 1)
            for k in range(TAYLOR):
                pool.affine_select(out=kid[:, k, :, :], in_=kid[:, k, :, :], compare_op=ALU.not_equal,
                                   fill=float(k + 1), base=0, pattern=[[P, KD], [-1, D]],
                                   channel_multiplier=1).then_inc(s_const, 1)
            stage_end(pool, 1)

            pool.sem_inc(s_x2t, 1)
            with pool.Fori(0, NC) as n:
                pool.wait_ge(s_x2c, n * KD + KD)
                alone(pool)
                pool.tensor_copy(xn2T[:, :, ds(n * CH, CH)], x2c[:, :, :]).then_inc(s_x2t, 1)
            stage_end(pool, 2)

            pool.memset(ks[ROWS:FULL, :, :, :], 1.0).then_inc(s_stack, 1)
            pool.wait_ge(s_stack, 1)
            po.link(pool.memset(vg[:, :, :, :, HS:32], 0.0))
            po.link(pool.memset(vg[:, :, :, :, HS:HS + 1], 1.0))

            def spread(g, par):
                pool.wait_ge(s_vl, (g + 1) * 16)
                alone(pool)
                pool.tensor_copy(vg[:, par, :, :, 0:HS], vl[:, :, :].rearrange("p t (h d) -> p t h d", h=HG)).then_inc(s_vg, 1)

            spread(0, 0)
            with pool.Fori(0, NG // 2 - 1) as i:
                for par in range(2):
                    g = i * 2 + par
                    pool.wait_ge(s_pv, g * STEPS + 2)
                    spread(g + 1, 1 - par)
            pool.wait_ge(s_pv, (NG - 2) * STEPS + 2)
            spread(NG - 1, 1)
            stage_end(pool, 3)

            pool.memset(moe[:, :, :], 0.0).then_inc(s_mz, 1)
            stage_end(pool, 4)

            with pool.Fori(0, NC // 2) as i:
                po.enter(i * 2)
                for par in range(2):
                    c = i * 2 + par
                    pool.wait_ge(s_ci[par], (i + 1) * 64)
                    pool.wait_ge(s_cx, c + 1)
                    po.link(pool.tensor_tensor(cmb[:, 0, :, :], inx[:, par, 0, :, :], inx[:, par, 1, :, :], ALU.add))
                    pool.tensor_tensor(cmb[:, 1, :, :], cmb[:, 0, :, :], inx[:, par, 2, :, :], ALU.add).then_inc(s_cb, 1)
                po.leave(NC // 2, 2)
            stage_end(pool, 5)

            po.mark(pool.memset(sel[:, :, :], 0.0))
            po.mark(pool.memset(flag[:, :], 1.0))
            po.mark(pool.memset(hst[:, :, :], 0.0))
            po.mark(pool.memset(xraw[:, :, 0:TAPS - 1], 0.0))
            po.mark(pool.memset(onef[:, :], 1.0))
            po.settle()
            for a in range(3):
                po.link(pool.affine_select(out=sel[:, :, :], in_=sel[:, :, :], compare_op=ALU.not_equal, fill=1.0,
                                           base=-2 * NS * a, pattern=[[-1, 2 * NS], [0, P]], channel_multiplier=1))
            for b in range(B + 1):
                po.link(pool.memset(flag[:, b * CPB:b * CPB + 1], 0.0))
            pool.sem_inc(s_setup, 1)
            pool.sem_inc(s_yz, 2)

            def series(m, k, par):
                pool.wait_ge(s_ln, m * 2 + (k + 1))
                p = dtx[:, par, 2 * k:2 * k + 2, :]
                alone(pool)
                po.link(pool.tensor_scalar(p, te[:, :, :], 1.0 / 3, -0.5, ALU.mult, ALU.add))
                po.link(pool.tensor_tensor(p, p, te[:, :, :], ALU.mult))
                alone(pool)
                po.link(pool.tensor_scalar(p, p, 1.0, None, ALU.add))
                pool.tensor_tensor(p, p, te[:, :, :], ALU.mult).then_inc(s_poly, 1)

            def gate_z(n, par):
                pool.wait_ge(s_y, n * KI + 2 * KI)
                pool.tensor_tensor(xs[:, par, :, :], xs[:, par, :, :], zs[:, par, :, :], ALU.mult).then_inc(s_yz, 1)

            def pool_body(n, par, first, last):
                for u in range(4 * NQ):
                    pool.wait_ge(s_h, n * 16 + (u + 1 + 2))
                    if u % 4 == 0:
                        pool.wait_ge(s_cfree, n * 32 + (u // 4 * 8 + 8 + 2))
                    h = hh[:, u % 4, :, :]
                    pool.tensor_tensor(h, h, Cq[:, u // 4 % 2, :, :], ALU.mult).then_inc(s_hc, 1)
                    if u == 1 and not first:
                        gate_z(n - 1, 1 - par)
                    if u in (13, 14) and not last:
                        series(n + 1, u - 13, 1 - par)

            pool.sem_inc(s_hc, 8)
            for k in range(2):
                series(0, k, 0)
            po.straight()
            pool_body(0, 0, True, False)
            pool_body(1, 1, False, False)
            with pool.Fori(1, NC // 2 - 1) as i:
                po.enter((i - 1) * 12)
                pool_body(i * 2, 0, False, False)
                pool_body(i * 2 + 1, 1, False, False)
                po.leave(NC // 2 - 2, 12)
            pool_body(NC - 2, 0, False, False)
            pool_body(NC - 1, 1, False, True)
            gate_z(NC - 1, 1)
            stage_end(pool, 6)

        @block.scalar
        def _(act):
            ac = Chain(act, c_act)
            act.wait_ge(s_g, 32)
            act.activation(gb[:, :, :, :], ga[:, :, :, :], ACT.Abs).then_inc(s_nrm_abs, 1)
            act.wait_ge(s_sc, 1)
            act.wait_ge(s_nrm_ps, 1)
            act.activation(gb[:, :, :, :], gt[:, :, :, :], ACT.Copy, scale=nrm[:, 1:2]).then_inc(s_scaled, 1)
            act.activation(er[:, :, :, :], ga[:, :, :, :], ACT.Copy, scale=nrm[:, 1:2]).then_inc(s_scaled, 1)
            for k in range(TAYLOR, 0, -1):
                for g in range(NROT):
                    act.wait_ge(s_hor, (TAYLOR - k) * NROT + g + 1)
                    act.activation(er[:, g, :, :], ps[:, g, :].rearrange("p (k n) -> p k n", k=KD), ACT.Copy,
                                   scale=1.0 / k).then_inc(s_hev, 1)
            for g in range(NROT):
                act.wait_ge(s_hor, TAYLOR * NROT + g + 1)
                act.activation(et[:, g, :, :], ps[:, 3 + g, :].rearrange("p (k n) -> p k n", k=KD), ACT.Copy).then_inc(s_hev, 1)
            squarings = act.value_load(nri[0:1, 2:3], min_val=1, max_val=200)
            with act.Fori(0, squarings) as i:
                for g in range(NROT):
                    act.wait_ge(s_sqp, i * NROT + (g + 1))
                    act.activation(er[:, g, :, :], ps[:, g, :].rearrange("p (k n) -> p k n", k=KD), ACT.Copy).then_inc(s_sqe, 1)
                    act.activation(et[:, g, :, :], ps[:, 3 + g, :].rearrange("p (k n) -> p k n", k=KD), ACT.Copy).then_inc(s_sqe, 1)
            act.wait_ge(s_fin, 1)
            act.activation(gb[:, 0, :, :], ps[:, 6, :].rearrange("p (k n) -> p k n", k=KD), ACT.Copy).then_inc(s_fev, 1)
            act.wait_ge(s_fin, 2)
            act.activation(rot[:, :, :], ps[:, 7, :].rearrange("p (k n) -> p k n", k=KD), ACT.Copy).then_inc(s_fev, 1)
            for k in range(2):
                act.wait_ge(s_var, k + 1)
                act.activation(sm[:, 6 * k + 3, :], sm[:, 6 * k + 2, :], ACT.Sqrt).then_inc(s_std, 1)
            stage_end(act, 1)

            act.wait_ge(s_w, 9 * 16)
            act.sem_inc(s_ac, 1)
            act.sem_inc(s_qf, 2)
            with act.Fori(0, NC) as n:
                act.wait_ge(s_tx, n + 1)
                act.wait_ge(s_nd, n * 16 + 16)
                alone(act)
                act.activation(XNc[:, :, :], XN[:, ds(n * TPC, TPC), :], ACT.Copy).then_inc(s_xnc, 1)
                act.wait_ge(s_tx, n + 2)
                act.wait_ge(s_vp, n + 1)
                act.activation(xTc[:, :, :], ps[:, 0:2, :], ACT.Copy).then_inc(s_xT, 1)
                for m in range(4):
                    act.wait_ge(s_qp, n * 4 + (m + 1))
                    act.wait_ge(s_q3, n * 4 + (m if m > 1 else 1))
                    act.activation(qf[:, m % 2, :], ps[:, 4 + m % 2, :], ACT.Identity, bias=bqk[:, m:m + 1]).then_inc(s_qf, 1)
                act.wait_ge(s_ap, n + 1)
                act.wait_ge(s_ad, n * 16 + 16)
                act.activation(ABc[:, :, :], ps[:, 0:2, :].rearrange("p k (t n) -> p (k t) n", n=D), ACT.Gelu).then_inc(s_ac, 1)
            act.wait_ge(s_top, 1)
            act.activation(sm[:, 2, :], sm[:, 1, :], ACT.Exp).then_inc(s_tex, 1)
            stage_end(act, 2)

            act.sem_inc(s_exp, NE)
            act.sem_inc(s_oT, 1)

            def evict(g, qc, base, plan):
                act.wait_ge(s_pv, g * STEPS + (LAST_STEP[qc] + 1 + 2))
                before = [r for r, u in enumerate(ring_of(plan)) if u == ("back", qc - 1)]
                act.wait_ge(s_full, base + (before[0] + 1 if before else 0))
                act.activation(oT[:, :], ps[:, 7, :], ACT.Copy).then_inc(s_oT, 1)

            def exps(g, base, plan):
                for n, (h, qc, kt, q0) in enumerate(EU):
                    if n % HG == 0:
                        act.wait_ge(s_pv, g * STEPS + (n // HG + 1))
                    act.wait_ge(s_score, g * NE + (n + 1))
                    act.activation(Pt[:, n % PRING, q0:CH], ps[:, 4 + n % SRING, q0:CH], ACT.Exp, scale=SCALE).then_inc(s_exp, 1)
                    if n % HG == HG - 1 and n // HG - 1 in LAST_STEP:
                        evict(g, EU[n - HG][1], base, plan)
                evict(g, CPB - 1, base, plan)

            with act.Fori(0, NG - 1) as g:
                exps(g, g * NR + NM, FULL_PLAN)
            exps(NG - 1, NM + (NG - 1) * NR, LAST_PLAN)
            stage_end(act, 3)

            act.wait_ge(s_b, 16)
            act.sem_inc(s_hT, 4)

            def hidden(e, u, slot):
                act.wait_ge(s_op, u * TPC + TPC)
                for f in range(KF):
                    act.wait_ge(s_hp, u * KF + (f + 1))
                    alone(act)
                    act.activation(hT[:, slot, f, :], ps[:, f % 4, :], ACT.Gelu, bias=B1[:, e, f:f + 1]).then_inc(s_hT, 1)

            with act.Fori(0, E) as e:
                for c in range(NC):
                    hidden(e, e * NC + c, c % 2)
            stage_end(act, 4)

            act.wait_ge(s_cw, 5 * 16)
            with act.Fori(0, NC) as c:
                act.wait_ge(s_ctp, c + 1)
                act.activation(atT[:, :, :], ps[:, 0:2, :], ACT.Copy).then_inc(s_cT, 1)
                act.activation(wdT[:, :], ps[0:E, 2, :], ACT.Copy).then_inc(s_cT, 1)
                act.wait_ge(s_cmp, c + 1)
                act.activation(moT[:, :, :], ps[:, 0:2, :], ACT.Copy).then_inc(s_cmT, 1)
                act.wait_ge(s_cz, c + 1)
                act.activation(gate[:, 3, :], gate[:, 2, :], ACT.Sigmoid, bias=mixb[:, 0:1]).then_inc(s_cg, 1)
                act.wait_ge(s_x1s, c + 1)
                act.activation(x1r[:, 1, :], x1r[:, 0, :], ACT.Sqrt).then_inc(s_x1q, 1)
                act.wait_ge(s_x1t, c + 1)
                act.wait_ge(s_x1d, c * 16 + 16)
                act.activation(x1T[:, :, :], ps[:, 0:2, :], ACT.Copy).then_inc(s_x1T, 1)
            stage_end(act, 5)

            act.wait_ge(s_lw, 12 * 16)
            for k in range(KD):
                act.activation(tq[:, k, :], tw[:, k, :], ACT.Abs, accum_out=tsum[:, k:k + 1]).then_inc(s_abs, 1)
            ac.link(act.activation(A[:, :, :], A[:, :, :], ACT.Exp))
            ac.link(act.activation(A[:, :, :], A[:, :, :], ACT.Copy, scale=-1.0))
            act.sem_inc(s_wfree, 1)
            act.sem_inc(s_cfree, 2)

            def raw(m, k):
                act.wait_ge(s_wfull, m * 8 + (k + 1))
                act.wait_ge(s_tail, m + 1)
                act.activation(xraw[:, 2 * k:2 * k + 2, TAPS - 1:], ps[:, 4:6, :], ACT.Copy).then_inc(s_wfree, 1)

            def silu_z(m, k, par):
                act.wait_ge(s_wfull, m * 8 + (k + 3))
                act.wait_ge(s_yz, m + 1)
                act.activation(zs[:, par, 2 * k:2 * k + 2, :], ps[:, 4:6, :], ACT.Silu).then_inc(s_wfree, 1)

            def silu_x(m, par):
                for d in range(KI):
                    act.wait_ge(s_conv, m * KI + (d + 1))
                    act.activation(xs[:, par, d, :], xs[:, par, d, :], ACT.Silu, bias=cb[:, d:d + 1]).then_inc(s_xs, 1)

            def take_xp(m):
                act.wait_ge(s_wfull, m * 8 + 5)
                act.wait_ge(s_bc3, m + 1)
                act.activation(xps[:, :], ps[0:NX, 4, :], ACT.Copy).then_inc(s_wfree, 1)

            def softplus(m, k, par, old):
                act.wait_ge(s_wfull, m * 8 + (k + 6))
                act.wait_ge(s_sp, m * 2 + (k + 1))
                if old:
                    act.wait_ge(s_h, m * 16 - 14)
                for j in range(2):
                    d = 2 * k + j
                    ac.mark(act.activation(te[:, j, :], ps[:, 4 + j, :], ACT.Abs, bias=dtb[:, d:d + 1]))
                    act.activation(dt[:, par, d, :], ps[:, 4 + j, :], ACT.Relu, bias=dtb[:, d:d + 1]).then_inc(s_wfree, j) if j else \
                        ac.mark(act.activation(dt[:, par, d, :], ps[:, 4 + j, :], ACT.Relu, bias=dtb[:, d:d + 1]))
                ac.settle()
                ac.link(act.activation(te[:, :, :], te[:, :, :], ACT.Exp, scale=-1.0))
                act.activation(tl[:, :, :], te[:, :, :], ACT.Ln, bias=1.0).then_inc(s_ln, 1)

            def spread_bc(n, q):
                act.wait_ge(s_bu, n * 16 + (q * 4 + 4))
                act.wait_ge(s_hc, n * 16 + (q * 4 + 4))
                for k in range(8):
                    c = q * 8 + k
                    act.wait_ge(s_cfull, n * 32 + (c + 1))
                    dst = Bq if k < 4 else Cq
                    act.activation(dst[:, q % 2, k % 4, :], ps[:, 6 + k % 2, :], ACT.Copy).then_inc(s_cfree, 1)

            def act_body(n, par, last):
                for u in range(4 * NQ):
                    q, d = u // 4, u % 4
                    if u == 0:
                        act.wait_ge(s_dt, n * 2 + 2)
                    act.wait_ge(s_h, n * 16 + (u + 1))
                    for j in range(4):
                        ins = act.activation(dA[:, u % 2, j, :], dt[:, par, d, :], ACT.Exp, scale=A[:, d, 4 * q + j:4 * q + j + 1])
                    ins.then_inc(s_dA, 1)
                    if not last:
                        if u in (4, 5):
                            raw(n + 1, u - 4)
                        if u in (6, 7):
                            silu_z(n + 1, u - 6, 1 - par)
                        if u == 9:
                            silu_x(n + 1, 1 - par)
                        if u == 11:
                            take_xp(n + 1)
                        if u in (13, 14):
                            softplus(n + 1, u - 13, 1 - par, not (isinstance(n, int) and n == 0))
                    if u % 4 == 3 and (q < NQ - 1 or not last):
                        spread_bc(n + (q + 1) // NQ, (q + 1) % NQ)

            for k in range(2):
                raw(0, k)
            for k in range(2):
                silu_z(0, k, 0)
            silu_x(0, 0)
            take_xp(0)
            for k in range(2):
                softplus(0, k, 0, False)
            spread_bc(0, 0)
            act.drain().then_inc(s_wfree, 1)
            ac.straight()
            act_body(0, 0, False)
            act_body(1, 1, False)
            with act.Fori(1, NC // 2 - 1) as i:
                ac.enter((i - 1) * 16)
                act_body(i * 2, 0, False)
                act_body(i * 2 + 1, 1, False)
                ac.leave(NC // 2 - 2, 16)
            act_body(NC - 2, 0, False)
            act_body(NC - 1, 1, True)
            stage_end(act, 6)

        @block.vector
        def _(dve):
            dv = Chain(dve, c_dve)
            dve.wait_ge(s_nrm_ps, 1)
            dv.link(dve.tensor_reduce(nrm[:, 0:1], ps[:, 6:8, 0:512], AX.XY, ALU.max))
            dv.link(dve.tensor_single_scalar(nri[:, 0:1], nrm[:, 0:1].bitcast(I32), 23, ALU.logical_shift_right))
            dv.link(dve.tensor_scalar(nri[:, 2:3], nri[:, 0:1], -126.0, 1.0, ALU.add, ALU.max))
            dv.link(dve.tensor_scalar(nri[:, 3:4], nri[:, 2:3], -1.0, 127.0, ALU.mult, ALU.add))
            dve.tensor_single_scalar(nrm[:, 1:2].bitcast(I32), nri[:, 3:4], 23, ALU.logical_shift_left).then_inc(s_sc, 1)

            def statistics(k):
                v = [sm[:, 6 * k + j, :] for j in range(6)]
                dv.link(dve.tensor_tensor(v[0], st[:, :, 1], st[:, :, 4], ALU.add))
                dv.link(dve.tensor_tensor(v[1], st[:, :, 1], st[:, :, 4], ALU.subtract))
                dv.link(dve.tensor_tensor(v[4], v[1], v[1], ALU.mult))
                dv.link(dve.tensor_tensor(v[5], st[:, :, 2], st[:, :, 5], ALU.add))
                dv.link(dve.tensor_scalar(v[5], v[5], 1.0 / D, EPS, ALU.mult, ALU.add))
                dve.scalar_tensor_tensor(out=v[2], in0=v[4], scalar=0.25, in1=v[5], op0=ALU.mult, op1=ALU.add).then_inc(s_var, 1)
                dve.wait_ge(s_std, k + 1)
                dv.link(dve.reciprocal(v[4], v[3]))
                dv.link(dve.scalar_tensor_tensor(out=v[5], in0=v[0], scalar=-0.5, in1=v[4], op0=ALU.mult, op1=ALU.mult))

            dve.wait_ge(s_x, 64)
            with dve.Fori(0, NT) as i:
                dv.enter(i)
                dv.mark(dve.bn_stats(st[:, ds(i, 1), :], X[:, ds(i, 1), :]))
                dv.leave(NT, 1)
            dv.settle()
            statistics(0)
            with dve.Fori(0, NT) as i:
                dv.enter(i * 2)
                dv.link(dve.tensor_scalar(XN[:, ds(i, 1), :], X[:, ds(i, 1), :], sm[:, 4, ds(i, 1)], sm[:, 5, ds(i, 1)],
                                          ALU.mult, ALU.add))
                dv.mark(dve.bn_stats(st[:, ds(i, 1), :], XN[:, ds(i, 1), :]))
                dv.leave(NT, 2)
            dv.settle()
            statistics(1)
            dve.sem_inc(s_q3, 1)
            dve.sem_inc(s_vc, 1)
            dve.sem_inc(s_lc, 1)
            stage_end(dve, 1)

            dve.wait_ge(s_w, 9 * 16)
            with dve.Fori(0, NC) as n:
                dv.enter(n * 12)
                dve.wait_ge(s_t2, n + 1)
                for t in range(TPC):
                    i = n * TPC + t
                    dve.tensor_scalar(x2h[:, t, :], XN[:, ds(i, 1), :], sm[:, 10, ds(i, 1)], sm[:, 11, ds(i, 1)],
                                      ALU.mult, ALU.add).then_inc(s_x2h, 1)
                dve.wait_ge(s_t2, n + 2)
                dve.wait_ge(s_lp, n + 1)
                dve.wait_ge(s_x2t, n + 1)
                for k in range(KD):
                    dve.tensor_scalar(x2c[:, k, :], ps[:, 2 + k, :], lng[:, 0, k:k + 1], lng[:, 1, k:k + 1],
                                      ALU.mult, ALU.add).then_inc(s_x2c, 1)
                dve.wait_ge(s_qd, n * 64 + 64)
                for m in range(4):
                    dve.wait_ge(s_qf, n * 4 + (m + 3))
                    dv.link(dve.tensor_copy(q3[:, m, 0, :], qf[:, m % 2, :]))
                    dv.link(dve.tensor_tensor(qr[:, :], qf[:, m % 2, :], q3[:, m, 0, :], ALU.subtract))
                    dv.link(dve.tensor_copy(q3[:, m, 1, :], qr[:, :]))
                    dve.tensor_tensor(q3[:, m, 2, :], qr[:, :], q3[:, m, 1, :], ALU.subtract).then_inc(s_q3, 1)
                    dve.wait_ge(s_q3, n * 4 + (m + 2))
                dve.wait_ge(s_vp, n + 2)
                dve.wait_ge(s_vd, n * 16 + 16)
                dve.tensor_copy(Vc[:, :, :], ps[:, 6:8, :].rearrange("p k (t n) -> p (k t) n", n=D)).then_inc(s_vc, 1)
                dve.wait_ge(s_lp, n + 2)
                dve.tensor_copy(lgt[:, ds(n * TPC, TPC), :], ps[:, 2, 0:TPC * E].rearrange("p (t e) -> p t e", e=E)).then_inc(s_lc, 1)
                dv.leave(NC, 12)
            dve.wait_ge(s_lc, NC + 1)
            dv.settle()
            rank, tmp, s0, s1 = (top[:, k, :, :] for k in range(4))
            dv.link(dve.memset(rank, 0.0))
            for e in range(E):
                big = lgt[:, :, e:e + 1]
                dv.mark(dve.tensor_tensor(tmp[:, :, 0:e + 1], big.broadcast_to([P, NT, e + 1]), lgt[:, :, 0:e + 1], ALU.is_gt))
                if e + 1 < E:
                    dv.mark(dve.tensor_tensor(tmp[:, :, e + 1:E], big.broadcast_to([P, NT, E - e - 1]), lgt[:, :, e + 1:E], ALU.is_ge))
                dv.settle()
                dv.link(dve.tensor_tensor(rank, rank, tmp, ALU.add))
            dv.mark(dve.tensor_scalar(s0, rank, 0.0, None, ALU.is_equal))
            dv.mark(dve.tensor_scalar(s1, rank, 1.0, None, ALU.is_equal))
            dv.settle()
            dv.link(dve.tensor_tensor(tmp, s1, s0, ALU.subtract))
            dv.link(dve.tensor_tensor(tmp, tmp, lgt[:, :, :], ALU.mult))
            dve.tensor_reduce(sm[:, 1, :], tmp, AX.X, ALU.add).then_inc(s_top, 1)
            dve.wait_ge(s_tex, 1)
            dv.link(dve.tensor_scalar(sm[:, 3, :], sm[:, 2, :], 1.0, None, ALU.add))
            dv.link(dve.reciprocal(sm[:, 4, :], sm[:, 3, :]))
            dv.link(dve.tensor_tensor(sm[:, 5, :], sm[:, 2, :], sm[:, 4, :], ALU.mult))

            def per_token(v):
                return v.rearrange("p (t a) -> p t a", a=1).broadcast_to([P, NT, E])

            dv.link(dve.tensor_tensor(s0, s0, per_token(sm[:, 4, :]), ALU.mult))
            dv.link(dve.tensor_tensor(s1, s1, per_token(sm[:, 5, :]), ALU.mult))
            dv.link(dve.tensor_tensor(wd[:, :, :], s0, s1, ALU.add))
            stage_end(dve, 2)

            def ring(gm, gx, base, plan):
                for r, u in enumerate(ring_of(plan)):
                    slot = ps[:, 2 * (r % 2):2 * (r % 2) + 2, :].rearrange("p a n -> p (a n)")
                    dve.wait_ge(s_full, base + (r + 1))
                    if u[0] == "max":
                        _, h, t, k0, n = u
                        qc = t // TPC
                        dve.tensor_reduce(mp[:, qc, h, t % TPC, k0 // 1024:k0 // 1024 + 1], slot[:, 0:n], AX.X, ALU.max).then_inc(s_free, 1)
                        if (h, t) == (HG - 1, TPC * (qc + 1) - 1) and k0 + n == P * (t + 1):
                            dve.wait_ge(s_free, base + (r + 1))
                            w = 2 if qc * CH >= 1024 else 1
                            dve.tensor_reduce(mn[:, qc, :], mp[:, qc, :, :, 0:w].rearrange("p h t w -> p (h t) w"), AX.X,
                                              ALU.max, negate=True).then_inc(s_mn, 1)
                            dve.wait_ge(s_mn, gm * CPB + (qc + 1))
                    elif u[0] == "turn":
                        qc = u[1]
                        if plan is not FIRST_PLAN:
                            dve.wait_ge(s_mrow[qc], gm * 16)
                        v = slot[0:HG * TPC, 0:P]
                        dv.link(dve.tensor_copy(n3[:, qc, 0, :], v))
                        dve.tensor_tensor(nr[:, :], v, n3[:, qc, 0, :], ALU.subtract).then_inc(s_free, 1)
                        dve.wait_ge(s_free, base + (r + 1))
                        dv.link(dve.tensor_copy(n3[:, qc, 1, :], nr[:, :]))
                        dve.tensor_tensor(n3[:, qc, 2, :], nr[:, :], n3[:, qc, 1, :], ALU.subtract).then_inc(s_mr, 1)
                        dve.wait_ge(s_mr, gm * CPB + (qc + 1))
                    else:
                        qc = u[1]
                        v = slot[:, 0:CH].rearrange("p (t h c) -> p t h c", t=TPC, h=HG)
                        dv.link(dve.reciprocal(rec[:, :, :], v[:, :, :, HS]))
                        dve.wait_ge(s_aod, gx * (16 * CPB) + (qc + 1) * 16)
                        o = ao[:, :, :].rearrange("p t (h d) -> p t h d", h=HG)
                        r4 = rec[:, :, :].rearrange("p t (h a) -> p t h a", a=1).broadcast_to([P, TPC, HG, HS])
                        dve.tensor_tensor(o, v[:, :, :, 0:HS], r4, ALU.mult).then_inc(s_free, 1)
                        dve.wait_ge(s_free, base + (r + 1))

            ring(0, None, 0, FIRST_PLAN)
            with dve.Fori(0, NG - 1) as g:
                dv.enter(g * 12)
                ring(g + 1, g, g * NR + NM, FULL_PLAN)
                dv.leave(NG - 1, 12)
            ring(None, NG - 1, NM + (NG - 1) * NR, LAST_PLAN)
            stage_end(dve, 3)

            dve.sem_inc(s_moe, 4)
            dve.wait_ge(s_mz, 1)
            with dve.Fori(0, E) as e:
                with dve.Fori(0, NC) as c:
                    u = e * NC + c
                    for t in range(TPC):
                        i = c * TPC + t
                        dve.wait_ge(s_op, u * TPC + (2 * TPC + t + 1))
                        dve.wait_ge(s_moe, u * TPC + (t + 1))
                        dve.scalar_tensor_tensor(out=moe[:, ds(i, 1), :], in0=ps[:, 4 + t, 0:D], scalar=wd[:, ds(i, 1), ds(e, 1)],
                                                 in1=moe[:, ds(i, 1), :], op0=ALU.mult, op1=ALU.add).then_inc(s_moe, 1)
            stage_end(dve, 4)

            dve.sem_inc(s_cx, 1)
            dve.wait_ge(s_cw, 5 * 16)
            with dve.Fori(0, NC // 2) as i:
                dv.enter(i * 32)
                for par in range(2):
                    c = i * 2 + par
                    big = [P, TPC, D]
                    dve.wait_ge(s_ci[par], (i + 1) * 64)
                    dve.tensor_copy(wdc[:, :, :], wd[:, ds(c * TPC, TPC), :]).then_inc(s_cwd, 1)
                    abel = inx[:, par, 2, :, :]
                    dv.link(dve.tensor_tensor(cmb[:, 2, :, :], abel, mixw[:, 0:1, :].broadcast_to(big), ALU.mult))
                    dv.link(dve.tensor_reduce(gate[:, 0, :], cmb[:, 2, :, :], AX.X, ALU.add))
                    dve.wait_ge(s_cpr, c * 2 + 1)
                    dve.tensor_tensor(mot[:, :, :], moe[:, ds(c * TPC, TPC), :], ps[:, 6:8, :].rearrange("p k (t n) -> p (k t) n", n=D),
                                      ALU.add).then_inc(s_cmo, 1)
                    dve.wait_ge(s_cpr, c * 2 + 2)
                    dve.wait_ge(s_cb, c + 1)
                    dv.link(dve.tensor_tensor(cmb[:, 3, :, :], cmb[:, 1, :, :], ps[:, 4:6, :].rearrange("p k (t n) -> p (k t) n", n=D), ALU.add))
                    dve.wait_ge(s_cnb, c + 1)
                    nonabel = ps[:, 2:4, :].rearrange("p k (t n) -> p (k t) n", n=D)
                    dv.link(dve.tensor_tensor(cmb[:, 2, :, :], nonabel, mixw[:, 1:2, :].broadcast_to(big), ALU.mult))
                    dv.link(dve.tensor_reduce(gate[:, 1, :], cmb[:, 2, :, :], AX.X, ALU.add))
                    dve.tensor_tensor(gate[:, 2, :], gate[:, 0, :], gate[:, 1, :], ALU.add).then_inc(s_cz, 1)
                    dv.link(dve.tensor_tensor(cmb[:, 2, :, :], nonabel, abel, ALU.subtract))
                    dve.wait_ge(s_cg, c + 1)
                    g4 = gate[:, 3, :].rearrange("p (t a) -> p t a", a=1).broadcast_to(big)
                    dv.link(dve.tensor_tensor(cmb[:, 2, :, :], cmb[:, 2, :, :], g4, ALU.mult))
                    dve.wait_ge(s_co, c * 16 + 16)
                    dve.tensor_tensor(x1c[:, :, :], cmb[:, 2, :, :], cmb[:, 3, :, :], ALU.add).then_inc(s_cx, 1)
                    dve.wait_ge(s_cx, c + 2)
                    for t in range(TPC):
                        dv.mark(dve.bn_stats(x1s[:, t, :], x1c[:, t, :]))
                    dv.settle()
                    alone(dve)
                    for t in range(TPC):
                        dv.mark(dve.bn_aggr(x1v[:, t, :], x1s[:, t, :]))
                    dv.settle()
                    dve.tensor_scalar(x1r[:, 0, :], x1v[:, :, 1], EPS, None, ALU.add).then_inc(s_x1s, 1)
                    dve.wait_ge(s_x1q, c + 1)
                    dv.link(dve.reciprocal(x1r[:, 2, :], x1r[:, 1, :]))
                    for t in range(TPC):
                        dve.tensor_scalar(x1n[:, t, :], x1c[:, t, :], x1v[:, t, 0:1], x1r[:, 2, t:t + 1],
                                          ALU.subtract, ALU.mult).then_inc(s_x1n, 1)
                    dve.wait_ge(s_x1n, c * TPC + TPC)
                dv.leave(NC // 2, 2 * (7 + 9))
            stage_end(dve, 5)

            dve.sem_inc(s_bc3, 1)
            dve.sem_inc(s_sp, 1)
            dve.sem_inc(s_y, KI)
            dve.sem_inc(s_bu, 8)
            dve.sem_inc(s_h, 2)
            dve.sem_inc(s_tail, 1)
            dve.wait_ge(s_abs, 2)
            dve.tensor_tensor(tsum[:, 2:3], tsum[:, 0:1], tsum[:, 1:2], ALU.add).then_inc(s_tern, 1)
            dve.wait_ge(s_tps, 1)
            dv.link(dve.tensor_scalar(tsum[:, 3:4], ps[:, 0, 0:1], 0.7 / (D * D), None, ALU.mult))
            dv.link(dve.tensor_scalar(tsum[:, 4:5], tsum[:, 3:4], -1.0, None, ALU.mult))
            dv.mark(dve.tensor_scalar(tq[:, :, :], tw[:, :, :], tsum[:, 3:4], None, ALU.is_gt))
            dv.link(dve.tensor_scalar(tw[:, :, :], tw[:, :, :], tsum[:, 4:5], None, ALU.is_lt))
            dv.link(dve.tensor_tensor(tw[:, :, :], tq[:, :, :], tw[:, :, :], ALU.subtract))
            dve.tensor_scalar(tw[:, :, :], tw[:, :, :], alph[:, 0:1], None, ALU.mult).then_inc(s_tern, 1)
            dve.wait_ge(s_setup, 1)
            dve.wait_ge(s_lw, 12 * 16)

            def conv(m, k, par):
                dve.wait_ge(s_wfree, m * 8 + (k + 2))
                for d in range(2 * k, 2 * k + 2):
                    o = xs[:, par, d, :]
                    dv.link(dve.tensor_scalar(o, xraw[:, d, 0:CH], cw[:, d, 0:1], None, ALU.mult))
                    for j in range(1, TAPS):
                        ins = dve.scalar_tensor_tensor(out=o, in0=xraw[:, d, j:j + CH], scalar=cw[:, d, j:j + 1], in1=o,
                                                       op0=ALU.mult, op1=ALU.add)
                        if j < TAPS - 1:
                            dv.link(ins)
                    ins.then_inc(s_conv, 1)
                if k == 1:
                    dve.wait_ge(s_conv, m * KI + KI)
                    dve.tensor_scalar(xraw[:, :, 0:TAPS - 1], xraw[:, :, CH:], flag[:, ds(m + 1, 1)], None, ALU.mult).then_inc(s_tail, 1)

            def split_bc(m, par):
                dve.wait_ge(s_wfree, m * 8 + 6)
                v = xps[0:2 * NS, :]
                dv.link(dve.tensor_copy(bc3[0:2 * NS, par, :], v))
                dv.link(dve.tensor_tensor(bcr[:, :], v, bc3[0:2 * NS, par, :], ALU.subtract))
                dv.link(dve.tensor_copy(bc2[:, :], bcr[:, :]))
                dv.mark(dve.tensor_tensor(bc3[4 * NS:6 * NS, par, :], bcr[:, :], bc2[:, :], ALU.subtract))
                dve.tensor_copy(bc3[2 * NS:4 * NS, par, :], bc2[:, :]).then_inc(s_bc3, 1)

            def step_size(m, k, par):
                two = slice(2 * k, 2 * k + 2)
                dve.wait_ge(s_poly, m * 2 + (k + 1))
                small = te[:, :, :].bitcast(I32)
                dv.link(dve.tensor_scalar(small, te[:, :, :], 2.0 ** -6, None, ALU.is_lt))
                alone(dve)
                dv.link(dve.copy_predicated(tl[:, :, :], small, dtx[:, par, two, :]))
                dve.tensor_tensor(dt[:, par, two, :], dt[:, par, two, :], tl[:, :, :], ALU.add).then_inc(s_sp, 1)
                dve.wait_ge(s_sp, m * 2 + (k + 2))
                dve.wait_ge(s_xs, m * KI + KI)
                dve.tensor_tensor(dtx[:, par, two, :], dt[:, par, two, :], xs[:, par, two, :], ALU.mult).then_inc(s_dt, 1)

            def skip(n, par):
                dve.wait_ge(s_acc, n * 16 + 20)
                for d in range(KI):
                    dve.scalar_tensor_tensor(out=xs[:, par, d, :], in0=xs[:, par, d, :], scalar=Dv[:, d:d + 1], in1=ps[:, d, :],
                                             op0=ALU.mult, op1=ALU.add).then_inc(s_y, 1)

            def add(n, job):
                dve.wait_ge(s_wfull, job + 1)
                dve.wait_ge(s_xo, n * 16 + 16)
                dve.tensor_tensor(xo[:, :, :], xo[:, :, :], ps[:, 4:6, :].rearrange("p k (t n) -> p (k t) n", n=D), ALU.add)\
                    .then_inc(s_add, 1)
                dve.wait_ge(s_add, n + 1)
                dve.sem_inc(s_wfree, 1)

            def dve_body(n, par, first, last):
                for u in range(4 * NQ):
                    q, d = u // 4, u % 4
                    if u == 0:
                        dve.wait_ge(s_dt, n * 2 + 2)
                    if d == 0:
                        dve.wait_ge(s_cfree, n * 32 + (8 * q + 4 + 2))
                    dve.wait_ge(s_acc, n * 16 + (u + 1))
                    h = hh[:, u % 4, :, :]
                    x4 = dtx[:, par, d:d + 1, :].broadcast_to([P, 4, CH])
                    dve.tensor_tensor(h, x4, Bq[:, q % 2, :, :], ALU.mult).then_inc(s_bu, 1)
                    dve.wait_ge(s_bu, n * 16 + (u + 1 + 8))
                    dve.wait_ge(s_dA, n * 16 + (u + 1))
                    dve.wait_ge(s_h, n * 16 + (u + 2))
                    for j in range(4):
                        ins = dve.tensor_tensor_scan(h[:, j, :], dA[:, u % 2, j, :], h[:, j, :], hst[:, u, j:j + 1], ALU.mult, ALU.add)
                    dv.link(ins)
                    dve.tensor_scalar(hst[:, u, :], h[:, :, CH - 1], flag[:, ds(n + 1, 1)], None, ALU.mult).then_inc(s_h, 1)
                    if u == 1 and not first:
                        skip(n - 1, 1 - par)
                    if u == 4 and not first:
                        add(n - 1, n * 8 + 7)
                    if last:
                        continue
                    if u in (5, 6):
                        conv(n + 1, u - 5, 1 - par)
                    if u == 11:
                        split_bc(n + 1, 1 - par)
                    if u in (14, 15):
                        step_size(n + 1, u - 14, 1 - par)

            for k in range(2):
                conv(0, k, 0)
            split_bc(0, 0)
            for k in range(2):
                step_size(0, k, 0)
            dv.straight()
            dve_body(0, 0, True, False)
            dve_body(1, 1, False, False)
            with dve.Fori(1, NC // 2 - 1) as i:
                dv.enter((i - 1) * 72)
                dve_body(i * 2, 0, False, False)
                dve_body(i * 2 + 1, 1, False, False)
                dv.leave(NC // 2 - 2, 72)
            dve_body(NC - 2, 0, False, False)
            dve_body(NC - 1, 1, False, True)
            skip(NC - 1, 1)
            add(NC - 1, NC * 8)
            stage_end(dve, 6)

        @block.tensor
        def _(pe):
            def mm(o, lhsT, rhs, start=True, stop=True, **kw):
                return pe.matmul(o, lhsT, rhs, start=start, stop=stop, **kw)

            def half(bank, m):
                return ps[:, bank, m * D:(m + 1) * D]

            pe.wait_ge(s_const, 6 + TAYLOR)
            pe.wait_ge(s_nrm_abs, 1)
            for g in range(NROT + 1):
                for k in range(KD):
                    last = mm(half(6 + g // 2, g % 2), ones_s[:, :], gb[:, min(g, NROT - 1), k, :], k == 0, k == KD - 1)
            last.then_inc(s_nrm_ps, 1)
            pe.wait_ge(s_scaled, 2)
            for k in range(TAYLOR, 0, -1):
                for g in range(NROT):
                    if k < TAYLOR:
                        pe.wait_ge(s_hev, (TAYLOR - 1 - k) * NROT + g + 1)
                    for m in range(KD):
                        mm(half(g, m), idb[:, :], kid[:, k - 1, m, :], True, False)
                        if k == TAYLOR:
                            last = mm(half(g, m), idf[:, :], er[:, g, m, :], False, True)
                        else:
                            for j in range(KD):
                                last = mm(half(g, m), gb[:, g, j, m * P:(m + 1) * P], er[:, g, j, :], False, j == KD - 1)
                    last.then_inc(s_hor, 1)
            for g in range(NROT):
                pe.wait_ge(s_hev, (TAYLOR - 1) * NROT + g + 1)
                for m in range(KD):
                    for j in range(KD):
                        last = pe.transpose(ps[:, 3 + g, m * D + j * P:m * D + (j + 1) * P], er[:, g, j, m * P:(m + 1) * P], idf[:, :])
                last.then_inc(s_hor, 1)
            pe.wait_ge(s_hev, (TAYLOR + 1) * NROT)
            squarings = pe.value_load(nri[0:1, 2:3], min_val=1, max_val=200)
            pe.sem_inc(s_sqe, 2 * NROT)
            with pe.Fori(0, squarings) as i:
                for g in range(NROT):
                    pe.wait_ge(s_sqe, i * (2 * NROT) + 2 * (g + 1))
                    for m in range(KD):
                        for j in range(KD):
                            mm(half(g, m), et[:, g, j, m * P:(m + 1) * P], er[:, g, j, :], j == 0, j == KD - 1)
                    for m in range(KD):
                        for j in range(KD):
                            last = mm(half(3 + g, m), er[:, g, j, m * P:(m + 1) * P], et[:, g, j, :], j == 0, j == KD - 1)
                    last.then_inc(s_sqp, 1)
            pe.wait_ge(s_sqe, squarings * (2 * NROT) + 2 * NROT)
            for m in range(KD):
                for j in range(KD):
                    last = mm(half(6, m), er[:, 1, j, m * P:(m + 1) * P], et[:, 0, j, :], j == 0, j == KD - 1)
            last.then_inc(s_fin, 1)
            pe.wait_ge(s_fev, 1)
            for m in range(KD):
                for j in range(KD):
                    last = mm(half(7, m), gb[:, 0, j, m * P:(m + 1) * P], er[:, 2, j, :], j == 0, j == KD - 1)
            last.then_inc(s_fin, 1)
            stage_end(pe, 1)

            pe.sem_inc(s_tx, 1)
            pe.sem_inc(s_t2, 1)
            pe.sem_inc(s_vp, 1)
            pe.sem_inc(s_lp, 1)
            pe.wait_ge(s_w, 9 * 16)
            with pe.Fori(0, NC) as n:
                for src, bank, got, done, free in ((XNc, 0, (s_xnc, n + 1), s_tx, s_ac), (x2h, 2, (s_x2h, n * 4 + 4), s_t2, s_lc)):
                    pe.wait_ge(*got)
                    pe.wait_ge(free, n + 1)
                    for t in range(TPC):
                        for k in range(KD):
                            last = pe.transpose(ps[:, bank + k, t * P:(t + 1) * P], src[:, t, k * P:(k + 1) * P], idf[:, :])
                    last.then_inc(done, 1)
                pe.wait_ge(s_xT, n + 1)
                for m in range(4):
                    pe.wait_ge(s_qf, n * 4 + (m + 1))
                    for k in range(KD):
                        last = mm(ps[:, 4 + m % 2, :], wqkv[:, k, m * P:(m + 1) * P], xTc[:, k, :], k == 0, k == KD - 1)
                    last.then_inc(s_qp, 1)
                pe.wait_ge(s_vc, n + 1)
                for t in range(TPC):
                    o = half(6 + t // 2, t % 2)
                    for k in range(KD):
                        mm(o, xTc[:, k, t * P:(t + 1) * P], wqkv[:, k, 2 * D:3 * D], k == 0, False)
                    last = mm(o, ones_r[:, :], bv[:, :], False, True)
                last.then_inc(s_vp, 1)
                pe.wait_ge(s_x2c, n * KD + KD)
                for t in range(TPC):
                    o = half(t // 2, t % 2)
                    for k in range(KD):
                        mm(o, x2c[:, k, t * P:(t + 1) * P], wab[:, k, :], k == 0, False)
                    last = mm(o, ones_r[:, :], bab[:, :], False, True)
                last.then_inc(s_ap, 1)
                for t in range(TPC):
                    o = ps[:, 2, t * E:(t + 1) * E]
                    for k in range(KD):
                        mm(o, x2c[:, k, t * P:(t + 1) * P], wg[:, k, :], k == 0, False)
                    last = mm(o, ones_r[:, :], bg[:, :], False, True)
                last.then_inc(s_lp, 1)
            stage_end(pe, 2)

            pe.sem_inc(s_pv, 2)

            def attention(g, gm, base, plan, par, loads):
                r = 0
                for u in plan:
                    if u[0] == "score":
                        n = u[1]
                        h, qc, kt, q0 = EU[n]
                        if n == 0 or EU[n - 1][1] != qc:
                            pe.wait_ge(s_mrow[qc], g * 16 + 16)
                        back = n - SRING if n >= SRING else max(k for k in range(NE) if k % SRING == n) - NE
                        pe.wait_ge(s_exp, g * NE + (back + 1 + NE))
                        o = ps[:, 4 + n % SRING, q0:CH]
                        diagonal = kt >= TPC * qc
                        last = mm(o, ks[0:FULL, par, h, kt * P:(kt + 1) * P], qs[0:FULL, par, h, qc * CH + q0:(qc + 1) * CH],
                                  True, not diagonal)
                        if diagonal:
                            last = mm(ps[:, 4 + n % SRING, q0:q0 + P], idb[:, :], mask_k[:, :], False, True)
                        last.then_inc(s_score, 1)
                        continue
                    if u[0] == "pv":
                        step = u[1]
                        _, qc, kt, q0 = EU[HG * step]
                        pe.wait_ge(s_exp, g * NE + (HG * (step + 1) + NE))
                        if step == 0:
                            pe.wait_ge(s_vg, g + 1)
                        if kt == 0:
                            pe.wait_ge(s_oT, g * CPB + (qc + 1))
                        for h in range(HG):
                            last = mm(ps[32 * h:32 * h + 32, 7, q0:CH], vg[:, par, kt, h, :], Pt[:, (HG * step + h) % PRING, q0:CH],
                                      kt == 0, kt == TPC * (qc + 1) - 1, tile_position=(0, 32 * h))
                        last.then_inc(s_pv, 1)
                        continue
                    bank = 2 * (r % 2)
                    if not (isinstance(base, int) and base + r < 2):
                        pe.wait_ge(s_free, base + (r - 1))
                    if u[0] == "max":
                        _, h, t, k0, n = u
                        if r == 0:
                            pe.wait_ge(s_qk[1 - par], loads)
                        for j in range(0, n, 512):
                            w = min(512, n - j)
                            diagonal = k0 + j + w == P * (t + 1)
                            last = mm(ps[:, bank + j // 512, 0:w], qs[0:ROWS, 1 - par, h, t * P:(t + 1) * P],
                                      ks[0:ROWS, 1 - par, h, k0 + j:k0 + j + w], True, not diagonal)
                            if diagonal:
                                last = mm(ps[:, bank + j // 512, w - P:w], idb[:, :], mask_q[:, :], False, True)
                    elif u[0] == "turn":
                        pe.wait_ge(s_mn, gm * CPB + (u[1] + 1))
                        last = pe.transpose(ps[0:HG * TPC, bank, 0:P], mn[:, u[1], :], idf[:, :])
                    else:
                        pe.wait_ge(s_oT, g * CPB + (u[1] + 2))
                        for t in range(TPC):
                            last = pe.transpose(ps[:, bank, t * P:(t + 1) * P], oT[:, t * P:(t + 1) * P], idf[:, :])
                    last.then_inc(s_full, 1)
                    r += 1

            pe.wait_ge(s_stack, 1)
            attention(None, 0, 0, FIRST_PLAN, 1, 192)
            with pe.Fori(0, NG // 2 - 1) as i:
                for par in range(2):
                    g = i * 2 + par
                    attention(g, g + 1, g * NR + NM, FULL_PLAN, par, i * 192 + 192 * (par + 1))
            attention(NG - 2, NG - 1, NM + (NG - 2) * NR, FULL_PLAN, 0, NG // 2 * 192)
            attention(NG - 1, None, NM + (NG - 1) * NR, LAST_PLAN, 1, None)
            stage_end(pe, 3)

            pe.sem_inc(s_op, 2 * TPC)

            def hidden(u, c, par):
                for f in range(KF):
                    pe.wait_ge(s_hT, u * KF + (f + 1))
                    for k in range(KD):
                        last = mm(ps[:, f % 4, :], W1[:, par, k, f * P:(f + 1) * P], xn2T[:, k, ds(c * CH, CH)], k == 0, k == KD - 1)
                    last.then_inc(s_hp, 1)

            def down(u, slot, par):
                pe.wait_ge(s_hT, u * KF + (KF + 4))
                for t in range(TPC):
                    pe.wait_ge(s_moe, u * TPC + (t + 1))
                    for f in range(KF):
                        last = mm(ps[:, 4 + t, 0:D], hT[:, slot, f, t * P:(t + 1) * P], W2[:, par, f, :], f == 0, f == KF - 1)
                    last.then_inc(s_op, 1)

            with pe.Fori(0, E // 2) as i:
                for par in range(2):
                    pe.wait_ge(s_ew[par], i * 32 + 32)
                    alone(pe)
                    with pe.Fori(0, NC // 4) as j:
                        for c in range(4):
                            u = (i * 2 + par) * NC + j * 4 + c
                            hidden(u, j * 4 + c, par)
                            if c:
                                down(u - 1, (c - 1) % 2, par)
                        down((i * 2 + par) * NC + j * 4 + 3, 1, par)
            stage_end(pe, 4)

            pe.wait_ge(s_cw, 5 * 16)
            with pe.Fori(0, NC // 2) as i:
                for par in range(2):
                    c = i * 2 + par
                    pe.wait_ge(s_ci[par], (i + 1) * 64)
                    pe.wait_ge(s_cwd, c + 1)
                    pe.wait_ge(s_cx, c + 1)
                    for t in range(TPC):
                        for k in range(KD):
                            pe.transpose(ps[:, k, t * P:(t + 1) * P], inx[:, par, 3, t, k * P:(k + 1) * P], idf[:, :])
                        last = pe.transpose(ps[0:E, 2, t * P:(t + 1) * P], wdc[:, t, :], idf[:, :])
                    last.then_inc(s_ctp, 1)
                    pe.wait_ge(s_cT, c * 2 + 2)
                    for t in range(TPC):
                        last = mm(half(6 + t // 2, t % 2), wdT[:, t * P:(t + 1) * P], B2[:, :])
                    last.then_inc(s_cpr, 1)
                    for t in range(TPC):
                        o = half(4 + t // 2, t % 2)
                        for k in range(KD):
                            mm(o, atT[:, k, t * P:(t + 1) * P], wpj[:, k, :], k == 0, False)
                        last = mm(o, ones_r[:, :], bpj[:, :], False, True)
                    last.then_inc(s_cpr, 1)
                    pe.wait_ge(s_cmo, c + 1)
                    for t in range(TPC):
                        for k in range(KD):
                            last = pe.transpose(ps[:, k, t * P:(t + 1) * P], mot[:, t, k * P:(k + 1) * P], idf[:, :])
                    last.then_inc(s_cmp, 1)
                    pe.wait_ge(s_cmT, c + 1)
                    for t in range(TPC):
                        for k in range(KD):
                            last = mm(half(2 + t // 2, t % 2), moT[:, k, t * P:(t + 1) * P], rot[:, k, :], k == 0, k == KD - 1)
                    last.then_inc(s_cnb, 1)
                    pe.wait_ge(s_x1n, c * TPC + TPC)
                    for t in range(TPC):
                        for k in range(KD):
                            last = pe.transpose(ps[:, k, t * P:(t + 1) * P], x1n[:, t, k * P:(k + 1) * P], idf[:, :])
                    last.then_inc(s_x1t, 1)
                    pe.wait_ge(s_x1T, c + 1)
            stage_end(pe, 5)

            pe.wait_ge(s_lw, 12 * 16)
            pe.wait_ge(s_setup, 1)
            pe.wait_ge(s_tern, 1)
            mm(ps[:, 0, 0:1], onef[:, :], tsum[:, 2:3]).then_inc(s_tps, 1)
            pe.wait_ge(s_tern, 2)

            def job(n, what):
                pe.wait_ge(s_wfree, n + 1)
                what().then_inc(s_wfull, 1)

            def project(m, k, par):
                def what():
                    for j in range(2):
                        c = 2 * k + j
                        for i in range(KD):
                            last = mm(ps[:, 4 + j, :], inw[:, i, c * P:(c + 1) * P], xin[:, par, i, :], i == 0, i == KD - 1)
                    return last
                job(m * 8 + k, what)

            def project_xp(m, par):
                def what():
                    for d in range(KI):
                        last = mm(ps[0:NX, 4, :], xpw[:, d, :], xs[:, par, d, :], d == 0, d == KI - 1)
                    return last
                pe.wait_ge(s_xs, m * KI + KI)
                job(m * 8 + 4, what)

            def project_dt(m, k):
                def what():
                    for j in range(2):
                        d = 2 * k + j
                        last = mm(ps[:, 4 + j, :], dtw[2 * NS:, d * P:(d + 1) * P], xps[2 * NS:, :], tile_position=(2 * NS, 0))
                    return last
                job(m * 8 + (5 + k), what)

            def output(n, par, at):
                def what():
                    for t in range(TPC):
                        o = half(4 + t // 2, t % 2)
                        for d in range(KI):
                            mm(o, xs[:, par, d, t * P:(t + 1) * P], outw[:, d, :], d == 0, False)
                        for k in range(KD):
                            mm(o, xin[:, par, k, t * P:(t + 1) * P], tw[:, k, :], False, False)
                        last = mm(o, ones_r[:, :], tb[:, :], False, True)
                    return last
                pe.wait_ge(s_yz, n + 3)
                job(at, what)

            def broadcast(n, q, par):
                if q == 0:
                    pe.wait_ge(s_bc3, n + 2)
                for k in range(8):
                    pe.wait_ge(s_cfree, n * 32 + (q * 8 + k + 1))
                    r = (NS if k >= 4 else 0) + 4 * q + k % 4
                    mm(ps[:, 6 + k % 2, :], sel[:, r, :], bc3[:, par, :]).then_inc(s_cfull, 1)

            def accumulate(n, u):
                q, d = u // 4, u % 4
                pe.wait_ge(s_hc, n * 16 + (u + 1 + 8))
                if q == 0:
                    pe.wait_ge(s_y, n * KI + (d + 1))
                for j in range(4):
                    last = mm(ps[:, d, :], idf[:, :], hh[:, u % 4, j, :], q == 0 and j == 0, q == NQ - 1 and j == 3)
                last.then_inc(s_acc, 1)

            def pe_body(n, par, first, last):
                for u in range(4 * NQ):
                    if not last:
                        if u in (2, 3, 4, 5):
                            if u == 2:
                                pe.wait_ge(s_xin[1 - par], (n + 1) // 2 * 16 + 16)
                            project(n + 1, u - 2, 1 - par)
                        if u == 8:
                            project_xp(n + 1, 1 - par)
                        if u in (9, 10):
                            project_dt(n + 1, u - 9)
                    if u % 4 == 1 and (u < 13 or not last):
                        q = u // 4 + 1
                        broadcast(n + q // NQ, q % NQ, par if q < NQ else 1 - par)
                    accumulate(n, u)
                    if u == 1 and not first:
                        output(n - 1, 1 - par, n * 8 + 7)

            pe.sem_inc(s_acc, 4)
            pe.wait_ge(s_xin[0], 16)
            for k in range(4):
                project(0, k, 0)
            project_xp(0, 0)
            for k in range(2):
                project_dt(0, k)
            pe.drain().then_inc(s_wfull, 1)
            broadcast(0, 0, 0)
            pe_body(0, 0, True, False)
            pe_body(1, 1, False, False)
            with pe.Fori(1, NC // 2 - 1) as i:
                pe_body(i * 2, 0, False, False)
                pe_body(i * 2 + 1, 1, False, False)
            pe_body(NC - 2, 0, False, False)
            pe_body(NC - 1, 1, False, True)
            output(NC - 1, 1, NC * 8)
            stage_end(pe, 6)


_ORDER = ["L0_attn_x", "L0_attn_c_attn_w", "L0_attn_c_attn_b", "L0_attn_c_proj_w", "L0_attn_c_proj_b",
          "L0_ffn_ln_g", "L0_ffn_ln_b", "L0_ffn_abel_w", "L0_ffn_abel_b", "L0_ffn_gate_w_moe", "L0_ffn_gate_b_moe",
          "L0_ffn_w1", "L0_ffn_b1", "L0_ffn_w2", "L0_ffn_b2", "L0_ffn_gens", "gens_transposed",
          "L0_ffn_mix_w", "L0_ffn_mix_b", "in_proj_transposed", "L1_attn_conv_w", "L1_attn_conv_b",
          "x_proj_transposed", "dt_proj_transposed", "L1_attn_dt_proj_b", "L1_attn_A_log", "L1_attn_D",
          "out_proj_transposed", "ternary_transposed", "L1_ffn_alpha", "L1_ffn_bias"]


def kernel(**inputs):
    import numpy as _np
    import concourse.bacc as _bacc
    from concourse import mybir as _mybir
    from concourse.bass_utils import run_bass_kernel_spmd as _run

    laid = dict(inputs)
    laid["gens_transposed"] = _np.asarray(inputs["L0_ffn_gens"]).transpose(0, 2, 1)
    for name, source in (("in_proj_transposed", "L1_attn_in_proj_w"), ("x_proj_transposed", "L1_attn_x_proj_w"),
                         ("dt_proj_transposed", "L1_attn_dt_proj_w"), ("out_proj_transposed", "L1_attn_out_proj_w"),
                         ("ternary_transposed", "L1_ffn_weight")):
        laid[name] = _np.asarray(inputs[source]).T
    laid["x_proj_transposed"] = _np.roll(laid["x_proj_transposed"], -RANK, axis=1)
    nc = _bacc.Bacc("TRN2", target_bir_lowering=False, num_devices=1)
    arrays, args = {}, []
    for name in _ORDER:
        a = _np.ascontiguousarray(laid[name])
        arrays[f"in_{name}"] = a
        args.append(nc.dram_tensor(f"in_{name}", a.shape, _mybir.dt.from_np(a.dtype), kind="ExternalInput").ap())
    args.append(nc.dram_tensor("out_0", (B, S, D), F32, kind="ExternalOutput").ap())
    build(nc, *args)
    r = _run(nc, [arrays], core_ids=[0])
    return r.results[0]["out_0"]
```

```python
from contextlib import ExitStack

import concourse.bass as bass
from concourse import mybir

F32 = mybir.dt.float32
BF16 = mybir.dt.bfloat16
I32 = mybir.dt.int32
ALU = mybir.AluOpType
ACT = mybir.ActivationFunctionType
AX = mybir.AxisListType
ds = bass.ds

P = 128
B, S, D = 2, 2048, 256
T = B * S
NT = T // P
KD = D // P
H, HS = 16, 16
SCALE = float(HS) ** -0.5
E, DF = 8, 4 * D
KF = DF // P
NROT = 3
EPS = 1e-5
CH = 512
TPC = CH // P
NC = T // CH
CPB = S // CH
QT = S // P
HG = 4
NG = B * H // HG
GPB = NG // B
GR = HG * HS
QPART = (0, 0, 1, 0, 2, 1)
KPART = (0, 1, 0, 2, 0, 1)
ROWS = len(QPART) * HS
FULL = ROWS + 3
MASKED = -1e30
TAYLOR = 10
INNER = 2 * D
KI = INNER // P
NS = 16
RANK = D // 16
TAPS = 4
NX = RANK + 2 * NS
TOPK = 2
NBLK = TOPK * NT + E
BIG = [P, TPC, D]
NQ = NS // 4


class Chain:

    def __init__(self, eng, sem):
        self.eng, self.sem, self.base, self.turn, self.n = eng, sem, 0, 0, 0

    def enter(self, turn):
        self.base, self.n, self.turn = self.base + self.n, 0, turn

    def leave(self, turns, per):
        assert self.n == per, (self.n, per)
        self.base, self.turn, self.n = self.base + turns * per, 0, 0

    def mark(self, ins):
        ins.then_inc(self.sem, 1)
        self.n += 1
        return self.base + self.turn + self.n

    def link(self, ins):
        self.eng.wait_ge(self.sem, self.mark(ins))

    def straight(self):
        self.base, self.n = self.base + self.n, 0

    def settle(self):
        self.eng.wait_ge(self.sem, self.base + self.turn + self.n)


def max_units():
    out = []
    for qc in range(CPB):
        units = [("max", h, t, k0, min(1024, P * (t + 1) - k0)) for h in range(HG)
                 for t in range(TPC * qc, TPC * (qc + 1)) for k0 in range(0, P * (t + 1), 1024)]
        if qc:
            units.insert(2, ("turn", qc - 1))
        out += units
    return out + [("turn", CPB - 1)]


EU = [(h, qc, kt, max(0, kt * P - qc * CH))
      for qc in range(CPB) for kt in range(TPC * (qc + 1)) for h in range(HG)]
MU = max_units()
NM, NE = len(MU), len(EU)
STEPS = NE // HG
SRING, PRING = 3, 8
LATE = 10
LAST_STEP = [max(n // HG for n in range(NE) if EU[n][1] == qc) for qc in range(CPB)]


def period_plan(with_exp, with_max):
    out, m, late = [], 0, []
    for n in range(NE if with_exp else 0):
        out.append(("score", n))
        if n % HG == HG - 1 and n > HG:
            step = n // HG - 1
            out.append(("pv", step))
            if step in LAST_STEP:
                late.append((n + 6, LAST_STEP.index(step)))
        while with_max and n >= LATE and m * (NE - LATE) < NM * (n + 1 - LATE):
            out.append(MU[m])
            m += 1
        if late and late[0][0] == n:
            out.append(("back", late.pop(0)[1]))
    if with_exp:
        out.append(("pv", STEPS - 1))
        out += [("back", qc) for _, qc in late] + [("back", CPB - 1)]
    elif with_max:
        out += MU
    return out


def ring_of(plan):
    return [u for u in plan if u[0] in ("max", "turn", "back")]


FULL_PLAN, FIRST_PLAN, LAST_PLAN = period_plan(True, True), period_plan(False, True), period_plan(True, False)
NR = len(ring_of(FULL_PLAN))


def build(nc, x, aw, ab, pw, pb, ln_g, ln_b, abel_w, abel_b, gate_w, gate_b, w1, b1, w2, b2, gens, gens_t,
          mix_w, mix_b, in_wt, conv_w, conv_b, xp_wt, dt_wt, dt_b, a_log, dd, out_wt, tern_wt, alpha, tern_b, out):
    with ExitStack() as ctx:
        ctx.enter_context(nc.allow_non_contiguous_dma(reason="vectors of a few hundred elements"))

        def sb(name, shape, dt=F32, at=ctx):
            return at.enter_context(nc.sbuf_tensor(name, shape, dt))

        def sem(name):
            return ctx.enter_context(nc.semaphore(name))

        def dram(name, shape, dt=F32):
            return nc.dram_tensor(name, shape, dt, kind="Internal").ap()

        def row(t):
            return t.rearrange("(a n) -> a n", a=1)

        def cols(t):
            return t.rearrange("(k p) -> p k", p=P)

        def rows(t):
            return t.rearrange("(t p) d -> p t d", p=P)

        def fat(t):
            return t.rearrange("(k p) n -> p k n", p=P)

        qk_d = dram("qk_parts", [3, 2, NG * GR, S], BF16)
        v_d = dram("v_rows", [T, D])
        xn_d = dram("xn_rows", [T, D])
        ab_d = dram("abel_rows", [T, D])
        at_d = dram("attn_rows", [T, D])
        max_d = dram("max_rows", [CPB, 3, HG * CH], BF16)
        x1_d = dram("x1_rows", [T, D])
        x2_d = dram("x2_rows", [T, D])
        xs_d = dram("expert_in", [NBLK * P, D])
        ys_d = dram("expert_out", [NBLK * P, D])
        x1T_d = dram("x1_columns", [NC, P, KD, CH])

        ps = ctx.enter_context(nc.psum_tensor("ps", [P, 8, 512], F32))
        idf = sb("idf", [P, P])
        ones_r = sb("ones_r", [1, P])
        inw = sb("inw", [P, KD, 2 * INNER])
        cw = sb("cw", [P, KI, TAPS])
        cb = sb("cb", [P, KI])
        xpw = sb("xpw", [P, KI, NX])
        dtw = sb("dtw", [2 * NS + RANK, INNER])
        dtb = sb("dtb", [P, KI])
        A = sb("A", [P, KI, NS])
        Dv = sb("Dv", [P, KI])
        outw = sb("outw", [P, KI, D])
        m0 = ExitStack()
        idb = sb("idb", [P, P], BF16, at=m0)
        mask_q = sb("mask_q", [P, P], BF16, at=m0)
        mask_k = sb("mask_k", [P, P], BF16, at=m0)
        ones_s = sb("ones_s", [P, P], at=m0)
        lng = sb("lng", [P, 2, KD], at=m0)
        slot = sb("slot", [P, NT, TOPK], I32, at=m0)
        wt = sb("wt", [P, TOPK, NT], at=m0)
        eid = sb("eid", [P, NBLK], at=m0)
        eidi = sb("eidi", [P, NBLK], I32, at=m0)
        wd = sb("wd", [P, NT, E], at=m0)
        rot = sb("rot", [P, KD, D], at=m0)
        tb = sb("tb", [1, D], at=m0)
        alph = sb("alph", [P, 1], at=m0)
        tw = sb("tw", [P, KD, D], at=m0)
        mixb = sb("mixb", [P, 1], at=m0)
        mixw = sb("mixw", [P, 2, D], at=m0)
        B2 = sb("B2", [E, D], at=m0)
        bpj = sb("bpj", [1, D], at=m0)
        wpj = sb("wpj", [P, KD, D], at=m0)

        m1 = ExitStack()
        X = sb("X", [P, NT, D], at=m1)
        XN = sb("XN", [P, NT, D], at=m1)
        st = sb("st", [P, NT, 6], at=m1)
        sm = sb("sm", [P, 12, NT], at=m1)
        ga = sb("ga", [P, NROT, KD, D], at=m1)
        gt = sb("gt", [P, NROT, KD, D], at=m1)
        gb = sb("gb", [P, NROT, KD, D], at=m1)
        er = sb("er", [P, NROT, KD, D], at=m1)
        et = sb("et", [P, NROT, KD, D], at=m1)
        kid = sb("kid", [P, TAYLOR, KD, D], BF16, at=m1)
        nrm = sb("nrm", [P, 8], at=m1)
        nri = sb("nri", [P, 8], I32, at=m1)
        wqkv = sb("wqkv", [P, KD, 3 * D], at=m1)
        bqk = sb("bqk", [P, 4], at=m1)
        bv = sb("bv", [1, D], at=m1)
        wab = sb("wab", [P, KD, D], at=m1)
        bab = sb("bab", [1, D], at=m1)
        wg = sb("wg", [P, KD, E], at=m1)
        bg = sb("bg", [1, E], at=m1)
        XNc = sb("XNc", [P, TPC, D], at=m1)
        x2h = sb("x2h", [P, TPC, D], at=m1)
        xTc = sb("xTc", [P, KD, CH], at=m1)
        x2c = sb("x2c", [P, KD, CH], at=m1)
        qf = sb("qf", [P, 2, CH], at=m1)
        qr = sb("qr", [P, CH], at=m1)
        q3 = sb("q3", [P, 4, 3, CH], BF16, at=m1)
        Vc = sb("Vc", [P, TPC, D], at=m1)
        ABc = sb("ABc", [P, TPC, D], at=m1)
        lgt = sb("lgt", [P, NT, E], at=m1)
        top = sb("top", [P, 6, NT, E], at=m1)
        tri = sb("tri", [P, P], at=m1)
        onet = sb("onet", [P, NT], at=m1)
        run = sb("run", [P, E, NT], at=m1)
        blk = sb("blk", [P, NBLK], at=m1)
        blki = sb("blki", [P, NBLK], I32, at=m1)
        ex = sb("ex", [P, 6, E], at=m1)
        exi = sb("exi", [P, 2, E], I32, at=m1)
        sl = sb("sl", [P, TOPK, NT], at=m1)
        zero = sb("zero", [P, 8 * D], at=m1)
        m1.close()

        mw = ExitStack()
        W1 = sb("W1", [P, E, KD, DF], at=mw)

        m2 = ExitStack()
        x2g = sb("x2g", [P, TPC, D], at=m2)
        sidx = sb("sidx", [P, TPC, TOPK], I32, at=m2)
        qs = sb("qs", [P, 2, HG, S], BF16, at=m2)
        ks = sb("ks", [P, 2, HG, S], BF16, at=m2)
        vg = sb("vg", [P, 2, QT, HG, 32], at=m2)
        vl = sb("vl", [P, QT, GR], at=m2)
        Pt = sb("Pt", [P, PRING, CH], at=m2)
        oT = sb("oT", [P, CH], at=m2)
        ao = sb("ao", [P, TPC, GR], at=m2)
        rec = sb("rec", [P, TPC, HG], at=m2)
        mp = sb("mp", [P, CPB, HG, TPC, 2], at=m2)
        mn = sb("mn", [P, CPB, HG * TPC], at=m2)
        n3 = sb("n3", [HG * TPC, CPB, 3, P], BF16, at=m2)
        nr = sb("nr", [HG * TPC, P], at=m2)
        m2.close()

        m4 = ExitStack()
        W2 = sb("W2", [P, E, KF, D], at=m4)
        bt = sb("bt", [P, DF], at=m4)
        b3 = sb("b3", [P, DF], BF16, at=m4)
        row_e = sb("row_e", [P, 1], at=m4)
        pick = sb("pick", [P, NBLK], at=m4)
        pickb = sb("pickb", [P, NBLK, P], BF16, at=m4)
        xg = sb("xg", [P, 2, D], at=m4)
        xgT = sb("xgT", [P, 2, KD, P], at=m4)
        hg = sb("hg", [P, 2, DF], at=m4)
        br = hg[:, 0, :]
        hT = sb("hT", [P, 2, KF, P], at=m4)
        yb = sb("yb", [P, 2, D], at=m4)
        m4.close()
        mw.close()

        m3 = ExitStack()
        yg = sb("yg", [P, 2, TPC, TOPK, D], at=m3)
        gidx = sb("gidx", [P, 2, TPC, TOPK], I32, at=m3)
        inx = sb("inx", [P, 2, 4, TPC, D], at=m3)
        atT = sb("atT", [P, KD, CH], at=m3)
        mot = sb("mot", [P, TPC, D], at=m3)
        moT = sb("moT", [P, KD, CH], at=m3)
        wdc = sb("wdc", [P, TPC, E], at=m3)
        wtc = sb("wtc", [P, TOPK, TPC], at=m3)
        wdT = sb("wdT", [E, CH], at=m3)
        cmb = sb("cmb", [P, 4, TPC, D], at=m3)
        x1c = sb("x1c", [P, TPC, D], at=m3)
        gate = sb("gate", [P, 4, TPC], at=m3)
        x1s = sb("x1s", [P, TPC, 6], at=m3)
        x1v = sb("x1v", [P, TPC, 2], at=m3)
        x1r = sb("x1r", [P, 3, TPC], at=m3)
        x1n = sb("x1n", [P, TPC, D], at=m3)
        x1T = sb("x1T", [P, KD, CH], at=m3)
        x1o = sb("x1o", [P, TPC, D], at=m3)
        tq = sb("tq", [P, KD, D], at=m3)
        tsum = sb("tsum", [P, 8], at=m3)
        m3.close()
        m0.close()

        sel = sb("sel", [6 * NS, 2 * NS, P], BF16)
        flag = sb("flag", [P, NC + 1])
        xin = sb("xin", [P, 2, KD, CH])
        xraw = sb("xraw", [P, KI, TAPS - 1 + CH])
        xs = sb("xs", [P, 2, KI, CH])
        zs = sb("zs", [P, 2, KI, CH])
        dt = sb("dt", [P, 2, KI, CH])
        dtx = sb("dtx", [P, 2, KI, CH])
        te = sb("te", [P, 2, CH])
        tl = sb("tl", [P, 2, CH])
        xps = sb("xps", [NX, CH])
        bcr = sb("bcr", [2 * NS, CH])
        bc2 = sb("bc2", [2 * NS, CH], BF16)
        bc3 = sb("bc3", [6 * NS, 2, CH], BF16)
        Bq = sb("Bq", [P, 2, 4, CH])
        Cq = sb("Cq", [P, 2, 4, CH])
        dA = sb("dA", [P, 2, 4, CH])
        hh = sb("hh", [P, 4, 4, CH])
        hst = sb("hst", [P, 4 * NQ, 4])
        xo = sb("xo", [P, TPC, D])

        s_phase = sem("s_phase")
        s_alone = sem("s_alone")
        c_dve, c_act, c_pool, s_const = sem("c_dve"), sem("c_act"), sem("c_pool"), sem("s_const")
        s_x, s_w, s_g = sem("s_x"), sem("s_w"), sem("s_g")
        s_nrm_abs, s_nrm_ps, s_sc, s_scaled = sem("s_nrm_abs"), sem("s_nrm_ps"), sem("s_sc"), sem("s_scaled")
        s_hor, s_hev, s_sqp, s_sqe, s_fin, s_fev = (sem(n) for n in ("s_hor", "s_hev", "s_sqp", "s_sqe", "s_fin", "s_fev"))
        s_var, s_std = sem("s_var"), sem("s_std")
        s_xnc, s_x2h = sem("s_xnc"), sem("s_x2h")
        s_tx, s_xT, s_t2, s_x2c = sem("s_tx"), sem("s_xT"), sem("s_t2"), sem("s_x2c")
        s_qp, s_qf, s_q3, s_qd = sem("s_qp"), sem("s_qf"), sem("s_q3"), sem("s_qd")
        s_vp, s_vc, s_vd = sem("s_vp"), sem("s_vc"), sem("s_vd")
        s_ap, s_ac, s_ad = sem("s_ap"), sem("s_ac"), sem("s_ad")
        s_lp, s_lc, s_nd = sem("s_lp"), sem("s_lc"), sem("s_nd")
        s_top, s_tex = sem("s_top"), sem("s_tex")
        s_stack = sem("s_stack")
        s_qk = [[sem(f"s_qk{i}{j}") for j in range(2)] for i in range(2)]
        s_vl, s_vg = sem("s_vl"), sem("s_vg")
        s_full, s_free = sem("s_full"), sem("s_free")
        s_score, s_exp, s_pv = sem("s_score"), sem("s_exp"), sem("s_pv")
        s_md = sem("s_md")
        s_oT, s_aod = sem("s_oT"), sem("s_aod")
        s_mn, s_mr, s_mrow = sem("s_mn"), sem("s_mr"), [sem(f"s_mrow{i}") for i in range(CPB)]
        s_ew, s_ew2, s_b = sem("s_ew"), sem("s_ew2"), sem("s_b")
        s_zero, s_zd, s_x2d, s_cnt, s_pos, s_x2g, s_sct, s_sent = (sem(n) for n in ("s_zero", "s_zd", "s_x2d", "s_cnt", "s_pos", "s_x2g", "s_sct", "s_sent"))
        s_bz, s_pick = sem("s_bz"), sem("s_pick")
        s_xg, s_ys = [sem(f"s_xg{i}") for i in range(2)], [sem(f"s_ys{i}") for i in range(2)]
        s_tp, s_xgT, s_hid, s_gelu, s_turn, s_hT, s_dn, s_yb = (sem(n) for n in ("s_tp", "s_xgT", "s_hid", "s_gelu", "s_turn", "s_hT", "s_dn", "s_yb"))
        s_tw, s_tout, s_res = sem("s_tw"), sem("s_tout"), sem("s_res")
        s_yg = [sem(f"s_yg{i}") for i in range(2)]
        s_cw, s_ci = sem("s_cw"), [sem(f"s_ci{i}") for i in range(2)]
        s_cwd, s_ctp, s_cT, s_cpr, s_cmo, s_cmp, s_cmT, s_cnb = (sem(f"s_c_{n}") for n in ("wd", "tp", "T", "pr", "mo", "mp", "mT", "nb"))
        s_cz, s_cg, s_cb, s_cx, s_co = (sem(f"s_c_{n}") for n in ("z", "g", "b", "x", "o"))

        s_x1s, s_x1q, s_x1n, s_x1t, s_x1T, s_x1d = (sem(n) for n in ("s_x1s", "s_x1q", "s_x1n", "s_x1t", "s_x1T", "s_x1d"))
        s_lw, s_xin, s_xo, s_od = sem("s_lw"), [sem(f"s_xin{i}") for i in range(2)], sem("s_xo"), sem("s_od")
        s_setup, s_abs, s_tps, s_tern = (sem(n) for n in ("s_setup", "s_abs", "s_tps", "s_tern"))
        s_wfull, s_wfree = sem("s_wfull"), sem("s_wfree")
        s_conv, s_tail, s_xs, s_bc3 = (sem(n) for n in ("s_conv", "s_tail", "s_xs", "s_bc3"))
        s_sp, s_ln, s_poly, s_dt, s_bu = (sem(n) for n in ("s_sp", "s_ln", "s_poly", "s_dt", "s_bu"))
        s_cfull, s_cfree = sem("s_cfull"), sem("s_cfree")
        s_dA, s_h, s_hc, s_acc, s_y, s_yz, s_add = (sem(n) for n in ("s_dA", "s_h", "s_hc", "s_acc", "s_y", "s_yz", "s_add"))

        block = ctx.enter_context(nc.Block())

        def stage_end(eng, k):
            eng.drain().then_inc(s_phase, 1)
            eng.wait_ge(s_phase, 5 * k)

        def alone(eng):
            eng.sem_inc(s_alone, 1)

        x_t = x.rearrange("b (t p) d -> p (b t) d", p=P)
        out_t = out.rearrange("b (t p) d -> p (b t) d", p=P)

        @block.sync
        def _(sp):
            n = NT // 4
            for c in range(4):
                sp.dma_start(X[:, c * n:(c + 1) * n, :], x_t[:, c * n:(c + 1) * n, :]).then_inc(s_x, 16)
            sp.dma_start(ga[:, :, :, :], gens.rearrange("g (k p) n -> p g k n", p=P)).then_inc(s_g, 16)
            sp.dma_start(gt[:, :, :, :], gens_t.rearrange("g (k p) n -> p g k n", p=P)).then_inc(s_g, 16)
            sp.sem_inc(s_nd, 16)
            sp.sem_inc(s_x2d, 16)
            sp.sem_inc(s_sent, 1)
            sp.sem_inc(s_qd, 64)
            sp.sem_inc(s_vd, 16)
            sp.sem_inc(s_ad, 16)
            sp.sem_inc(s_aod, 16)
            sp.dma_start(wqkv[:, :, :], fat(aw)).then_inc(s_w, 16)
            sp.dma_start(bqk[:, :], cols(ab[0:2 * D])).then_inc(s_w, 16)
            sp.dma_start(bv[:, :], row(ab[2 * D:3 * D])).then_inc(s_w, 16)
            sp.dma_start(wab[:, :, :], fat(abel_w)).then_inc(s_w, 16)
            sp.dma_start(bab[:, :], row(abel_b)).then_inc(s_w, 16)
            sp.dma_start(wg[:, :, :], fat(gate_w)).then_inc(s_w, 16)
            sp.dma_start(bg[:, :], row(gate_b)).then_inc(s_w, 16)
            sp.dma_start(lng[:, 0, :], cols(ln_g)).then_inc(s_w, 16)
            sp.dma_start(lng[:, 1, :], cols(ln_b)).then_inc(s_w, 16)
            sp.wait_ge(s_zero, 1)
            for c in range(NBLK // 8):
                sp.dma_start(rows(xs_d)[:, c * 8:(c + 1) * 8, :], zero[:, :].rearrange("p (t n) -> p t n", n=D)).then_inc(s_zd, 16)
            stage_end(sp, 1)

            with sp.Fori(0, NC) as n:
                b, c = n // CPB, n % CPB
                sp.wait_ge(s_xnc, n + 1)
                sp.dma_start(rows(xn_d)[:, ds(n * TPC, TPC), :], XNc[:, :, :]).then_inc(s_nd, 16)
                sp.wait_ge(s_x2h, n * TPC + TPC)
                sp.dma_start(rows(x2_d)[:, ds(n * TPC, TPC), :], x2h[:, :, :]).then_inc(s_x2d, 16)
                for m in range(4):
                    sp.wait_ge(s_q3, n * 4 + (m + 1 + 1))
                    dst = qk_d[:, m // 2, :, :].rearrange("a r t -> r a t")[
                        ds(b * (2 * P) + (m % 2) * P, P), :, ds(c * CH, CH)]
                    sp.dma_start(dst, q3[:, m, :, :]).then_inc(s_qd, 16)
                sp.wait_ge(s_vc, n + 2)
                sp.dma_start(rows(v_d)[:, ds(n * TPC, TPC), :], Vc[:, :, :]).then_inc(s_vd, 16)
                sp.wait_ge(s_ac, n + 2)
                sp.dma_start(rows(ab_d)[:, ds(n * TPC, TPC), :], ABc[:, :, :]).then_inc(s_ad, 16)
            sp.wait_ge(s_nd, 16 * (NC + 1))
            sp.wait_ge(s_qd, 64 * (NC + 1))
            sp.wait_ge(s_vd, 16 * (NC + 1))
            sp.wait_ge(s_ad, 16 * (NC + 1))
            sp.wait_ge(s_x2d, 16 * (NC + 1))
            sp.wait_ge(s_zd, 16 * (NBLK // 8))
            stage_end(sp, 2)

            def load_stack(g, par, w, part):
                half = slice(part * (S // 2), (part + 1) * (S // 2))
                for c in range(len(QPART)):
                    src = qk_d[(QPART, KPART)[w][c], w, ds(g * GR, GR), half].rearrange("(h d) t -> d h t", h=HG)
                    sp.dma_start((qs, ks)[w][c * HS:(c + 1) * HS, par, :, half], src).then_inc(s_qk[par][part], 16)

            def load_group(g, par):
                load_stack(g, par, 0, 0)
                load_rest(g, par)

            def load_rest(g, par):
                load_stack(g, par, 1, 0)
                load_stack(g, par, 0, 1)
                load_stack(g, par, 1, 1)

            def batch_rows(t, g):
                return t.rearrange("(b t p) n -> b p t n", p=P, b=B)[g // GPB, :, :, ds((g % GPB) * GR, GR)]

            def load_v(g):
                sp.dma_start(vl[:, :, :], batch_rows(v_d, g)).then_inc(s_vl, 16)

            def store_max(g, par, qc):
                sp.wait_ge(s_mr, g * CPB + (qc + 1))
                sp.dma_start(max_d[qc].rearrange("a (r q) -> r a q", q=P), n3[:, qc, :, :]).then_inc(s_md, 16)
                sp.wait_ge(s_md, (g * CPB + (qc + 1)) * 16)
                sp.dma_start(qs[ROWS:FULL, par, :, qc * CH:(qc + 1) * CH],
                             max_d[qc].rearrange("a (h n) -> a h n", h=HG)).then_inc(s_mrow[qc], 16)

            def load_rows(c):
                sp.wait_ge(s_sent, c + 1)
                sp.dma_start(x2g[:, :, :], rows(x2_d)[:, ds(c * TPC, TPC), :]).then_inc(s_x2g, 16)

            def period(g, par, plan, base, more, stack):
                load_rows(g)
                if more:
                    sp.wait_ge(s_vg, g + 1)
                    load_v(g + 1)
                for r, u in enumerate(ring_of(plan)):
                    if u[0] == "turn":
                        store_max(g + 1, 1 - par, u[1])
                    if u[0] == "back":
                        sp.wait_ge(s_free, base + (r + 1))
                        sp.dma_start(batch_rows(at_d, g)[:, u[1] * TPC:(u[1] + 1) * TPC, :],
                                     ao[:, :, :]).then_inc(s_aod, 16)
                        if u[1] == CPB // 2 - 1 and stack:
                            load_stack(g + 2, par, 0, 0)
                if stack:
                    sp.wait_ge(s_pv, (g + 1) * STEPS + 2)
                    load_rest(g + 2, par)

            load_v(0)
            load_group(0, 0)
            load_group(1, 1)
            sp.dma_start(tw[:, :, :], fat(tern_wt)).then_inc(s_tw, 16)
            sp.dma_start(alph[:, :], row(alpha).broadcast_to([P, 1])).then_inc(s_tw, 16)
            sp.dma_start(tb[:, :], row(tern_b)).then_inc(s_tw, 16)
            sp.dma_start(wpj[:, :, :], fat(pw)).then_inc(s_cw, 16)
            sp.dma_start(bpj[:, :], row(pb)).then_inc(s_cw, 16)
            sp.dma_start(B2[:, :], b2).then_inc(s_cw, 16)
            sp.dma_start(mixw[:, :, :], mix_w.rearrange("(a k n) c -> a k (n c)", a=1, k=2).broadcast_to([P, 2, D])).then_inc(s_cw, 16)
            sp.dma_start(mixb[:, :], row(mix_b).broadcast_to([P, 1])).then_inc(s_cw, 16)
            for dst, src in ((inw[:, :, :], fat(in_wt)), (cw[:, :, :], conv_w.rearrange("(k p) a t -> p k (a t)", p=P)),
                             (cb[:, :], cols(conv_b)), (xpw[:, :, :], fat(xp_wt)), (dtw[2 * NS:, :], dt_wt),
                             (dtb[:, :], cols(dt_b)), (A[:, :, :], a_log.rearrange("(k p) n -> p k n", p=P)),
                             (Dv[:, :], cols(dd)), (outw[:, :, :], fat(out_wt))):
                sp.dma_start(dst, src).then_inc(s_lw, 16)
            for e in range(E):
                sp.dma_start(W1[:, e, :, :], w1[e, :, :].rearrange("(k p) f -> p k f", p=P)).then_inc(s_ew, 16)
            for qc in range(CPB):
                store_max(0, 0, qc)
            with sp.Fori(0, NG // 2 - 1) as i:
                for par in range(2):
                    g = i * 2 + par
                    period(g, par, FULL_PLAN, g * NR + NM, True, True)
            period(NG - 2, 0, FULL_PLAN, NM + (NG - 2) * NR, True, False)
            period(NG - 1, 1, LAST_PLAN, NM + (NG - 1) * NR, False, False)
            sp.wait_ge(s_aod, 16 * (NG * CPB + 1))
            stage_end(sp, 3)

            sp.wait_ge(s_bz, 1)
            for a in range(3):
                sp.dma_start(bt[32 * a:32 * a + E, :], b1).then_inc(s_b, 16)

            def load_block(i, par):
                sp.dma_start(xg[:, par, :], xs_d[ds(i * P, P), :]).then_inc(s_xg[par], 16)

            def store_block(i, par):
                sp.wait_ge(s_yb, i + 2)
                sp.dma_start(ys_d[ds(i * P, P), :], yb[:, par, :]).then_inc(s_ys[par], 16)

            sp.sem_inc(s_ys[0], 16)
            sp.sem_inc(s_ys[1], 16)
            load_block(0, 0)
            load_block(1, 1)
            for e in range(E):
                sp.dma_start(W2[:, e, :, :], w2[e, :, :].rearrange("(k p) f -> p k f", p=P)).then_inc(s_ew2, 16)
            with sp.Fori(0, NBLK // 2 - 1) as i:
                for par in range(2):
                    sp.wait_ge(s_tp, i * 2 + (par + 1))
                    load_block(i * 2 + (par + 2), par)
                    store_block(i * 2 + par, par)
            store_block(NBLK - 2, 0)
            store_block(NBLK - 1, 1)
            for par in range(2):
                sp.wait_ge(s_ys[par], 16 * (NBLK // 2 + 1))
            stage_end(sp, 4)

            def load_chunk(c, par):
                for k, src in enumerate((x_t, rows(xn_d), rows(ab_d), rows(at_d))):
                    sp.dma_start(inx[:, par, k, :, :], src[:, ds(c * TPC, TPC), :]).then_inc(s_ci[par], 16)

            def store_columns(c):
                sp.wait_ge(s_x1T, c + 1)
                sp.dma_start(x1T_d[c, :, :, :], x1T[:, :, :]).then_inc(s_x1d, 16)

            def store_rows(c):
                sp.wait_ge(s_res, c + 3)
                sp.dma_start(rows(x1_d)[:, ds(c * TPC, TPC), :], x1o[:, :, :]).then_inc(s_co, 16)

            load_chunk(0, 0)
            load_chunk(1, 1)
            sp.sem_inc(s_co, 16)
            sp.sem_inc(s_x1d, 16)
            sp.wait_ge(s_cx, 2)
            load_chunk(2, 0)
            store_columns(0)
            with sp.Fori(0, NC // 2 - 2) as i:
                for par in (1, 0):
                    c = i * 2 + (2 - par)
                    sp.wait_ge(s_cx, c + 2)
                    load_chunk(c + 2, par)
                    store_columns(c)
                    store_rows(c - 1)
            for c in range(NC - 3, NC):
                if c + 2 < NC:
                    sp.wait_ge(s_cx, c + 2)
                    load_chunk(c + 2, c % 2)
                store_columns(c)
                store_rows(c - 1)
            store_rows(NC - 1)
            sp.wait_ge(s_co, 16 * (NC + 1))
            sp.wait_ge(s_x1d, 16 * (NC + 1))
            stage_end(sp, 5)

            def load_columns(n, par):
                sp.dma_start(xin[:, par, :, :], x1T_d[n, :, :, :]).then_inc(s_xin[par], 16)

            def finish(n):
                sp.dma_start(xo[:, :, :], rows(x1_d)[:, ds(n * TPC, TPC), :]).then_inc(s_xo, 16)
                sp.wait_ge(s_add, n + 1)
                sp.dma_start(out_t[:, ds(n * TPC, TPC), :], xo[:, :, :]).then_inc(s_od, 16)
                sp.wait_ge(s_od, n * 16 + 16)
                alone(sp)

            load_columns(0, 0)
            load_columns(1, 1)
            sp.wait_ge(s_wfree, 5)
            load_columns(2, 0)
            finish(0)
            with sp.Fori(0, (NC - 4) // 2) as i:
                for k in (1, 2):
                    n = i * 2 + k
                    sp.wait_ge(s_wfree, n * 8 + 5)
                    load_columns(n + 2, k % 2)
                    finish(n)
            sp.wait_ge(s_wfree, (NC - 3) * 8 + 5)
            load_columns(NC - 1, 1)
            for n in range(NC - 3, NC):
                finish(n)
            stage_end(sp, 6)

        @block.gpsimd
        def _(pool):
            po = Chain(pool, c_pool)
            pool.memset(zero[:, :], 0.0).then_inc(s_zero, 1)
            po.mark(pool.memset(idf[:, :], 0.0))
            po.mark(pool.memset(idb[:, :], 0.0))
            po.mark(pool.memset(mask_q[:, :], 0.0))
            po.mark(pool.memset(mask_k[:, :], 0.0))
            po.mark(pool.memset(kid[:, :, :, :], 0.0))
            pool.memset(ones_r[:, :], 1.0).then_inc(s_const, 1)
            pool.memset(ones_s[:, :], 1.0).then_inc(s_const, 1)
            po.settle()
            for m in (idf, idb):
                pool.affine_select(out=m[:, :], in_=m[:, :], compare_op=ALU.not_equal, fill=1.0, base=0,
                                   pattern=[[-1, P]], channel_multiplier=1).then_inc(s_const, 1)
            pool.affine_select(out=mask_q[:, :], in_=mask_q[:, :], compare_op=ALU.is_ge, fill=MASKED, base=0,
                               pattern=[[-1, P]], channel_multiplier=1).then_inc(s_const, 1)
            pool.affine_select(out=mask_k[:, :], in_=mask_k[:, :], compare_op=ALU.is_ge, fill=MASKED, base=0,
                               pattern=[[1, P]], channel_multiplier=-1).then_inc(s_const, 1)
            for k in range(TAYLOR):
                pool.affine_select(out=kid[:, k, :, :], in_=kid[:, k, :, :], compare_op=ALU.not_equal,
                                   fill=float(k + 1), base=0, pattern=[[P, KD], [-1, D]],
                                   channel_multiplier=1).then_inc(s_const, 1)
            stage_end(pool, 1)

            po.mark(pool.memset(onet[:, :], 1.0))
            po.link(pool.memset(tri[:, :], 1.0))
            po.mark(pool.affine_select(out=tri[:, :], in_=tri[:, :], compare_op=ALU.is_gt, fill=0.0, base=0,
                                       pattern=[[1, P]], channel_multiplier=-1))
            po.link(pool.iota(blki[:, :], pattern=[[1, NBLK]], base=0, channel_multiplier=0))
            pool.sem_inc(s_pos, 1)
            stage_end(pool, 2)

            pool.memset(ks[ROWS:FULL, :, :, :], 1.0).then_inc(s_stack, 1)
            pool.wait_ge(s_stack, 1)
            po.link(pool.memset(vg[:, :, :, :, HS:32], 0.0))
            po.link(pool.memset(vg[:, :, :, :, HS:HS + 1], 1.0))

            def spread(g, par):
                pool.wait_ge(s_vl, (g + 1) * 16)
                alone(pool)
                pool.tensor_copy(vg[:, par, :, :, 0:HS], vl[:, :, :].rearrange("p t (h d) -> p t h d", h=HG)).then_inc(s_vg, 1)

            def scatter(c):
                pool.wait_ge(s_x2g, c * 16 + 16)
                alone(pool)
                po.link(pool.tensor_copy(sidx[:, :, :], slot[:, ds(c * TPC, TPC), :]))
                alone(pool)
                for t in range(TPC):
                    for k in range(TOPK):
                        pool.indirect_dma_start(xs_d[:, :], bass.IndirectOffsetOnAxis(ap=sidx[:, t, k:k + 1], axis=0),
                                                x2g[:, t, :], None).then_inc(s_sct, 16)
                pool.wait_ge(s_sct, (c + 1) * (16 * TPC * TOPK))
                pool.sem_inc(s_sent, 1)

            spread(0, 0)
            with pool.Fori(0, NG // 2 - 1) as i:
                po.enter(i * 2)
                for par in range(2):
                    g = i * 2 + par
                    pool.wait_ge(s_pv, g * STEPS + 2)
                    spread(g + 1, 1 - par)
                    scatter(g)
                po.leave(NG // 2 - 1, 2)
            pool.wait_ge(s_pv, (NG - 2) * STEPS + 2)
            spread(NG - 1, 1)
            scatter(NG - 2)
            scatter(NG - 1)
            stage_end(pool, 3)

            pool.memset(bt[:, :], 0.0).then_inc(s_bz, 1)
            po.link(pool.memset(row_e[:, :], -1.0))
            for e in range(E):
                for a in range(3):
                    po.link(pool.affine_select(out=row_e[:, :], in_=row_e[:, :], compare_op=ALU.not_equal, fill=float(e),
                                               base=-32 * a - e, pattern=[[0, 1]], channel_multiplier=1))
            pool.sem_inc(s_bz, 1)
            stage_end(pool, 4)

            def gather(c, par):
                alone(pool)
                po.link(pool.tensor_copy(gidx[:, par, :, :], slot[:, ds(c * TPC, TPC), :]))
                alone(pool)
                for t in range(TPC):
                    for k in range(TOPK):
                        pool.indirect_dma_start(yg[:, par, t, k, :], None, ys_d[:, :],
                                                bass.IndirectOffsetOnAxis(ap=gidx[:, par, t, k:k + 1], axis=0)).then_inc(s_yg[par], 16)

            def base_sum(c, par):
                pool.wait_ge(s_ci[par], c // 2 * 64 + 64)
                pool.wait_ge(s_cx, c + 1)
                po.link(pool.tensor_tensor(cmb[:, 0, :, :], inx[:, par, 0, :, :], inx[:, par, 1, :, :], ALU.add))
                pool.tensor_tensor(cmb[:, 1, :, :], cmb[:, 0, :, :], inx[:, par, 2, :, :], ALU.add).then_inc(s_cb, 1)

            gather(0, 0)
            gather(1, 1)
            with pool.Fori(0, NC // 2 - 1) as i:
                po.enter(i * 4)
                for par in range(2):
                    base_sum(i * 2 + par, par)
                    pool.wait_ge(s_cx, i * 2 + (par + 2))
                    gather(i * 2 + (par + 2), par)
                po.leave(NC // 2 - 1, 4)
            base_sum(NC - 2, 0)
            base_sum(NC - 1, 1)
            po.straight()
            stage_end(pool, 5)

            po.mark(pool.memset(flag[:, :], 1.0))
            po.mark(pool.memset(hst[:, :, :], 0.0))
            po.mark(pool.memset(xraw[:, :, 0:TAPS - 1], 0.0))
            po.settle()
            for b in range(B + 1):
                po.link(pool.memset(flag[:, b * CPB:b * CPB + 1], 0.0))
            pool.sem_inc(s_setup, 1)
            po.link(pool.memset(sel[:, :, :], 0.0))
            for a in range(3):
                po.link(pool.affine_select(out=sel[:, :, :], in_=sel[:, :, :], compare_op=ALU.not_equal, fill=1.0,
                                           base=-2 * NS * a, pattern=[[-1, 2 * NS], [0, P]], channel_multiplier=1))
            pool.sem_inc(s_setup, 1)
            pool.sem_inc(s_yz, 2)

            def series(m, k, par):
                pool.wait_ge(s_ln, m * 2 + (k + 1))
                p = dtx[:, par, 2 * k:2 * k + 2, :]
                alone(pool)
                po.link(pool.tensor_scalar(p, te[:, :, :], 1.0 / 3, -0.5, ALU.mult, ALU.add))
                po.link(pool.tensor_tensor(p, p, te[:, :, :], ALU.mult))
                alone(pool)
                po.link(pool.tensor_scalar(p, p, 1.0, None, ALU.add))
                pool.tensor_tensor(p, p, te[:, :, :], ALU.mult).then_inc(s_poly, 1)

            def gate_z(n, par):
                pool.wait_ge(s_y, n * KI + 2 * KI)
                pool.tensor_tensor(xs[:, par, :, :], xs[:, par, :, :], zs[:, par, :, :], ALU.mult).then_inc(s_yz, 1)

            def pool_body(n, par, first, last):
                for u in range(4 * NQ):
                    pool.wait_ge(s_h, n * 16 + (u + 1 + 2))
                    if u % 4 == 0:
                        pool.wait_ge(s_cfree, n * 32 + (u // 4 * 8 + 8 + 2))
                    h = hh[:, u % 4, :, :]
                    pool.tensor_tensor(h, h, Cq[:, u // 4 % 2, :, :], ALU.mult).then_inc(s_hc, 1)
                    if u == 1 and not first:
                        gate_z(n - 1, 1 - par)
                    if u in (10, 13) and not last:
                        series(n + 1, u // 13, 1 - par)

            pool.sem_inc(s_hc, 8)
            for k in range(2):
                series(0, k, 0)
            po.straight()
            pool_body(0, 0, True, False)
            pool_body(1, 1, False, False)
            with pool.Fori(1, NC // 2 - 1) as i:
                po.enter((i - 1) * 12)
                pool_body(i * 2, 0, False, False)
                pool_body(i * 2 + 1, 1, False, False)
                po.leave(NC // 2 - 2, 12)
            pool_body(NC - 2, 0, False, False)
            pool_body(NC - 1, 1, False, True)
            gate_z(NC - 1, 1)
            stage_end(pool, 6)

        @block.scalar
        def _(act):
            ac = Chain(act, c_act)
            def deviation(k):
                act.wait_ge(s_var, k + 1)
                act.activation(sm[:, 6 * k + 3, :], sm[:, 6 * k + 2, :], ACT.Sqrt).then_inc(s_std, 1)

            act.wait_ge(s_g, 32)
            act.activation(gb[:, :, :, :], ga[:, :, :, :], ACT.Abs).then_inc(s_nrm_abs, 1)
            act.wait_ge(s_sc, 1)
            act.wait_ge(s_nrm_ps, 1)
            act.activation(gb[:, :, :, :], gt[:, :, :, :], ACT.Copy, scale=nrm[:, 1:2]).then_inc(s_scaled, 1)
            act.activation(er[:, :, :, :], ga[:, :, :, :], ACT.Copy, scale=nrm[:, 1:2]).then_inc(s_scaled, 1)
            for k in range(TAYLOR, 0, -1):
                for g in range(NROT):
                    act.wait_ge(s_hor, (TAYLOR - k) * NROT + g + 1)
                    act.activation(er[:, g, :, :], ps[:, g, :].rearrange("p (k n) -> p k n", k=KD), ACT.Copy,
                                   scale=1.0 / k).then_inc(s_hev, 1)
                if k == TAYLOR // 2:
                    deviation(0)
            for g in range(NROT):
                act.wait_ge(s_hor, TAYLOR * NROT + g + 1)
                act.activation(et[:, g, :, :], ps[:, 3 + g, :].rearrange("p (k n) -> p k n", k=KD), ACT.Copy).then_inc(s_hev, 1)
            squarings = act.value_load(nri[0:1, 2:3], min_val=1, max_val=200)
            with act.Fori(0, squarings) as i:
                for g in range(NROT):
                    act.wait_ge(s_sqp, i * NROT + (g + 1))
                    act.activation(er[:, g, :, :], ps[:, g, :].rearrange("p (k n) -> p k n", k=KD), ACT.Copy).then_inc(s_sqe, 1)
                    act.activation(et[:, g, :, :], ps[:, 3 + g, :].rearrange("p (k n) -> p k n", k=KD), ACT.Copy).then_inc(s_sqe, 1)
            deviation(1)
            act.wait_ge(s_fin, 1)
            act.activation(gb[:, 0, :, :], ps[:, 6, :].rearrange("p (k n) -> p k n", k=KD), ACT.Copy).then_inc(s_fev, 1)
            act.wait_ge(s_fin, 2)
            act.activation(rot[:, :, :], ps[:, 7, :].rearrange("p (k n) -> p k n", k=KD), ACT.Copy).then_inc(s_fev, 1)
            stage_end(act, 1)

            act.wait_ge(s_w, 9 * 16)
            act.sem_inc(s_ac, 1)
            act.sem_inc(s_qf, 2)
            with act.Fori(0, NC) as n:
                act.wait_ge(s_tx, n + 1)
                act.wait_ge(s_nd, n * 16 + 16)
                alone(act)
                act.activation(XNc[:, :, :], XN[:, ds(n * TPC, TPC), :], ACT.Copy).then_inc(s_xnc, 1)
                act.wait_ge(s_tx, n + 2)
                act.wait_ge(s_vp, n + 1)
                act.activation(xTc[:, :, :], ps[:, 0:2, :], ACT.Copy).then_inc(s_xT, 1)
                for m in range(4):
                    act.wait_ge(s_qp, n * 4 + (m + 1))
                    act.wait_ge(s_q3, n * 4 + (m if m > 1 else 1))
                    act.activation(qf[:, m % 2, :], ps[:, 4 + m % 2, :], ACT.Identity, bias=bqk[:, m:m + 1]).then_inc(s_qf, 1)
                act.wait_ge(s_ap, n + 1)
                act.wait_ge(s_ad, n * 16 + 16)
                act.activation(ABc[:, :, :], ps[:, 0:2, :].rearrange("p k (t n) -> p (k t) n", n=D), ACT.Gelu).then_inc(s_ac, 1)
            act.wait_ge(s_top, 1)
            act.activation(sm[:, 2, :], sm[:, 1, :], ACT.Exp).then_inc(s_tex, 1)
            stage_end(act, 2)

            act.sem_inc(s_exp, NE)
            act.sem_inc(s_oT, 1)

            def evict(g, qc, base, plan):
                act.wait_ge(s_pv, g * STEPS + (LAST_STEP[qc] + 1 + 2))
                before = [r for r, u in enumerate(ring_of(plan)) if u == ("back", qc - 1)]
                act.wait_ge(s_full, base + (before[0] + 1 if before else 0))
                act.activation(oT[:, :], ps[:, 7, :], ACT.Copy).then_inc(s_oT, 1)

            def exps(g, base, plan):
                for n, (h, qc, kt, q0) in enumerate(EU):
                    if n % HG == 0:
                        act.wait_ge(s_pv, g * STEPS + (n // HG + 1))
                    act.wait_ge(s_score, g * NE + (n + 1))
                    act.activation(Pt[:, n % PRING, q0:CH], ps[:, 4 + n % SRING, q0:CH], ACT.Exp, scale=SCALE).then_inc(s_exp, 1)
                    if n % HG == HG - 1 and n // HG - 1 in LAST_STEP:
                        evict(g, EU[n - HG][1], base, plan)
                evict(g, CPB - 1, base, plan)

            with act.Fori(0, NG - 1) as g:
                exps(g, g * NR + NM, FULL_PLAN)
            exps(NG - 1, NM + (NG - 1) * NR, LAST_PLAN)
            stage_end(act, 3)

            act.sem_inc(s_xgT, 1)
            act.sem_inc(s_gelu, 2)

            def columns(i, par):
                act.wait_ge(s_tp, i + 1)
                act.wait_ge(s_hid, i + 1)
                for k in range(KD):
                    ins = act.activation(xgT[:, par, k, :], ps[:, 6, k * P:(k + 1) * P], ACT.Identity,
                                         bias=lng[:, 1, k:k + 1], scale=lng[:, 0, k:k + 1])
                ins.then_inc(s_xgT, 1)

            def gelu(i, par):
                act.wait_ge(s_hid, i + 3)
                act.wait_ge(s_turn, i + 1)
                act.activation(hg[:, par, :], ps[:, 2 * par:2 * par + 2, :].rearrange("p a n -> p (a n)"), ACT.Gelu).then_inc(s_gelu, 1)

            columns(0, 0)
            gelu(0, 0)
            columns(1, 1)
            with act.Fori(0, NBLK // 2 - 1) as i:
                for par in (1, 0):
                    j = i * 2 + (2 - par)
                    gelu(j, par)
                    columns(j + 1, 1 - par)
            gelu(NBLK - 1, 1)
            stage_end(act, 4)

            act.wait_ge(s_tw, 3 * 16)
            for k in range(KD):
                act.activation(tq[:, k, :], tw[:, k, :], ACT.Abs, accum_out=tsum[:, k:k + 1]).then_inc(s_abs, 1)
            act.wait_ge(s_cw, 5 * 16)
            def front_columns(c):
                act.wait_ge(s_ctp, c + 1)
                act.activation(atT[:, :, :], ps[:, 0:2, :], ACT.Copy).then_inc(s_cT, 1)
                act.activation(wdT[:, :], ps[0:E, 2, :], ACT.Copy).then_inc(s_cT, 1)

            def moe_columns(c):
                act.wait_ge(s_cmp, c + 1)
                act.activation(moT[:, :, :], ps[:, 0:2, :], ACT.Copy).then_inc(s_cmT, 1)

            def combine(c, more):
                act.wait_ge(s_cz, c + 1)
                act.activation(gate[:, 3, :], gate[:, 2, :], ACT.Sigmoid, bias=mixb[:, 0:1]).then_inc(s_cg, 1)
                if more:
                    front_columns(c + 1)
                act.wait_ge(s_x1s, c + 1)
                act.activation(x1r[:, 1, :], x1r[:, 0, :], ACT.Sqrt).then_inc(s_x1q, 1)
                if more:
                    moe_columns(c + 1)
                act.wait_ge(s_x1t, c + 1)
                act.wait_ge(s_x1d, c * 16 + 16)
                act.activation(x1T[:, :, :], ps[:, 0:2, :], ACT.Copy).then_inc(s_x1T, 1)

            front_columns(0)
            moe_columns(0)
            with act.Fori(0, NC - 1) as c:
                combine(c, True)
            combine(NC - 1, False)
            stage_end(act, 5)

            act.wait_ge(s_lw, 9 * 16)
            ac.link(act.activation(A[:, :, :], A[:, :, :], ACT.Exp))
            ac.link(act.activation(A[:, :, :], A[:, :, :], ACT.Copy, scale=-1.0))
            act.sem_inc(s_wfree, 1)
            act.sem_inc(s_cfree, 2)

            def raw(m, k):
                act.wait_ge(s_wfull, m * 8 + (k + 1))
                act.wait_ge(s_tail, m + 1)
                act.activation(xraw[:, 2 * k:2 * k + 2, TAPS - 1:], ps[:, 4:6, :], ACT.Copy).then_inc(s_wfree, 1)

            def silu_z(m, k, par):
                act.wait_ge(s_wfull, m * 8 + (k + 3))
                act.wait_ge(s_yz, m + 1)
                act.activation(zs[:, par, 2 * k:2 * k + 2, :], ps[:, 4:6, :], ACT.Silu).then_inc(s_wfree, 1)

            def silu_x(m, par):
                for d in range(KI):
                    act.wait_ge(s_conv, m * KI + (d + 1))
                    act.activation(xs[:, par, d, :], xs[:, par, d, :], ACT.Silu, bias=cb[:, d:d + 1]).then_inc(s_xs, 1)

            def take_xp(m):
                act.wait_ge(s_wfull, m * 8 + 5)
                act.wait_ge(s_bc3, m + 1)
                act.activation(xps[:, :], ps[0:NX, 4, :], ACT.Copy).then_inc(s_wfree, 1)

            def softplus(m, k, par, old):
                act.wait_ge(s_wfull, m * 8 + (k + 6))
                act.wait_ge(s_sp, m * 2 + (k + 1))
                if old:
                    act.wait_ge(s_h, m * 16 - 14)
                for j in range(2):
                    d = 2 * k + j
                    ac.mark(act.activation(te[:, j, :], ps[:, 4 + j, :], ACT.Abs, bias=dtb[:, d:d + 1]))
                    act.activation(dt[:, par, d, :], ps[:, 4 + j, :], ACT.Relu, bias=dtb[:, d:d + 1]).then_inc(s_wfree, j) if j else \
                        ac.mark(act.activation(dt[:, par, d, :], ps[:, 4 + j, :], ACT.Relu, bias=dtb[:, d:d + 1]))
                ac.settle()
                ac.link(act.activation(te[:, :, :], te[:, :, :], ACT.Exp, scale=-1.0))
                act.activation(tl[:, :, :], te[:, :, :], ACT.Ln, bias=1.0).then_inc(s_ln, 1)

            def spread_bc(n, q):
                act.wait_ge(s_bu, n * 16 + (q * 4 + 4))
                act.wait_ge(s_hc, n * 16 + (q * 4 + 4))
                for k in range(8):
                    c = q * 8 + k
                    act.wait_ge(s_cfull, n * 32 + (c + 1))
                    dst = Bq if k < 4 else Cq
                    act.activation(dst[:, q % 2, k % 4, :], ps[:, 6 + k % 2, :], ACT.Copy).then_inc(s_cfree, 1)

            def act_body(n, par, last):
                for u in range(4 * NQ):
                    q, d = u // 4, u % 4
                    if u == 0:
                        act.wait_ge(s_dt, n * 2 + 2)
                    act.wait_ge(s_h, n * 16 + (u + 1))
                    for j in range(4):
                        ins = act.activation(dA[:, u % 2, j, :], dt[:, par, d, :], ACT.Exp, scale=A[:, d, 4 * q + j:4 * q + j + 1])
                    ins.then_inc(s_dA, 1)
                    if not last:
                        if u in (4, 5):
                            raw(n + 1, u - 4)
                        if u in (6, 7):
                            silu_z(n + 1, u - 6, 1 - par)
                        if u == 8:
                            silu_x(n + 1, 1 - par)
                        if u == 10:
                            take_xp(n + 1)
                        if u in (11, 14):
                            softplus(n + 1, u // 14, 1 - par, not (isinstance(n, int) and n == 0))
                    if u % 4 == 3 and (q < NQ - 1 or not last):
                        spread_bc(n + (q + 1) // NQ, (q + 1) % NQ)

            for k in range(2):
                raw(0, k)
            for k in range(2):
                silu_z(0, k, 0)
            silu_x(0, 0)
            take_xp(0)
            for k in range(2):
                softplus(0, k, 0, False)
            spread_bc(0, 0)
            act.drain().then_inc(s_wfree, 1)
            ac.straight()
            act_body(0, 0, False)
            act_body(1, 1, False)
            with act.Fori(1, NC // 2 - 1) as i:
                ac.enter((i - 1) * 16)
                act_body(i * 2, 0, False)
                act_body(i * 2 + 1, 1, False)
                ac.leave(NC // 2 - 2, 16)
            act_body(NC - 2, 0, False)
            act_body(NC - 1, 1, True)
            stage_end(act, 6)

        @block.vector
        def _(dve):
            dv = Chain(dve, c_dve)
            dve.wait_ge(s_nrm_ps, 1)
            dv.link(dve.tensor_reduce(nrm[:, 0:1], ps[:, 6:8, 0:512], AX.XY, ALU.max))
            dv.link(dve.tensor_single_scalar(nri[:, 0:1], nrm[:, 0:1].bitcast(I32), 23, ALU.logical_shift_right))
            dv.link(dve.tensor_scalar(nri[:, 2:3], nri[:, 0:1], -126.0, 1.0, ALU.add, ALU.max))
            dv.link(dve.tensor_scalar(nri[:, 3:4], nri[:, 2:3], -1.0, 127.0, ALU.mult, ALU.add))
            dve.tensor_single_scalar(nrm[:, 1:2].bitcast(I32), nri[:, 3:4], 23, ALU.logical_shift_left).then_inc(s_sc, 1)

            def statistics(k):
                v = [sm[:, 6 * k + j, :] for j in range(6)]
                dv.link(dve.tensor_tensor(v[0], st[:, :, 1], st[:, :, 4], ALU.add))
                dv.link(dve.tensor_tensor(v[1], st[:, :, 1], st[:, :, 4], ALU.subtract))
                dv.link(dve.tensor_tensor(v[4], v[1], v[1], ALU.mult))
                dv.link(dve.tensor_tensor(v[5], st[:, :, 2], st[:, :, 5], ALU.add))
                dv.link(dve.tensor_scalar(v[5], v[5], 1.0 / D, EPS, ALU.mult, ALU.add))
                dve.scalar_tensor_tensor(out=v[2], in0=v[4], scalar=0.25, in1=v[5], op0=ALU.mult, op1=ALU.add).then_inc(s_var, 1)
                dve.wait_ge(s_std, k + 1)
                dv.link(dve.reciprocal(v[4], v[3]))
                dv.link(dve.scalar_tensor_tensor(out=v[5], in0=v[0], scalar=-0.5, in1=v[4], op0=ALU.mult, op1=ALU.mult))

            dve.wait_ge(s_x, 64)
            with dve.Fori(0, NT) as i:
                dv.enter(i)
                dv.mark(dve.bn_stats(st[:, ds(i, 1), :], X[:, ds(i, 1), :]))
                dv.leave(NT, 1)
            dv.settle()
            statistics(0)
            with dve.Fori(0, NT) as i:
                dv.enter(i * 2)
                dv.link(dve.tensor_scalar(XN[:, ds(i, 1), :], X[:, ds(i, 1), :], sm[:, 4, ds(i, 1)], sm[:, 5, ds(i, 1)],
                                          ALU.mult, ALU.add))
                dv.mark(dve.bn_stats(st[:, ds(i, 1), :], XN[:, ds(i, 1), :]))
                dv.leave(NT, 2)
            dv.settle()
            statistics(1)
            dve.sem_inc(s_q3, 1)
            dve.sem_inc(s_vc, 1)
            dve.sem_inc(s_lc, 1)
            stage_end(dve, 1)

            dve.wait_ge(s_w, 9 * 16)
            with dve.Fori(0, NC) as n:
                dv.enter(n * 12)
                dve.wait_ge(s_t2, n + 1)
                dve.wait_ge(s_x2d, n * 16 + 16)
                for t in range(TPC):
                    i = n * TPC + t
                    dve.tensor_scalar(x2h[:, t, :], XN[:, ds(i, 1), :], sm[:, 10, ds(i, 1)], sm[:, 11, ds(i, 1)],
                                      ALU.mult, ALU.add).then_inc(s_x2h, 1)
                dve.wait_ge(s_t2, n + 2)
                dve.wait_ge(s_lp, n + 1)
                for k in range(KD):
                    dve.tensor_scalar(x2c[:, k, :], ps[:, 2 + k, :], lng[:, 0, k:k + 1], lng[:, 1, k:k + 1],
                                      ALU.mult, ALU.add).then_inc(s_x2c, 1)
                dve.wait_ge(s_qd, n * 64 + 64)
                for m in range(4):
                    dve.wait_ge(s_qf, n * 4 + (m + 3))
                    dv.link(dve.tensor_copy(q3[:, m, 0, :], qf[:, m % 2, :]))
                    dv.link(dve.tensor_tensor(qr[:, :], qf[:, m % 2, :], q3[:, m, 0, :], ALU.subtract))
                    dv.link(dve.tensor_copy(q3[:, m, 1, :], qr[:, :]))
                    dve.tensor_tensor(q3[:, m, 2, :], qr[:, :], q3[:, m, 1, :], ALU.subtract).then_inc(s_q3, 1)
                    dve.wait_ge(s_q3, n * 4 + (m + 2))
                dve.wait_ge(s_vp, n + 2)
                dve.wait_ge(s_vd, n * 16 + 16)
                dve.tensor_copy(Vc[:, :, :], ps[:, 6:8, :].rearrange("p k (t n) -> p (k t) n", n=D)).then_inc(s_vc, 1)
                dve.wait_ge(s_lp, n + 2)
                dve.tensor_copy(lgt[:, ds(n * TPC, TPC), :], ps[:, 2, 0:TPC * E].rearrange("p (t e) -> p t e", e=E)).then_inc(s_lc, 1)
                dv.leave(NC, 12)
            dve.wait_ge(s_lc, NC + 1)
            dv.settle()
            rank, tmp, s0, s1 = (top[:, k, :, :] for k in range(4))
            dv.link(dve.memset(rank, 0.0))
            for e in range(E):
                big = lgt[:, :, e:e + 1]
                dv.mark(dve.tensor_tensor(tmp[:, :, 0:e + 1], big.broadcast_to([P, NT, e + 1]), lgt[:, :, 0:e + 1], ALU.is_gt))
                if e + 1 < E:
                    dv.mark(dve.tensor_tensor(tmp[:, :, e + 1:E], big.broadcast_to([P, NT, E - e - 1]), lgt[:, :, e + 1:E], ALU.is_ge))
                dv.settle()
                dv.link(dve.tensor_tensor(rank, rank, tmp, ALU.add))
            dv.mark(dve.tensor_scalar(s0, rank, 0.0, None, ALU.is_equal))
            dv.mark(dve.tensor_scalar(s1, rank, 1.0, None, ALU.is_equal))
            dv.settle()
            dv.link(dve.tensor_tensor(tmp, s1, s0, ALU.subtract))
            dv.link(dve.tensor_tensor(tmp, tmp, lgt[:, :, :], ALU.mult))
            dve.tensor_reduce(sm[:, 1, :], tmp, AX.X, ALU.add).then_inc(s_top, 1)
            dve.wait_ge(s_tex, 1)
            dv.link(dve.tensor_scalar(sm[:, 3, :], sm[:, 2, :], 1.0, None, ALU.add))
            dv.link(dve.reciprocal(sm[:, 4, :], sm[:, 3, :]))
            dv.link(dve.tensor_tensor(sm[:, 5, :], sm[:, 2, :], sm[:, 4, :], ALU.mult))

            def per_token(v):
                return v.rearrange("p (t a) -> p t a", a=1).broadcast_to([P, NT, E])

            both, place = top[:, 4, :, :], top[:, 5, :, :]
            dve.tensor_tensor(both, s0, s1, ALU.add).then_inc(s_cnt, 1)
            dve.wait_ge(s_cnt, 2)
            before = ps[:, 6, 0:NT * E].rearrange("p (t e) -> p t e", e=E)
            total = ps[:, 7, 0:NT * E].rearrange("p (t e) -> p t e", e=E)
            dve.wait_ge(s_pos, 1)
            for e in range(E):
                dv.mark(dve.tensor_tensor_scan(run[:, e, :], onet[:, :], total[:, :, e], 0.0, ALU.mult, ALU.add))
            dv.settle()
            dv.link(dve.tensor_scalar(exi[:, 0, :], run[:, :, NT - 1], float(P - 1), None, ALU.add))
            dv.link(dve.tensor_single_scalar(exi[:, 1, :], exi[:, 0, :], P.bit_length() - 1, ALU.logical_shift_right))
            dv.link(dve.tensor_copy(ex[:, 0, :], exi[:, 1, :]))
            dv.link(dve.tensor_tensor_scan(ex[:, 1, :], onet[:, 0:E], ex[:, 0, :], 0.0, ALU.mult, ALU.add))
            dv.link(dve.tensor_tensor(ex[:, 2, :], ex[:, 1, :], ex[:, 0, :], ALU.subtract))
            dv.link(dve.tensor_scalar(ex[:, 3, :], ex[:, 2, :], float(P), None, ALU.mult))
            dv.link(dve.tensor_tensor(place, before, run[:, :, :].rearrange("p e t -> p t e"), ALU.add))
            dv.link(dve.tensor_tensor(place, place, total, ALU.subtract))
            dv.link(dve.tensor_tensor(place, place, ex[:, 3:4, :].broadcast_to([P, NT, E]), ALU.add))
            for k, sk in enumerate((s0, s1)):
                dv.link(dve.tensor_tensor(tmp, sk, place, ALU.mult))
                dv.link(dve.tensor_reduce(sl[:, k, :], tmp, AX.X, ALU.add))
                dv.link(dve.tensor_copy(slot[:, :, k], sl[:, k, :]))
                dv.link(dve.tensor_copy(wt[:, k, :], sm[:, 4 + k, :]))
            dv.mark(dve.tensor_copy(blk[:, :], blki[:, :]))
            dv.link(dve.memset(eid[:, :], 0.0))
            for e in range(E):
                dv.link(dve.scalar_tensor_tensor(out=eid[:, :], in0=blk[:, :], scalar=ex[:, 1, e:e + 1], in1=eid[:, :],
                                                 op0=ALU.is_ge, op1=ALU.add))
            dv.link(dve.tensor_scalar(eid[:, :], eid[:, :], float(E - 1), None, ALU.min))
            dv.link(dve.tensor_copy(eidi[:, :], eid[:, :]))
            dv.link(dve.tensor_tensor(s0, s0, per_token(sm[:, 4, :]), ALU.mult))
            dv.link(dve.tensor_tensor(s1, s1, per_token(sm[:, 5, :]), ALU.mult))
            dv.link(dve.tensor_tensor(wd[:, :, :], s0, s1, ALU.add))
            stage_end(dve, 2)

            def ring(gm, gx, base, plan):
                for r, u in enumerate(ring_of(plan)):
                    slot = ps[:, 2 * (r % 2):2 * (r % 2) + 2, :].rearrange("p a n -> p (a n)")
                    dve.wait_ge(s_full, base + (r + 1))
                    if u[0] == "max":
                        _, h, t, k0, n = u
                        qc = t // TPC
                        dve.tensor_reduce(mp[:, qc, h, t % TPC, k0 // 1024:k0 // 1024 + 1], slot[:, 0:n], AX.X, ALU.max).then_inc(s_free, 1)
                        if (h, t) == (HG - 1, TPC * (qc + 1) - 1) and k0 + n == P * (t + 1):
                            dve.wait_ge(s_free, base + (r + 1))
                            w = 2 if qc * CH >= 1024 else 1
                            dve.tensor_reduce(mn[:, qc, :], mp[:, qc, :, :, 0:w].rearrange("p h t w -> p (h t) w"), AX.X,
                                              ALU.max, negate=True).then_inc(s_mn, 1)
                            dve.wait_ge(s_mn, gm * CPB + (qc + 1))
                    elif u[0] == "turn":
                        qc = u[1]
                        if plan is not FIRST_PLAN:
                            dve.wait_ge(s_mrow[qc], gm * 16)
                        v = slot[0:HG * TPC, 0:P]
                        dv.link(dve.tensor_copy(n3[:, qc, 0, :], v))
                        dve.tensor_tensor(nr[:, :], v, n3[:, qc, 0, :], ALU.subtract).then_inc(s_free, 1)
                        dve.wait_ge(s_free, base + (r + 1))
                        dv.link(dve.tensor_copy(n3[:, qc, 1, :], nr[:, :]))
                        dve.tensor_tensor(n3[:, qc, 2, :], nr[:, :], n3[:, qc, 1, :], ALU.subtract).then_inc(s_mr, 1)
                        dve.wait_ge(s_mr, gm * CPB + (qc + 1))
                    else:
                        qc = u[1]
                        v = slot[:, 0:CH].rearrange("p (t h c) -> p t h c", t=TPC, h=HG)
                        dv.link(dve.reciprocal(rec[:, :, :], v[:, :, :, HS]))
                        dve.wait_ge(s_aod, gx * (16 * CPB) + (qc + 1) * 16)
                        o = ao[:, :, :].rearrange("p t (h d) -> p t h d", h=HG)
                        r4 = rec[:, :, :].rearrange("p t (h a) -> p t h a", a=1).broadcast_to([P, TPC, HG, HS])
                        dve.tensor_tensor(o, v[:, :, :, 0:HS], r4, ALU.mult).then_inc(s_free, 1)
                        dve.wait_ge(s_free, base + (r + 1))

            ring(0, None, 0, FIRST_PLAN)
            with dve.Fori(0, NG - 1) as g:
                dv.enter(g * 12)
                ring(g + 1, g, g * NR + NM, FULL_PLAN)
                dv.leave(NG - 1, 12)
            ring(None, NG - 1, NM + (NG - 1) * NR, LAST_PLAN)
            stage_end(dve, 3)

            dve.sem_inc(s_hT, 1)
            dve.sem_inc(s_yb, 1)
            dve.wait_ge(s_b, 48)
            dve.wait_ge(s_bz, 2)
            dv.link(dve.tensor_copy(b3[:, :], bt[:, :]))
            dv.link(dve.tensor_tensor(br[:, :], bt[:, :], b3[:, :], ALU.subtract))
            dv.mark(dve.tensor_copy(b3[32:64, :], br[32:64, :]))
            dv.link(dve.tensor_copy(b3[64:P, :], br[64:P, :]))
            dv.link(dve.tensor_tensor(br[64:P, :], br[64:P, :], b3[64:P, :], ALU.subtract))
            dv.link(dve.tensor_copy(b3[64:P, :], br[64:P, :]))
            dv.link(dve.tensor_scalar(pick[:, :], eid[:, :], row_e[:, 0:1], None, ALU.is_equal))
            dve.tensor_copy(pickb[:, :, :], pick[:, :].rearrange("p (i a) -> p i a", a=1).broadcast_to([P, NBLK, P])).then_inc(s_pick, 1)

            def turned(i, par):
                dve.wait_ge(s_turn, i + 3)
                dve.wait_ge(s_dn, i + 1)
                dve.tensor_copy(hT[:, par, :, :], ps[:, 4:6, :].rearrange("p a (f t) -> p (a f) t", t=P)).then_inc(s_hT, 1)

            def result(i, par):
                dve.wait_ge(s_dn, i + 3)
                dve.wait_ge(s_ys[par], i // 2 * 16 + 16)
                dve.tensor_copy(yb[:, par, :], ps[:, 7, 0:D]).then_inc(s_yb, 1)

            turned(0, 0)
            with dve.Fori(0, NBLK // 2 - 1) as i:
                for par in (1, 0):
                    j = i * 2 + (2 - par)
                    result(j - 1, 1 - par)
                    turned(j, par)
            result(NBLK - 2, 0)
            turned(NBLK - 1, 1)
            result(NBLK - 1, 1)
            stage_end(dve, 4)

            dve.sem_inc(s_cx, 1)
            dve.sem_inc(s_res, 2)
            dve.wait_ge(s_abs, 2)
            dve.tensor_tensor(tsum[:, 2:3], tsum[:, 0:1], tsum[:, 1:2], ALU.add).then_inc(s_tern, 1)
            dve.wait_ge(s_tps, 1)
            dv.link(dve.tensor_scalar(tsum[:, 3:4], ps[:, 3, 0:1], 0.7 / (D * D), None, ALU.mult))
            dv.link(dve.tensor_scalar(tsum[:, 4:5], tsum[:, 3:4], -1.0, None, ALU.mult))
            dv.mark(dve.tensor_scalar(tq[:, :, :], tw[:, :, :], tsum[:, 3:4], None, ALU.is_gt))
            dv.link(dve.tensor_scalar(tw[:, :, :], tw[:, :, :], tsum[:, 4:5], None, ALU.is_lt))
            dv.link(dve.tensor_tensor(tw[:, :, :], tq[:, :, :], tw[:, :, :], ALU.subtract))
            dve.tensor_scalar(tw[:, :, :], tw[:, :, :], alph[:, 0:1], None, ALU.mult).then_inc(s_tern, 1)
            dve.wait_ge(s_cw, 5 * 16)
            def expert_weights(c):
                if not (isinstance(c, int) and c == 0):
                    dve.wait_ge(s_ctp, c)
                dve.tensor_copy(wdc[:, :, :], wd[:, ds(c * TPC, TPC), :]).then_inc(s_cwd, 1)

            def moe(c, par):
                dv.link(dve.tensor_copy(wtc[:, :, :], wt[:, :, ds(c * TPC, TPC)]))
                dve.wait_ge(s_ci[par], c // 2 * 64 + 64)
                dve.wait_ge(s_cpr, c * 2 + 1)
                dve.wait_ge(s_yg[par], c // 2 * (16 * TPC * TOPK) + 16 * TPC * TOPK)
                for t in range(TPC):
                    dv.mark(dve.scalar_tensor_tensor(out=cmb[:, 2, t, :], in0=yg[:, par, t, 0, :], scalar=wtc[:, 0, t:t + 1],
                                                     in1=ps[:, 6 + t // 2, t % 2 * D:(t % 2 + 1) * D], op0=ALU.mult, op1=ALU.add))
                dv.settle()
                for t in range(TPC):
                    ins = dve.scalar_tensor_tensor(out=mot[:, t, :], in0=yg[:, par, t, 1, :], scalar=wtc[:, 1, t:t + 1],
                                                   in1=cmb[:, 2, t, :], op0=ALU.mult, op1=ALU.add)
                ins.then_inc(s_cmo, 1)
                dve.wait_ge(s_cmo, c + 1)
                dv.link(dve.tensor_tensor(cmb[:, 2, :, :], inx[:, par, 2, :, :], mixw[:, 0:1, :].broadcast_to(BIG), ALU.mult))
                dv.link(dve.tensor_reduce(gate[:, 0, :], cmb[:, 2, :, :], AX.X, ALU.add))

            def residual(c):
                dve.wait_ge(s_tout, c + 1)
                dve.wait_ge(s_co, c * 16 + 16)
                dve.tensor_tensor(x1o[:, :, :], x1c[:, :, :], ps[:, 6:8, :].rearrange("p k (t n) -> p (k t) n", n=D),
                                  ALU.add).then_inc(s_res, 1)
                dve.wait_ge(s_res, c + 3)

            def combine(c, par, more, first=False):
                abel = inx[:, par, 2, :, :]
                dve.wait_ge(s_cpr, c * 2 + 2)
                dve.wait_ge(s_cb, c + 1)
                dv.link(dve.tensor_tensor(cmb[:, 3, :, :], cmb[:, 1, :, :], ps[:, 4:6, :].rearrange("p k (t n) -> p (k t) n", n=D), ALU.add))
                dve.wait_ge(s_cnb, c + 1)
                nonabel = ps[:, 2:4, :].rearrange("p k (t n) -> p (k t) n", n=D)
                dv.link(dve.tensor_tensor(cmb[:, 2, :, :], nonabel, mixw[:, 1:2, :].broadcast_to(BIG), ALU.mult))
                dv.link(dve.tensor_reduce(gate[:, 1, :], cmb[:, 2, :, :], AX.X, ALU.add))
                dve.tensor_tensor(gate[:, 2, :], gate[:, 0, :], gate[:, 1, :], ALU.add).then_inc(s_cz, 1)
                dv.link(dve.tensor_tensor(cmb[:, 2, :, :], nonabel, abel, ALU.subtract))
                if not first:
                    residual(c - 1)
                dve.wait_ge(s_cg, c + 1)
                g4 = gate[:, 3, :].rearrange("p (t a) -> p t a", a=1).broadcast_to(BIG)
                dv.link(dve.tensor_tensor(cmb[:, 2, :, :], cmb[:, 2, :, :], g4, ALU.mult))
                dve.tensor_tensor(x1c[:, :, :], cmb[:, 2, :, :], cmb[:, 3, :, :], ALU.add).then_inc(s_cx, 1)
                dve.wait_ge(s_cx, c + 2)
                for t in range(TPC):
                    dv.mark(dve.bn_stats(x1s[:, t, :], x1c[:, t, :]))
                dv.settle()
                alone(dve)
                for t in range(TPC):
                    dv.mark(dve.bn_aggr(x1v[:, t, :], x1s[:, t, :]))
                dv.settle()
                dve.tensor_scalar(x1r[:, 0, :], x1v[:, :, 1], EPS, None, ALU.add).then_inc(s_x1s, 1)
                if more:
                    moe(c + 1, 1 - par)
                if more > 1:
                    expert_weights(c + 2)
                dve.wait_ge(s_x1q, c + 1)
                dv.link(dve.reciprocal(x1r[:, 2, :], x1r[:, 1, :]))
                for t in range(TPC):
                    dve.tensor_scalar(x1n[:, t, :], x1c[:, t, :], x1v[:, t, 0:1], x1r[:, 2, t:t + 1],
                                      ALU.subtract, ALU.mult).then_inc(s_x1n, 1)
                dve.wait_ge(s_x1n, c * TPC + TPC)

            expert_weights(0)
            moe(0, 0)
            expert_weights(1)
            combine(0, 0, 2, True)
            dv.straight()
            with dve.Fori(0, NC // 2 - 2) as i:
                dv.enter(i * 42)
                for par in (1, 0):
                    combine(i * 2 + (2 - par), par, 2)
                dv.leave(NC // 2 - 2, 42)
            combine(NC - 3, 1, 2)
            combine(NC - 2, 0, 1)
            combine(NC - 1, 1, 0)
            residual(NC - 1)
            dv.straight()
            stage_end(dve, 5)

            dve.sem_inc(s_bc3, 1)
            dve.sem_inc(s_sp, 1)
            dve.sem_inc(s_y, KI)
            dve.sem_inc(s_bu, 8)
            dve.sem_inc(s_h, 2)
            dve.sem_inc(s_tail, 1)
            dve.wait_ge(s_setup, 1)
            dve.wait_ge(s_lw, 9 * 16)

            def conv(m, k, par):
                dve.wait_ge(s_wfree, m * 8 + (k + 2))
                for d in range(2 * k, 2 * k + 2):
                    o = xs[:, par, d, :]
                    dv.link(dve.tensor_scalar(o, xraw[:, d, 0:CH], cw[:, d, 0:1], None, ALU.mult))
                    for j in range(1, TAPS):
                        ins = dve.scalar_tensor_tensor(out=o, in0=xraw[:, d, j:j + CH], scalar=cw[:, d, j:j + 1], in1=o,
                                                       op0=ALU.mult, op1=ALU.add)
                        if j < TAPS - 1:
                            dv.link(ins)
                    ins.then_inc(s_conv, 1)
                if k == 1:
                    dve.wait_ge(s_conv, m * KI + KI)
                    dve.tensor_scalar(xraw[:, :, 0:TAPS - 1], xraw[:, :, CH:], flag[:, ds(m + 1, 1)], None, ALU.mult).then_inc(s_tail, 1)

            def split_bc(m, par):
                dve.wait_ge(s_wfree, m * 8 + 6)
                v = xps[0:2 * NS, :]
                dv.link(dve.tensor_copy(bc3[0:2 * NS, par, :], v))
                dv.link(dve.tensor_tensor(bcr[:, :], v, bc3[0:2 * NS, par, :], ALU.subtract))
                dv.link(dve.tensor_copy(bc2[:, :], bcr[:, :]))
                dv.mark(dve.tensor_tensor(bc3[4 * NS:6 * NS, par, :], bcr[:, :], bc2[:, :], ALU.subtract))
                dve.tensor_copy(bc3[2 * NS:4 * NS, par, :], bc2[:, :]).then_inc(s_bc3, 1)

            def step_size(m, k, par):
                two = slice(2 * k, 2 * k + 2)
                dve.wait_ge(s_poly, m * 2 + (k + 1))
                small = te[:, :, :].bitcast(I32)
                dv.link(dve.tensor_scalar(small, te[:, :, :], 2.0 ** -6, None, ALU.is_lt))
                alone(dve)
                dv.link(dve.copy_predicated(tl[:, :, :], small, dtx[:, par, two, :]))
                dve.tensor_tensor(dt[:, par, two, :], dt[:, par, two, :], tl[:, :, :], ALU.add).then_inc(s_sp, 1)
                dve.wait_ge(s_sp, m * 2 + (k + 2))
                dve.wait_ge(s_xs, m * KI + KI)
                dve.tensor_tensor(dtx[:, par, two, :], dt[:, par, two, :], xs[:, par, two, :], ALU.mult).then_inc(s_dt, 1)

            def skip(n, par):
                dve.wait_ge(s_acc, n * 16 + 20)
                for d in range(KI):
                    dve.scalar_tensor_tensor(out=xs[:, par, d, :], in0=xs[:, par, d, :], scalar=Dv[:, d:d + 1], in1=ps[:, d, :],
                                             op0=ALU.mult, op1=ALU.add).then_inc(s_y, 1)

            def add(n, job):
                dve.wait_ge(s_wfull, job + 1)
                dve.wait_ge(s_xo, n * 16 + 16)
                dve.tensor_tensor(xo[:, :, :], xo[:, :, :], ps[:, 4:6, :].rearrange("p k (t n) -> p (k t) n", n=D), ALU.add)\
                    .then_inc(s_add, 1)
                dve.wait_ge(s_add, n + 1)
                dve.sem_inc(s_wfree, 1)

            def dve_body(n, par, first, last):
                for u in range(4 * NQ):
                    q, d = u // 4, u % 4
                    if u == 0:
                        dve.wait_ge(s_dt, n * 2 + 2)
                    if d == 0:
                        dve.wait_ge(s_cfree, n * 32 + (8 * q + 4 + 2))
                    dve.wait_ge(s_acc, n * 16 + (u + 1))
                    h = hh[:, u % 4, :, :]
                    x4 = dtx[:, par, d:d + 1, :].broadcast_to([P, 4, CH])
                    dve.tensor_tensor(h, x4, Bq[:, q % 2, :, :], ALU.mult).then_inc(s_bu, 1)
                    dve.wait_ge(s_bu, n * 16 + (u + 1 + 8))
                    dve.wait_ge(s_dA, n * 16 + (u + 1))
                    dve.wait_ge(s_h, n * 16 + (u + 2))
                    for j in range(4):
                        ins = dve.tensor_tensor_scan(h[:, j, :], dA[:, u % 2, j, :], h[:, j, :], hst[:, u, j:j + 1], ALU.mult, ALU.add)
                    dv.link(ins)
                    dve.tensor_scalar(hst[:, u, :], h[:, :, CH - 1], flag[:, ds(n + 1, 1)], None, ALU.mult).then_inc(s_h, 1)
                    if u == 1 and not first:
                        skip(n - 1, 1 - par)
                    if u == 4 and not first:
                        add(n - 1, n * 8 + 7)
                    if last:
                        continue
                    if u in (5, 6):
                        conv(n + 1, u - 5, 1 - par)
                    if u == 10:
                        split_bc(n + 1, 1 - par)
                    if u in (12, 15):
                        step_size(n + 1, u // 15, 1 - par)

            for k in range(2):
                conv(0, k, 0)
            split_bc(0, 0)
            for k in range(2):
                step_size(0, k, 0)
            dv.straight()
            dve_body(0, 0, True, False)
            dve_body(1, 1, False, False)
            with dve.Fori(1, NC // 2 - 1) as i:
                dv.enter((i - 1) * 72)
                dve_body(i * 2, 0, False, False)
                dve_body(i * 2 + 1, 1, False, False)
                dv.leave(NC // 2 - 2, 72)
            dve_body(NC - 2, 0, False, False)
            dve_body(NC - 1, 1, False, True)
            skip(NC - 1, 1)
            add(NC - 1, NC * 8)
            stage_end(dve, 6)

        @block.tensor
        def _(pe):
            def mm(o, lhsT, rhs, start=True, stop=True, **kw):
                return pe.matmul(o, lhsT, rhs, start=start, stop=stop, **kw)

            def half(bank, m):
                return ps[:, bank, m * D:(m + 1) * D]

            pe.wait_ge(s_const, 6 + TAYLOR)
            pe.wait_ge(s_nrm_abs, 1)
            for g in range(NROT + 1):
                for k in range(KD):
                    last = mm(half(6 + g // 2, g % 2), ones_s[:, :], gb[:, min(g, NROT - 1), k, :], k == 0, k == KD - 1)
            last.then_inc(s_nrm_ps, 1)
            pe.wait_ge(s_scaled, 2)
            for k in range(TAYLOR, 0, -1):
                for g in range(NROT):
                    if k < TAYLOR:
                        pe.wait_ge(s_hev, (TAYLOR - 1 - k) * NROT + g + 1)
                    for m in range(KD):
                        mm(half(g, m), idb[:, :], kid[:, k - 1, m, :], True, False)
                        if k == TAYLOR:
                            last = mm(half(g, m), idf[:, :], er[:, g, m, :], False, True)
                        else:
                            for j in range(KD):
                                last = mm(half(g, m), gb[:, g, j, m * P:(m + 1) * P], er[:, g, j, :], False, j == KD - 1)
                    last.then_inc(s_hor, 1)
            for g in range(NROT):
                pe.wait_ge(s_hev, (TAYLOR - 1) * NROT + g + 1)
                for m in range(KD):
                    for j in range(KD):
                        last = pe.transpose(ps[:, 3 + g, m * D + j * P:m * D + (j + 1) * P], er[:, g, j, m * P:(m + 1) * P], idf[:, :])
                last.then_inc(s_hor, 1)
            pe.wait_ge(s_hev, (TAYLOR + 1) * NROT)
            squarings = pe.value_load(nri[0:1, 2:3], min_val=1, max_val=200)
            pe.sem_inc(s_sqe, 2 * NROT)
            with pe.Fori(0, squarings) as i:
                for g in range(NROT):
                    pe.wait_ge(s_sqe, i * (2 * NROT) + 2 * (g + 1))
                    for m in range(KD):
                        for j in range(KD):
                            mm(half(g, m), et[:, g, j, m * P:(m + 1) * P], er[:, g, j, :], j == 0, j == KD - 1)
                    for m in range(KD):
                        for j in range(KD):
                            last = mm(half(3 + g, m), er[:, g, j, m * P:(m + 1) * P], et[:, g, j, :], j == 0, j == KD - 1)
                    last.then_inc(s_sqp, 1)
            pe.wait_ge(s_sqe, squarings * (2 * NROT) + 2 * NROT)
            for m in range(KD):
                for j in range(KD):
                    last = mm(half(6, m), er[:, 1, j, m * P:(m + 1) * P], et[:, 0, j, :], j == 0, j == KD - 1)
            last.then_inc(s_fin, 1)
            pe.wait_ge(s_fev, 1)
            for m in range(KD):
                for j in range(KD):
                    last = mm(half(7, m), gb[:, 0, j, m * P:(m + 1) * P], er[:, 2, j, :], j == 0, j == KD - 1)
            last.then_inc(s_fin, 1)
            stage_end(pe, 1)

            pe.sem_inc(s_tx, 1)
            pe.sem_inc(s_t2, 1)
            pe.sem_inc(s_vp, 1)
            pe.sem_inc(s_lp, 1)
            pe.wait_ge(s_w, 9 * 16)
            with pe.Fori(0, NC) as n:
                for src, bank, got, done, free in ((XNc, 0, (s_xnc, n + 1), s_tx, s_ac), (x2h, 2, (s_x2h, n * 4 + 4), s_t2, s_lc)):
                    pe.wait_ge(*got)
                    pe.wait_ge(free, n + 1)
                    for t in range(TPC):
                        for k in range(KD):
                            last = pe.transpose(ps[:, bank + k, t * P:(t + 1) * P], src[:, t, k * P:(k + 1) * P], idf[:, :])
                    last.then_inc(done, 1)
                pe.wait_ge(s_xT, n + 1)
                for m in range(4):
                    pe.wait_ge(s_qf, n * 4 + (m + 1))
                    for k in range(KD):
                        last = mm(ps[:, 4 + m % 2, :], wqkv[:, k, m * P:(m + 1) * P], xTc[:, k, :], k == 0, k == KD - 1)
                    last.then_inc(s_qp, 1)
                pe.wait_ge(s_vc, n + 1)
                for t in range(TPC):
                    o = half(6 + t // 2, t % 2)
                    for k in range(KD):
                        mm(o, xTc[:, k, t * P:(t + 1) * P], wqkv[:, k, 2 * D:3 * D], k == 0, False)
                    last = mm(o, ones_r[:, :], bv[:, :], False, True)
                last.then_inc(s_vp, 1)
                pe.wait_ge(s_x2c, n * KD + KD)
                for t in range(TPC):
                    o = half(t // 2, t % 2)
                    for k in range(KD):
                        mm(o, x2c[:, k, t * P:(t + 1) * P], wab[:, k, :], k == 0, False)
                    last = mm(o, ones_r[:, :], bab[:, :], False, True)
                last.then_inc(s_ap, 1)
                for t in range(TPC):
                    o = ps[:, 2, t * E:(t + 1) * E]
                    for k in range(KD):
                        mm(o, x2c[:, k, t * P:(t + 1) * P], wg[:, k, :], k == 0, False)
                    last = mm(o, ones_r[:, :], bg[:, :], False, True)
                last.then_inc(s_lp, 1)
            pe.wait_ge(s_cnt, 1)
            pe.wait_ge(s_pos, 1)
            both = top[:, 4, :, :].rearrange("p t e -> p (t e)")
            mm(ps[:, 6, 0:NT * E], tri[:, :], both)
            mm(ps[:, 7, 0:NT * E], ones_s[:, :], both).then_inc(s_cnt, 1)
            stage_end(pe, 2)

            pe.sem_inc(s_pv, 2)

            def attention(g, gm, base, plan, par, loads):
                r = 0
                for u in plan:
                    if u[0] == "score":
                        n = u[1]
                        h, qc, kt, q0 = EU[n]
                        if n == 0 or EU[n - 1][1] != qc:
                            pe.wait_ge(s_mrow[qc], g * 16 + 16)
                        back = n - SRING if n >= SRING else max(k for k in range(NE) if k % SRING == n) - NE
                        pe.wait_ge(s_exp, g * NE + (back + 1 + NE))
                        o = ps[:, 4 + n % SRING, q0:CH]
                        diagonal = kt >= TPC * qc
                        last = mm(o, ks[0:FULL, par, h, kt * P:(kt + 1) * P], qs[0:FULL, par, h, qc * CH + q0:(qc + 1) * CH],
                                  True, not diagonal)
                        if diagonal:
                            last = mm(ps[:, 4 + n % SRING, q0:q0 + P], idb[:, :], mask_k[:, :], False, True)
                        last.then_inc(s_score, 1)
                        continue
                    if u[0] == "pv":
                        step = u[1]
                        _, qc, kt, q0 = EU[HG * step]
                        pe.wait_ge(s_exp, g * NE + (HG * (step + 1) + NE))
                        if step == 0:
                            pe.wait_ge(s_vg, g + 1)
                        if kt == 0:
                            pe.wait_ge(s_oT, g * CPB + (qc + 1))
                        for h in range(HG):
                            last = mm(ps[32 * h:32 * h + 32, 7, q0:CH], vg[:, par, kt, h, :], Pt[:, (HG * step + h) % PRING, q0:CH],
                                      kt == 0, kt == TPC * (qc + 1) - 1, tile_position=(0, 32 * h))
                        last.then_inc(s_pv, 1)
                        continue
                    bank = 2 * (r % 2)
                    if not (isinstance(base, int) and base + r < 2):
                        pe.wait_ge(s_free, base + (r - 1))
                    if u[0] == "max":
                        _, h, t, k0, n = u
                        if (h, t, k0) in ((0, 0, 0), (0, QT // 2, 0)):
                            pe.wait_ge(s_qk[1 - par][t // (QT // 2)], loads)
                        for j in range(0, n, 512):
                            w = min(512, n - j)
                            diagonal = k0 + j + w == P * (t + 1)
                            last = mm(ps[:, bank + j // 512, 0:w], qs[0:ROWS, 1 - par, h, t * P:(t + 1) * P],
                                      ks[0:ROWS, 1 - par, h, k0 + j:k0 + j + w], True, not diagonal)
                            if diagonal:
                                last = mm(ps[:, bank + j // 512, w - P:w], idb[:, :], mask_q[:, :], False, True)
                    elif u[0] == "turn":
                        pe.wait_ge(s_mn, gm * CPB + (u[1] + 1))
                        last = pe.transpose(ps[0:HG * TPC, bank, 0:P], mn[:, u[1], :], idf[:, :])
                    else:
                        pe.wait_ge(s_oT, g * CPB + (u[1] + 2))
                        for t in range(TPC):
                            last = pe.transpose(ps[:, bank, t * P:(t + 1) * P], oT[:, t * P:(t + 1) * P], idf[:, :])
                    last.then_inc(s_full, 1)
                    r += 1

            pe.wait_ge(s_stack, 1)
            attention(None, 0, 0, FIRST_PLAN, 1, 192)
            with pe.Fori(0, NG // 2 - 1) as i:
                for par in range(2):
                    g = i * 2 + par
                    attention(g, g + 1, g * NR + NM, FULL_PLAN, par, i * 192 + 192 * (par + 1))
            attention(NG - 2, NG - 1, NM + (NG - 2) * NR, FULL_PLAN, 0, NG // 2 * 192)
            attention(NG - 1, None, NM + (NG - 1) * NR, LAST_PLAN, 1, None)
            stage_end(pe, 3)

            pe.sem_inc(s_hid, 2)
            pe.sem_inc(s_turn, 2)
            pe.sem_inc(s_dn, 2)
            pe.wait_ge(s_ew, E * 16)
            pe.wait_ge(s_pick, 1)

            def expert_of(i):
                return pe.value_load(eidi[0:1, ds(i, 1)], min_val=0, max_val=E - 1)

            def rows_in(i, par):
                pe.wait_ge(s_xg[par], i // 2 * 16 + 16)
                pe.wait_ge(s_xgT, i + 1)
                for k in range(KD):
                    last = pe.transpose(ps[:, 6, k * P:(k + 1) * P], xg[:, par, k * P:(k + 1) * P], idf[:, :])
                last.then_inc(s_tp, 1)

            def hidden(i, par):
                e = expert_of(i)
                pe.wait_ge(s_xgT, i + 2)
                pe.wait_ge(s_gelu, i + 1)
                for j in range(2):
                    o = ps[:, 2 * par + j, :]
                    mm(o, pickb[:, ds(i, 1), :].rearrange("p a n -> p (a n)"), b3[:, j * 512:(j + 1) * 512], True, False)
                    for k in range(KD):
                        last = mm(o, xgT[:, par, k, :], W1[:, ds(e, 1), k, j * 512:(j + 1) * 512], False, k == KD - 1)
                last.then_inc(s_hid, 1)

            def turn(i, par):
                pe.wait_ge(s_gelu, i + 3)
                pe.wait_ge(s_hT, i + 1)
                for f in range(KF):
                    last = pe.transpose(ps[:, 4 + f // 4, f % 4 * P:(f % 4 + 1) * P], hg[:, par, f * P:(f + 1) * P], idf[:, :])
                last.then_inc(s_turn, 1)

            def down(i, par):
                e = expert_of(i)
                pe.wait_ge(s_hT, i + 2)
                pe.wait_ge(s_yb, i + 1)
                for f in range(KF):
                    last = mm(ps[:, 7, 0:D], hT[:, par, f, :], W2[:, ds(e, 1), f, :], f == 0, f == KF - 1)
                last.then_inc(s_dn, 1)

            rows_in(0, 0)
            hidden(0, 0)
            rows_in(1, 1)
            turn(0, 0)
            pe.wait_ge(s_ew2, E * 16)
            with pe.Fori(0, NBLK // 2 - 1) as i:
                for par in (1, 0):
                    j = i * 2 + (2 - par)
                    hidden(j, par)
                    rows_in(j + 1, 1 - par)
                    down(j - 1, 1 - par)
                    turn(j, par)
            hidden(NBLK - 1, 1)
            down(NBLK - 2, 0)
            turn(NBLK - 1, 1)
            down(NBLK - 1, 1)
            stage_end(pe, 4)

            pe.wait_ge(s_cw, 5 * 16)
            def front(c, par):
                pe.wait_ge(s_ci[par], c // 2 * 64 + 64)
                pe.wait_ge(s_cwd, c + 1)
                pe.wait_ge(s_cx, c + 1)
                pe.wait_ge(s_res, c + 1)
                for t in range(TPC):
                    for k in range(KD):
                        pe.transpose(ps[:, k, t * P:(t + 1) * P], inx[:, par, 3, t, k * P:(k + 1) * P], idf[:, :])
                    last = pe.transpose(ps[0:E, 2, t * P:(t + 1) * P], wdc[:, t, :], idf[:, :])
                last.then_inc(s_ctp, 1)
                pe.wait_ge(s_cT, c * 2 + 2)
                for t in range(TPC):
                    last = mm(half(6 + t // 2, t % 2), wdT[:, t * P:(t + 1) * P], B2[:, :])
                last.then_inc(s_cpr, 1)
                for t in range(TPC):
                    o = half(4 + t // 2, t % 2)
                    for k in range(KD):
                        mm(o, atT[:, k, t * P:(t + 1) * P], wpj[:, k, :], k == 0, False)
                    last = mm(o, ones_r[:, :], bpj[:, :], False, True)
                last.then_inc(s_cpr, 1)

            def middle(c, par):
                pe.wait_ge(s_cmo, c + 1)
                for t in range(TPC):
                    for k in range(KD):
                        last = pe.transpose(ps[:, k, t * P:(t + 1) * P], mot[:, t, k * P:(k + 1) * P], idf[:, :])
                last.then_inc(s_cmp, 1)
                pe.wait_ge(s_cmT, c + 1)
                for t in range(TPC):
                    for k in range(KD):
                        last = mm(half(2 + t // 2, t % 2), moT[:, k, t * P:(t + 1) * P], rot[:, k, :], k == 0, k == KD - 1)
                last.then_inc(s_cnb, 1)

            def back(c, par):
                pe.wait_ge(s_x1n, c * TPC + TPC)
                for t in range(TPC):
                    for k in range(KD):
                        last = pe.transpose(ps[:, k, t * P:(t + 1) * P], x1n[:, t, k * P:(k + 1) * P], idf[:, :])
                last.then_inc(s_x1t, 1)

            def ternary(c):
                pe.wait_ge(s_x1T, c + 1)
                for t in range(TPC):
                    o = half(6 + t // 2, t % 2)
                    for k in range(KD):
                        mm(o, x1T[:, k, t * P:(t + 1) * P], tw[:, k, :], k == 0, False)
                    last = mm(o, ones_r[:, :], tb[:, :], False, True)
                last.then_inc(s_tout, 1)

            pe.wait_ge(s_tern, 1)
            mm(ps[:, 3, 0:1], ones_s[:, :], tsum[:, 2:3]).then_inc(s_tps, 1)
            pe.wait_ge(s_tern, 2)
            front(0, 0)
            middle(0, 0)
            with pe.Fori(0, NC // 2 - 1) as i:
                for par in range(2):
                    c = i * 2 + par
                    front(c + 1, 1 - par)
                    middle(c + 1, 1 - par)
                    back(c, par)
                    ternary(c)
            front(NC - 1, 1)
            middle(NC - 1, 1)
            for c in (NC - 2, NC - 1):
                back(c, c % 2)
                ternary(c)
            stage_end(pe, 5)

            pe.wait_ge(s_lw, 9 * 16)

            def job(n, what):
                pe.wait_ge(s_wfree, n + 1)
                what().then_inc(s_wfull, 1)

            def project(m, k, par):
                def what():
                    for j in range(2):
                        c = 2 * k + j
                        for i in range(KD):
                            last = mm(ps[:, 4 + j, :], inw[:, i, c * P:(c + 1) * P], xin[:, par, i, :], i == 0, i == KD - 1)
                    return last
                job(m * 8 + k, what)

            def project_xp(m, par):
                def what():
                    for d in range(KI):
                        last = mm(ps[0:NX, 4, :], xpw[:, d, :], xs[:, par, d, :], d == 0, d == KI - 1)
                    return last
                pe.wait_ge(s_xs, m * KI + KI)
                job(m * 8 + 4, what)

            def project_dt(m, k):
                def what():
                    for j in range(2):
                        d = 2 * k + j
                        last = mm(ps[:, 4 + j, :], dtw[2 * NS:, d * P:(d + 1) * P], xps[2 * NS:, :], tile_position=(2 * NS, 0))
                    return last
                job(m * 8 + (5 + k), what)

            def output(n, par, at):
                def what():
                    for t in range(TPC):
                        o = half(4 + t // 2, t % 2)
                        for d in range(KI):
                            last = mm(o, xs[:, par, d, t * P:(t + 1) * P], outw[:, d, :], d == 0, d == KI - 1)
                    return last
                pe.wait_ge(s_yz, n + 3)
                job(at, what)

            def broadcast(n, q, par):
                if q == 0:
                    pe.wait_ge(s_bc3, n + 2)
                for k in range(8):
                    pe.wait_ge(s_cfree, n * 32 + (q * 8 + k + 1))
                    r = (NS if k >= 4 else 0) + 4 * q + k % 4
                    mm(ps[:, 6 + k % 2, :], sel[:, r, :], bc3[:, par, :]).then_inc(s_cfull, 1)

            def accumulate(n, u):
                q, d = u // 4, u % 4
                pe.wait_ge(s_hc, n * 16 + (u + 1 + 8))
                if q == 0:
                    pe.wait_ge(s_y, n * KI + (d + 1))
                for j in range(4):
                    last = mm(ps[:, d, :], idf[:, :], hh[:, u % 4, j, :], q == 0 and j == 0, q == NQ - 1 and j == 3)
                last.then_inc(s_acc, 1)

            def pe_body(n, par, first, last):
                for u in range(4 * NQ):
                    if u == 2 and not first:
                        output(n - 1, 1 - par, n * 8 + 7)
                    if not last:
                        if u in (2, 3, 4, 5):
                            if u == 2:
                                pe.wait_ge(s_xin[1 - par], (n + 1) // 2 * 16 + 16)
                            project(n + 1, u - 2, 1 - par)
                        if u == 7:
                            project_xp(n + 1, 1 - par)
                        if u in (8, 10):
                            project_dt(n + 1, u // 2 - 4)
                    if u % 4 == 1 and (u < 13 or not last):
                        q = u // 4 + 1
                        broadcast(n + q // NQ, q % NQ, par if q < NQ else 1 - par)
                    accumulate(n, u)

            pe.sem_inc(s_acc, 4)
            pe.wait_ge(s_xin[0], 16)
            for k in range(4):
                project(0, k, 0)
            project_xp(0, 0)
            for k in range(2):
                project_dt(0, k)
            pe.drain().then_inc(s_wfull, 1)
            pe.wait_ge(s_setup, 2)
            broadcast(0, 0, 0)
            pe_body(0, 0, True, False)
            pe_body(1, 1, False, False)
            with pe.Fori(1, NC // 2 - 1) as i:
                pe_body(i * 2, 0, False, False)
                pe_body(i * 2 + 1, 1, False, False)
            pe_body(NC - 2, 0, False, False)
            pe_body(NC - 1, 1, False, True)
            output(NC - 1, 1, NC * 8)
            stage_end(pe, 6)


_ORDER = ["L0_attn_x", "L0_attn_c_attn_w", "L0_attn_c_attn_b", "L0_attn_c_proj_w", "L0_attn_c_proj_b",
          "L0_ffn_ln_g", "L0_ffn_ln_b", "L0_ffn_abel_w", "L0_ffn_abel_b", "L0_ffn_gate_w_moe", "L0_ffn_gate_b_moe",
          "L0_ffn_w1", "L0_ffn_b1", "L0_ffn_w2", "L0_ffn_b2", "L0_ffn_gens", "gens_transposed",
          "L0_ffn_mix_w", "L0_ffn_mix_b", "in_proj_transposed", "L1_attn_conv_w", "L1_attn_conv_b",
          "x_proj_transposed", "dt_proj_transposed", "L1_attn_dt_proj_b", "L1_attn_A_log", "L1_attn_D",
          "out_proj_transposed", "ternary_transposed", "L1_ffn_alpha", "L1_ffn_bias"]


def kernel(**inputs):
    import numpy as _np
    import concourse.bacc as _bacc
    from concourse import mybir as _mybir
    from concourse.bass_utils import run_bass_kernel_spmd as _run

    laid = dict(inputs)
    laid["gens_transposed"] = _np.asarray(inputs["L0_ffn_gens"]).transpose(0, 2, 1)
    for name, source in (("in_proj_transposed", "L1_attn_in_proj_w"), ("x_proj_transposed", "L1_attn_x_proj_w"),
                         ("dt_proj_transposed", "L1_attn_dt_proj_w"), ("out_proj_transposed", "L1_attn_out_proj_w"),
                         ("ternary_transposed", "L1_ffn_weight")):
        laid[name] = _np.asarray(inputs[source]).T
    laid["x_proj_transposed"] = _np.roll(laid["x_proj_transposed"], -RANK, axis=1)
    nc = _bacc.Bacc("TRN2", target_bir_lowering=False, num_devices=1)
    arrays, args = {}, []
    for name in _ORDER:
        a = _np.ascontiguousarray(laid[name])
        arrays[f"in_{name}"] = a
        args.append(nc.dram_tensor(f"in_{name}", a.shape, _mybir.dt.from_np(a.dtype), kind="ExternalInput").ap())
    args.append(nc.dram_tensor("out_0", (B, S, D), F32, kind="ExternalOutput").ap())
    build(nc, *args)
    r = _run(nc, [arrays], core_ids=[0])
    return r.results[0]["out_0"]
```
